# Optimizing a Trainium2 kernel written in Bass

```python
import numpy as np
import jax
import jax.numpy as jnp

def _softmax(x, axis=-1):
    return jax.nn.softmax(x, axis=axis)

def _gelu(x):
    return jax.nn.gelu(x, approximate=True)

def _silu(x):
    return jax.nn.silu(x)

def _sigmoid(x):
    return jax.nn.sigmoid(x)

def _layernorm(x, axis=-1, eps=1e-05):
    m = jnp.mean(x, axis=axis, keepdims=True)
    v = jnp.var(x, axis=axis, keepdims=True)
    return (x - m) / jnp.sqrt(v + eps)

def _scatter_add(tgt, idx, src, axis=0):
    return tgt.at[idx].add(src)

def _segment_sum(src, seg, n):
    return jax.ops.segment_sum(src, seg, n)
kernel_name = 'mk_gnn_resnorm_d4_gnn_r32_c02ce7'

def setup_inputs(seed: int=0):
    np.random.seed(seed)
    _w = jnp.asarray

    def _rec_inputs():
        import jax
        import jax.numpy as jnp
        _gk = jax.random.key(seed)
        x = -0.0005121 + 1.001 * jax.random.normal(jax.random.fold_in(_gk, 1), (3125, 160), jnp.float32)
        src = jax.random.randint(jax.random.fold_in(_gk, 2), (50000,), 0, 3125, jnp.int32)
        dst = jnp.minimum((3125 * jax.random.uniform(jax.random.fold_in(_gk, 3), (50000,)) ** 2.0).astype(jnp.int32), 99999)
        _o = jnp.argsort(dst, stable=True)
        src = src[_o]
        dst = dst[_o]
        edge_attr_16 = -0.000191324 + 0.999809 * jax.random.normal(jax.random.fold_in(_gk, 12), (50000, 16), jnp.float32)
        edge_attr_4 = 0.000735704 + 1.0001 * jax.random.normal(jax.random.fold_in(_gk, 13), (50000, 4), jnp.float32)
        edge_attr_64 = 0.000127647 + 1.00004 * jax.random.normal(jax.random.fold_in(_gk, 14), (50000, 64), jnp.float32)
        node_vec1 = -0.00719938 + 0.999885 * jax.random.normal(jax.random.fold_in(_gk, 16), (3125, 1), jnp.float32)
        return (x, src, dst, edge_attr_16, edge_attr_4, edge_attr_64, node_vec1)
    x, src, dst, edge_attr_16, edge_attr_4, edge_attr_64, node_vec1 = _rec_inputs()

    def _L0_gnn_setup():
        import jax, jax.numpy as jnp
        import numpy as np
        N = 625
        E = 20000
        INV_SQRT3 = 0.5773502691896258
        INV8 = 0.125
        INV_SQRT32 = 0.17677669529663687
        INV64 = 0.015625
        INV32 = 0.03125
        INV_SQRT2048 = 0.022097086912079608
        key = jax.random.key(seed)
        ks = jax.random.split(key, 16)
        f32 = jnp.float32
        return {'node_features': jax.random.normal(ks[0], (N, 160), f32), 'edge_index': jax.random.randint(ks[1], (2, E), 0, N), 'edge_attr_tensor': jax.random.normal(ks[2], (E, 4), f32), 'node_attr_scalar_raw': jax.random.normal(ks[3], (N, 1), f32), 'Wm_ss': jax.random.normal(ks[4], (64, 64), f32), 'Wm_vv': jax.random.normal(ks[5], (32, 64), f32), 'Wm_sv': jax.random.normal(ks[6], (64, 32), f32), 'Wm_vs': jax.random.normal(ks[7], (32, 32), f32), 'Lm_s': jax.random.normal(ks[8], (64, 64), f32), 'Lm_v': jax.random.normal(ks[9], (32, 32), f32), 'Wu_ss': jax.random.normal(ks[10], (64, 64, 64), f32), 'Wu_vv': jax.random.normal(ks[11], (32, 32, 64), f32), 'Wu_sv': jax.random.normal(ks[12], (64, 32, 32), f32), 'Wu_vs': jax.random.normal(ks[13], (32, 64, 32), f32), 'Lu_s': jax.random.normal(ks[14], (64, 64), f32), 'Lu_v': jax.random.normal(ks[15], (32, 32), f32)}
    _L0_gnn_all = _L0_gnn_setup()
    _L0_gnn_in = {k: v for k, v in _L0_gnn_all.items() if k in ('Wm_ss', 'Wm_vv', 'Wm_sv', 'Wm_vs', 'Lm_s', 'Lm_v', 'Wu_ss', 'Wu_vv', 'Wu_sv', 'Wu_vs', 'Lu_s', 'Lu_v')}
    del _L0_gnn_all

    def _L1_gnn_setup():
        import jax, jax.numpy as jnp
        import numpy as np
        N, E = (1250, 20000)
        S_IN, V_IN = (64, 32)
        S_MID, V_MID = (96, 128)
        S_OUT, V_OUT = (96, 32)
        R = 64
        FC_HID = 64
        W_NUMEL = 64 + 64 + 32 + 32 + 32
        NUM_NEIGHBORS = 16.0

        def _inv(d):
            return 1.0 / jnp.sqrt(jnp.float32(d))

        def _forward(node_features, node_attr, edge_attr, edge_scalars, lin1_ws, lin1_wv, fc_w1, fc_w2, sc_ws, sc_wv, lin2_ws, lin2_wv, edge_src, edge_dst):
            n = node_features.shape[0]
            s = node_features[:, :S_IN]
            v = node_features[:, S_IN:].reshape(n, V_IN, 3)
            a = node_attr
            sc_s = s @ sc_ws * a * _inv(S_IN)
            sc_v = jnp.einsum('nci,cd->ndi', v, sc_wv) * a[:, :, None] * _inv(V_IN)
            h_s = s @ lin1_ws * a * _inv(S_IN)
            h_v = jnp.einsum('nci,cd->ndi', v, lin1_wv) * a[:, :, None] * _inv(V_IN)
            hid = jax.nn.silu(edge_scalars @ fc_w1 * _inv(R))
            w = hid @ fc_w2 * _inv(FC_HID)
            w1, w2, w3, w4, w5 = jnp.split(w, [64, 128, 160, 192], axis=-1)
            es = h_s[edge_src]
            ev = h_v[edge_src]
            e0 = edge_attr[:, :1]
            e1 = edge_attr[:, 1:4]
            m_s1 = w1 * es * e0
            m_s2 = w4 * jnp.einsum('eci,ei->ec', ev, e1) * _inv(3)
            m_v1 = (w2 * es)[:, :, None] * e1[:, None, :]
            m_v2 = w3[:, :, None] * ev * e0[:, :, None]
            m_v3 = w5[:, :, None] * jnp.cross(ev, e1[:, None, :]) * _inv(2)
            mid_s = jnp.concatenate([m_s1, m_s2], axis=-1)
            mid_v = jnp.concatenate([m_v1, m_v2, m_v3], axis=1)
            inv_nn = 1.0 / jnp.sqrt(jnp.float32(NUM_NEIGHBORS))
            agg_s = jax.ops.segment_sum(mid_s, edge_dst, num_segments=n) * inv_nn
            agg_v = jax.ops.segment_sum(mid_v, edge_dst, num_segments=n) * inv_nn
            o_s = agg_s @ lin2_ws * a * _inv(S_MID)
            o_v = jnp.einsum('nci,cd->ndi', agg_v, lin2_wv) * a[:, :, None] * _inv(V_MID)
            pre_s = sc_s + o_s
            pre_v = sc_v + o_v
            scalars = jax.nn.silu(pre_s[:, :64])
            gates = jax.nn.sigmoid(pre_s[:, 64:96])
            gated = gates[:, :, None] * pre_v
            return jnp.concatenate([scalars, gated.reshape(n, 3 * V_OUT)], axis=-1)
        key = jax.random.key(seed)
        ks = jax.random.split(key, 13)
        return {'node_features': jax.random.normal(ks[0], (N, S_IN + 3 * V_IN), jnp.float32), 'node_attr': jnp.ones((N, 1), jnp.float32), 'edge_src': jax.random.randint(ks[1], (E,), 0, N), 'edge_dst': jax.random.randint(ks[2], (E,), 0, N), 'edge_attr': jax.random.normal(ks[3], (E, 4), jnp.float32), 'edge_scalars': jax.random.normal(ks[4], (E, R), jnp.float32), 'lin1_ws': jax.random.normal(ks[5], (S_IN, S_IN), jnp.float32), 'lin1_wv': jax.random.normal(ks[6], (V_IN, V_IN), jnp.float32), 'fc_w1': jax.random.normal(ks[7], (R, FC_HID), jnp.float32), 'fc_w2': jax.random.normal(ks[8], (FC_HID, W_NUMEL), jnp.float32), 'sc_ws': jax.random.normal(ks[9], (S_IN, S_OUT), jnp.float32), 'sc_wv': jax.random.normal(ks[10], (V_IN, V_OUT), jnp.float32), 'lin2_ws': jax.random.normal(ks[11], (S_MID, S_OUT), jnp.float32), 'lin2_wv': jax.random.normal(ks[12], (V_MID, V_OUT), jnp.float32)}
    _L1_gnn_all = _L1_gnn_setup()
    _L1_gnn_in = {k: v for k, v in _L1_gnn_all.items() if k in ('lin1_ws', 'lin1_wv', 'fc_w1', 'fc_w2', 'sc_ws', 'sc_wv', 'lin2_ws', 'lin2_wv')}
    del _L1_gnn_all

    def _L2_gnn_setup():
        import jax, jax.numpy as jnp
        import numpy as np
        N = 625
        E = 10000
        MUL0 = 64
        MUL1 = 32
        FC_IN = 16
        FC_H = 64
        WNUM = 192
        key = jax.random.key(seed)
        ks = jax.random.split(key, 16)
        return {'x': jax.random.normal(ks[0], (N, MUL0 + 3 * MUL1), jnp.float32), 'node_attr': jnp.ones((N, 1), jnp.float32), 'edge_scalars': jax.random.normal(ks[1], (E, FC_IN), jnp.float32), 'edge_attr_sh': jax.random.normal(ks[2], (E, 4), jnp.float32), 'edge_src': jax.random.randint(ks[3], (E,), 0, N), 'edge_dst': jax.random.randint(ks[4], (E,), 0, N), 'Wfc1': jax.random.normal(ks[5], (FC_IN, FC_H), jnp.float32), 'Wfc2': jax.random.normal(ks[6], (FC_H, WNUM), jnp.float32), 'Wsc0': jax.random.normal(ks[7], (MUL0, MUL0), jnp.float32), 'Wsc1': jax.random.normal(ks[8], (MUL1, MUL1), jnp.float32), 'Wl1_0': jax.random.normal(ks[9], (MUL0, MUL0), jnp.float32), 'Wl1_1': jax.random.normal(ks[10], (MUL1, MUL1), jnp.float32), 'Wl2_s': jax.random.normal(ks[11], (MUL0 + MUL1, MUL0), jnp.float32), 'Wl2_v': jax.random.normal(ks[12], (MUL0 + MUL1, MUL1), jnp.float32), 'Wa': 0.1 * jax.random.normal(ks[13], (MUL0 + MUL1, 1), jnp.float32)}
    _L2_gnn_all = _L2_gnn_setup()
    _L2_gnn_in = {k: v for k, v in _L2_gnn_all.items() if k in ('Wfc1', 'Wfc2', 'Wsc0', 'Wsc1', 'Wl1_0', 'Wl1_1', 'Wl2_s', 'Wl2_v', 'Wa')}
    del _L2_gnn_all

    def _L3_gnn_setup():
        import jax, jax.numpy as jnp
        import numpy as np
        MUL0, MUL1 = (64, 32)
        INV_SQRT3 = 1.0 / np.sqrt(3.0)

        def _split(x):
            return (x[:, :MUL0], x[:, MUL0:].reshape(x.shape[0], MUL1, 3))

        def _merge(o0, o1):
            return jnp.concatenate([o0, o1.reshape(o1.shape[0], -1)], axis=-1)

        def _tp(x0, x1, y0, y1, w000, w011, w101, w110):
            fan0 = x0.shape[1] * y0.shape[1] + x1.shape[1] * y1.shape[1]
            fan1 = x0.shape[1] * y1.shape[1] + x1.shape[1] * y0.shape[1]
            out0 = (jnp.einsum('eu,ev,uvw->ew', x0, y0, w000) + INV_SQRT3 * jnp.einsum('euk,evk,uvw->ew', x1, y1, w110)) / np.sqrt(fan0)
            out1 = (jnp.einsum('eu,evk,uvw->ewk', x0, y1, w011) + jnp.einsum('euk,ev,uvw->ewk', x1, y0, w101)) / np.sqrt(fan1)
            return (out0, out1)

        def _lin(x0, x1, w0, w1):
            return (x0 @ w0 / np.sqrt(x0.shape[1]), jnp.einsum('euk,uv->evk', x1, w1) / np.sqrt(x1.shape[1]))
        key = jax.random.key(seed)
        ks = jax.random.split(key, 20)
        N, E = (50000, 15625)
        inp = {'node_features': jax.random.normal(ks[0], (N, MUL0 + 3 * MUL1), dtype=jnp.float32), 'edge_index': jax.random.randint(ks[1], (2, E), 0, N, dtype=jnp.int64), 'edge_attr_tensor': jax.random.normal(ks[2], (E, 4), dtype=jnp.float32), 'node_attr_scalar_raw': jax.random.normal(ks[3], (N, 1), dtype=jnp.float32), 'wm000': jax.random.normal(ks[4], (MUL0, 1, MUL0), dtype=jnp.float32), 'wm011': jax.random.normal(ks[5], (MUL0, 1, MUL1), dtype=jnp.float32), 'wm101': jax.random.normal(ks[6], (MUL1, 1, MUL1), dtype=jnp.float32), 'wm110': jax.random.normal(ks[7], (MUL1, 1, MUL0), dtype=jnp.float32), 'lm0': jax.random.normal(ks[8], (MUL0, MUL0), dtype=jnp.float32), 'lm1': jax.random.normal(ks[9], (MUL1, MUL1), dtype=jnp.float32), 'wu000': jax.random.normal(ks[10], (MUL0, MUL0, MUL0), dtype=jnp.float32), 'wu011': jax.random.normal(ks[11], (MUL0, MUL1, MUL1), dtype=jnp.float32), 'wu101': jax.random.normal(ks[12], (MUL1, MUL0, MUL1), dtype=jnp.float32), 'wu110': jax.random.normal(ks[13], (MUL1, MUL1, MUL0), dtype=jnp.float32), 'lu0': jax.random.normal(ks[14], (MUL0, MUL0), dtype=jnp.float32), 'lu1': jax.random.normal(ks[15], (MUL1, MUL1), dtype=jnp.float32)}
        return inp
    _L3_gnn_all = _L3_gnn_setup()
    _L3_gnn_in = {k: v for k, v in _L3_gnn_all.items() if k in ('wm000', 'wm011', 'wm101', 'wm110', 'lm0', 'lm1', 'wu000', 'wu011', 'wu101', 'wu110', 'lu0', 'lu1')}
    del _L3_gnn_all
    return {'x': x, 'src': src, 'dst': dst, 'edge_attr_16': edge_attr_16, 'edge_attr_4': edge_attr_4, 'edge_attr_64': edge_attr_64, 'node_vec1': node_vec1, 'L0_gnn_Wm_ss': _L0_gnn_in['Wm_ss'], 'L0_gnn_Wm_vv': _L0_gnn_in['Wm_vv'], 'L0_gnn_Wm_sv': _L0_gnn_in['Wm_sv'], 'L0_gnn_Wm_vs': _L0_gnn_in['Wm_vs'], 'L0_gnn_Lm_s': _L0_gnn_in['Lm_s'], 'L0_gnn_Lm_v': _L0_gnn_in['Lm_v'], 'L0_gnn_Wu_ss': _L0_gnn_in['Wu_ss'], 'L0_gnn_Wu_vv': _L0_gnn_in['Wu_vv'], 'L0_gnn_Wu_sv': _L0_gnn_in['Wu_sv'], 'L0_gnn_Wu_vs': _L0_gnn_in['Wu_vs'], 'L0_gnn_Lu_s': _L0_gnn_in['Lu_s'], 'L0_gnn_Lu_v': _L0_gnn_in['Lu_v'], 'L1_gnn_lin1_ws': _L1_gnn_in['lin1_ws'], 'L1_gnn_lin1_wv': _L1_gnn_in['lin1_wv'], 'L1_gnn_fc_w1': _L1_gnn_in['fc_w1'], 'L1_gnn_fc_w2': _L1_gnn_in['fc_w2'], 'L1_gnn_sc_ws': _L1_gnn_in['sc_ws'], 'L1_gnn_sc_wv': _L1_gnn_in['sc_wv'], 'L1_gnn_lin2_ws': _L1_gnn_in['lin2_ws'], 'L1_gnn_lin2_wv': _L1_gnn_in['lin2_wv'], 'L2_gnn_Wfc1': _L2_gnn_in['Wfc1'], 'L2_gnn_Wfc2': _L2_gnn_in['Wfc2'], 'L2_gnn_Wsc0': _L2_gnn_in['Wsc0'], 'L2_gnn_Wsc1': _L2_gnn_in['Wsc1'], 'L2_gnn_Wl1_0': _L2_gnn_in['Wl1_0'], 'L2_gnn_Wl1_1': _L2_gnn_in['Wl1_1'], 'L2_gnn_Wl2_s': _L2_gnn_in['Wl2_s'], 'L2_gnn_Wl2_v': _L2_gnn_in['Wl2_v'], 'L2_gnn_Wa': _L2_gnn_in['Wa'], 'L3_gnn_wm000': _L3_gnn_in['wm000'], 'L3_gnn_wm011': _L3_gnn_in['wm011'], 'L3_gnn_wm101': _L3_gnn_in['wm101'], 'L3_gnn_wm110': _L3_gnn_in['wm110'], 'L3_gnn_lm0': _L3_gnn_in['lm0'], 'L3_gnn_lm1': _L3_gnn_in['lm1'], 'L3_gnn_wu000': _L3_gnn_in['wu000'], 'L3_gnn_wu011': _L3_gnn_in['wu011'], 'L3_gnn_wu101': _L3_gnn_in['wu101'], 'L3_gnn_wu110': _L3_gnn_in['wu110'], 'L3_gnn_lu0': _L3_gnn_in['lu0'], 'L3_gnn_lu1': _L3_gnn_in['lu1']}

def reference(x, src, dst, edge_attr_16, edge_attr_4, edge_attr_64, node_vec1, L0_gnn_Wm_ss, L0_gnn_Wm_vv, L0_gnn_Wm_sv, L0_gnn_Wm_vs, L0_gnn_Lm_s, L0_gnn_Lm_v, L0_gnn_Wu_ss, L0_gnn_Wu_vv, L0_gnn_Wu_sv, L0_gnn_Wu_vs, L0_gnn_Lu_s, L0_gnn_Lu_v, L1_gnn_lin1_ws, L1_gnn_lin1_wv, L1_gnn_fc_w1, L1_gnn_fc_w2, L1_gnn_sc_ws, L1_gnn_sc_wv, L1_gnn_lin2_ws, L1_gnn_lin2_wv, L2_gnn_Wfc1, L2_gnn_Wfc2, L2_gnn_Wsc0, L2_gnn_Wsc1, L2_gnn_Wl1_0, L2_gnn_Wl1_1, L2_gnn_Wl2_s, L2_gnn_Wl2_v, L2_gnn_Wa, L3_gnn_wm000, L3_gnn_wm011, L3_gnn_wm101, L3_gnn_wm110, L3_gnn_lm0, L3_gnn_lm1, L3_gnn_wu000, L3_gnn_wu011, L3_gnn_wu101, L3_gnn_wu110, L3_gnn_lu0, L3_gnn_lu1):
    import jax
    import jax.numpy as jnp

    def _L0_gnn_ref(node_features, edge_index, edge_attr_tensor, node_attr_scalar_raw, Wm_ss, Wm_vv, Wm_sv, Wm_vs, Lm_s, Lm_v, Wu_ss, Wu_vv, Wu_sv, Wu_vs, Lu_s, Lu_v):
        import jax, jax.numpy as jnp
        import numpy as np
        N = 625
        E = 20000
        INV_SQRT3 = 0.5773502691896258
        INV8 = 0.125
        INV_SQRT32 = 0.17677669529663687
        INV64 = 0.015625
        INV32 = 0.03125
        INV_SQRT2048 = 0.022097086912079608
        n = node_features.shape[0]
        e = edge_attr_tensor.shape[0]
        row, col = (edge_index[0], edge_index[1])
        r_vec = edge_attr_tensor[:, :3]
        dist = edge_attr_tensor[:, 3:4]
        xj = node_features[col]
        s = xj[:, :64]
        v = xj[:, 64:].reshape(e, 32, 3)
        m0 = s @ Wm_ss * dist * INV8 + jnp.einsum('eui,ei->eu', v, r_vec) @ Wm_vv * (INV_SQRT3 * INV_SQRT32)
        m1 = (s @ Wm_sv)[:, :, None] * r_vec[:, None, :] * INV8 + jnp.einsum('eui,uw->ewi', v, Wm_vs) * dist[:, :, None] * INV_SQRT32
        m0 = m0 + s @ Lm_s * INV8
        m1 = m1 + jnp.einsum('eui,uw->ewi', v, Lm_v) * INV_SQRT32
        msg = jnp.concatenate([m0, m1.reshape(e, 96)], axis=-1)
        agg = jax.ops.segment_sum(msg, row, num_segments=n)
        a0 = agg[:, :64]
        a1 = agg[:, 64:].reshape(n, 32, 3)
        xs = node_features[:, :64]
        xv = node_features[:, 64:].reshape(n, 32, 3)
        u0 = jnp.einsum('nu,nv,uvw->nw', xs, a0, Wu_ss) * INV64 + jnp.einsum('nui,nvi,uvw->nw', xv, a1, Wu_vv) * (INV_SQRT3 * INV32)
        u1 = jnp.einsum('nu,nvi,uvw->nwi', xs, a1, Wu_sv) * INV_SQRT2048 + jnp.einsum('nui,nv,uvw->nwi', xv, a0, Wu_vs) * INV_SQRT2048
        u0 = u0 + xs @ Lu_s * INV8
        u1 = u1 + jnp.einsum('nui,uw->nwi', xv, Lu_v) * INV_SQRT32
        upd = jnp.concatenate([u0, u1.reshape(n, 96)], axis=-1)
        return node_features + upd

    def _L1_gnn_ref(node_features, node_attr, edge_src, edge_dst, edge_attr, edge_scalars, lin1_ws, lin1_wv, fc_w1, fc_w2, sc_ws, sc_wv, lin2_ws, lin2_wv):
        import jax, jax.numpy as jnp
        import numpy as np
        N, E = (1250, 20000)
        S_IN, V_IN = (64, 32)
        S_MID, V_MID = (96, 128)
        S_OUT, V_OUT = (96, 32)
        R = 64
        FC_HID = 64
        W_NUMEL = 64 + 64 + 32 + 32 + 32
        NUM_NEIGHBORS = 16.0

        def _inv(d):
            return 1.0 / jnp.sqrt(jnp.float32(d))

        def _forward(node_features, node_attr, edge_attr, edge_scalars, lin1_ws, lin1_wv, fc_w1, fc_w2, sc_ws, sc_wv, lin2_ws, lin2_wv, edge_src, edge_dst):
            n = node_features.shape[0]
            s = node_features[:, :S_IN]
            v = node_features[:, S_IN:].reshape(n, V_IN, 3)
            a = node_attr
            sc_s = s @ sc_ws * a * _inv(S_IN)
            sc_v = jnp.einsum('nci,cd->ndi', v, sc_wv) * a[:, :, None] * _inv(V_IN)
            h_s = s @ lin1_ws * a * _inv(S_IN)
            h_v = jnp.einsum('nci,cd->ndi', v, lin1_wv) * a[:, :, None] * _inv(V_IN)
            hid = jax.nn.silu(edge_scalars @ fc_w1 * _inv(R))
            w = hid @ fc_w2 * _inv(FC_HID)
            w1, w2, w3, w4, w5 = jnp.split(w, [64, 128, 160, 192], axis=-1)
            es = h_s[edge_src]
            ev = h_v[edge_src]
            e0 = edge_attr[:, :1]
            e1 = edge_attr[:, 1:4]
            m_s1 = w1 * es * e0
            m_s2 = w4 * jnp.einsum('eci,ei->ec', ev, e1) * _inv(3)
            m_v1 = (w2 * es)[:, :, None] * e1[:, None, :]
            m_v2 = w3[:, :, None] * ev * e0[:, :, None]
            m_v3 = w5[:, :, None] * jnp.cross(ev, e1[:, None, :]) * _inv(2)
            mid_s = jnp.concatenate([m_s1, m_s2], axis=-1)
            mid_v = jnp.concatenate([m_v1, m_v2, m_v3], axis=1)
            inv_nn = 1.0 / jnp.sqrt(jnp.float32(NUM_NEIGHBORS))
            agg_s = jax.ops.segment_sum(mid_s, edge_dst, num_segments=n) * inv_nn
            agg_v = jax.ops.segment_sum(mid_v, edge_dst, num_segments=n) * inv_nn
            o_s = agg_s @ lin2_ws * a * _inv(S_MID)
            o_v = jnp.einsum('nci,cd->ndi', agg_v, lin2_wv) * a[:, :, None] * _inv(V_MID)
            pre_s = sc_s + o_s
            pre_v = sc_v + o_v
            scalars = jax.nn.silu(pre_s[:, :64])
            gates = jax.nn.sigmoid(pre_s[:, 64:96])
            gated = gates[:, :, None] * pre_v
            return jnp.concatenate([scalars, gated.reshape(n, 3 * V_OUT)], axis=-1)
        return _forward(node_features, node_attr, edge_attr, edge_scalars, lin1_ws, lin1_wv, fc_w1, fc_w2, sc_ws, sc_wv, lin2_ws, lin2_wv, edge_src, edge_dst)

    def _L2_gnn_ref(x, node_attr, edge_scalars, edge_attr_sh, edge_src, edge_dst, Wfc1, Wfc2, Wsc0, Wsc1, Wl1_0, Wl1_1, Wl2_s, Wl2_v, Wa):
        import jax, jax.numpy as jnp
        import numpy as np
        N = 625
        E = 10000
        MUL0 = 64
        MUL1 = 32
        FC_IN = 16
        FC_H = 64
        WNUM = 192
        n = x.shape[0]
        x0 = x[:, :MUL0]
        x1 = x[:, MUL0:].reshape(n, MUL1, 3)
        a = node_attr
        h = jax.nn.silu(edge_scalars @ (Wfc1 / jnp.sqrt(jnp.float32(FC_IN))))
        w = h @ (Wfc2 / jnp.sqrt(jnp.float32(FC_H)))
        w0 = w[:, :64]
        w1 = w[:, 64:128]
        w2 = w[:, 128:160]
        w3 = w[:, 160:192]
        inv8 = 1.0 / jnp.sqrt(jnp.float32(MUL0))
        inv32 = 1.0 / jnp.sqrt(jnp.float32(MUL1))
        sc = jnp.concatenate([x0 @ Wsc0 * a * inv8, (jnp.einsum('num,uv->nvm', x1, Wsc1) * a[..., None] * inv32).reshape(n, 3 * MUL1)], axis=1)
        f0 = x0 @ Wl1_0 * a * inv8
        f1 = jnp.einsum('num,uv->nvm', x1, Wl1_1) * a[..., None] * inv32
        e0 = f0[edge_src]
        e1 = f1[edge_src]
        sh0 = edge_attr_sh[:, :1]
        sh1 = edge_attr_sh[:, 1:4]
        mid0 = w0 * e0 * sh0
        mid1 = w3 * jnp.einsum('eum,em->eu', e1, sh1) / jnp.sqrt(3.0)
        mid2 = w1[:, :, None] * e0[:, :, None] * sh1[:, None, :]
        mid3 = w2[:, :, None] * e1 * sh0[:, :, None]
        cnt = jnp.clip(jax.ops.segment_sum(jnp.ones(edge_dst.shape, x.dtype), edge_dst, num_segments=n), 1.0)

        def smean(v):
            s = jax.ops.segment_sum(v, edge_dst, num_segments=n)
            return s / cnt.reshape((n,) + (1,) * (v.ndim - 1))
        n0, n1 = (smean(mid0), smean(mid1))
        n2, n3 = (smean(mid2), smean(mid3))
        scal = jnp.concatenate([n0, n1], axis=1)
        vec = jnp.concatenate([n2, n3], axis=1)
        inv96 = 1.0 / jnp.sqrt(jnp.float32(MUL0 + MUL1))
        alpha = scal @ Wa * a * inv96
        out_s = scal @ Wl2_s * a * inv96
        out_v = jnp.einsum('num,uv->nvm', vec, Wl2_v) * a[..., None] * inv96
        conv = jnp.concatenate([out_s, out_v.reshape(n, 3 * MUL1)], axis=1)
        return sc + alpha * conv

    def _L3_gnn_ref(node_features, edge_index, edge_attr_tensor, node_attr_scalar_raw, wm000, wm011, wm101, wm110, lm0, lm1, wu000, wu011, wu101, wu110, lu0, lu1):
        import jax, jax.numpy as jnp
        import numpy as np
        MUL0, MUL1 = (64, 32)
        INV_SQRT3 = 1.0 / np.sqrt(3.0)

        def _split(x):
            return (x[:, :MUL0], x[:, MUL0:].reshape(x.shape[0], MUL1, 3))

        def _merge(o0, o1):
            return jnp.concatenate([o0, o1.reshape(o1.shape[0], -1)], axis=-1)

        def _tp(x0, x1, y0, y1, w000, w011, w101, w110):
            fan0 = x0.shape[1] * y0.shape[1] + x1.shape[1] * y1.shape[1]
            fan1 = x0.shape[1] * y1.shape[1] + x1.shape[1] * y0.shape[1]
            out0 = (jnp.einsum('eu,ev,uvw->ew', x0, y0, w000) + INV_SQRT3 * jnp.einsum('euk,evk,uvw->ew', x1, y1, w110)) / np.sqrt(fan0)
            out1 = (jnp.einsum('eu,evk,uvw->ewk', x0, y1, w011) + jnp.einsum('euk,ev,uvw->ewk', x1, y0, w101)) / np.sqrt(fan1)
            return (out0, out1)

        def _lin(x0, x1, w0, w1):
            return (x0 @ w0 / np.sqrt(x0.shape[1]), jnp.einsum('euk,uv->evk', x1, w1) / np.sqrt(x1.shape[1]))
        N = node_features.shape[0]
        row, col = (edge_index[0], edge_index[1])
        r_vec = edge_attr_tensor[:, :3]
        dist = edge_attr_tensor[:, 3:4]
        e0 = dist
        e1 = r_vec[:, None, :]
        xj0, xj1 = _split(node_features[col])
        m0, m1 = _tp(xj0, xj1, e0, e1, wm000, wm011, wm101, wm110)
        d0, d1 = _lin(xj0, xj1, lm0, lm1)
        msgs = _merge(m0 + d0, m1 + d1)
        agg = jax.ops.segment_sum(msgs, row, num_segments=N)
        a0, a1 = _split(agg)
        x0, x1 = _split(node_features)
        u0, u1 = _tp(x0, x1, a0, a1, wu000, wu011, wu101, wu110)
        ud0, ud1 = _lin(x0, x1, lu0, lu1)
        return node_features + _merge(u0 + ud0, u1 + ud1)
    edge_index = jnp.stack([src, dst])
    x = _layernorm(x + _L0_gnn_ref(x, edge_index, edge_attr_4, node_vec1, L0_gnn_Wm_ss, L0_gnn_Wm_vv, L0_gnn_Wm_sv, L0_gnn_Wm_vs, L0_gnn_Lm_s, L0_gnn_Lm_v, L0_gnn_Wu_ss, L0_gnn_Wu_vv, L0_gnn_Wu_sv, L0_gnn_Wu_vs, L0_gnn_Lu_s, L0_gnn_Lu_v), axis=-1)
    x = _layernorm(x + _L1_gnn_ref(x, node_vec1, src, dst, edge_attr_4, edge_attr_64, L1_gnn_lin1_ws, L1_gnn_lin1_wv, L1_gnn_fc_w1, L1_gnn_fc_w2, L1_gnn_sc_ws, L1_gnn_sc_wv, L1_gnn_lin2_ws, L1_gnn_lin2_wv), axis=-1)
    x = _layernorm(x + _L2_gnn_ref(x, node_vec1, edge_attr_16, edge_attr_4, src, dst, L2_gnn_Wfc1, L2_gnn_Wfc2, L2_gnn_Wsc0, L2_gnn_Wsc1, L2_gnn_Wl1_0, L2_gnn_Wl1_1, L2_gnn_Wl2_s, L2_gnn_Wl2_v, L2_gnn_Wa), axis=-1)
    x = _layernorm(x + _L3_gnn_ref(x, edge_index, edge_attr_4, node_vec1, L3_gnn_wm000, L3_gnn_wm011, L3_gnn_wm101, L3_gnn_wm110, L3_gnn_lm0, L3_gnn_lm1, L3_gnn_wu000, L3_gnn_wu011, L3_gnn_wu101, L3_gnn_wu110, L3_gnn_lu0, L3_gnn_lu1), axis=-1)
    return x

_drawn_inputs = setup_inputs


def setup_inputs(seed=0):
    import zlib

    import numpy as np

    out = dict(_drawn_inputs(seed))
    spreads = {}
    factors = {'edge_attr_16': 8.0,
     'L2_gnn_Wfc1': 8.0,
     'L2_gnn_Wfc2': 8.0,
     'L2_gnn_Wl1_0': 8.0,
     'L2_gnn_Wl1_1': 8.0,
     'L2_gnn_Wl2_s': 8.0,
     'L2_gnn_Wl2_v': 8.0,
     'L2_gnn_Wa': 8.0}
    for name, (base, spread) in spreads.items():
        noise = np.random.default_rng([zlib.crc32(name.encode()), seed]).standard_normal(out[name].shape)
        drawn = base * np.exp(spread * noise) if base else spread * noise
        out[name] = jnp.asarray(drawn.astype(out[name].dtype))
    for name, factor in factors.items():
        out[name] = (out[name] * factor).astype(out[name].dtype)
    return out
```

```python
import numpy as np

N, E, C = 3125, 50000, 160
P = 128
NS, NV = 64, 32
NT = -(-N // P)
NFULL = N // P
NREST = N - NFULL * P
GROUP = 256
TPG = GROUP // P
NG = (E + NT * (GROUP - 1)) // GROUP
T = NG * TPG
EJ = -(-E // P)
EDUP = P * EJ - E
WS, WD = 6, 86
D_E64, D_E16, D_E4, D_IDX, D_LOC = 0, 64, 80, 84, 85
S_E4, S_IDX, S_LOC = 0, 4, 5
OV = {0: 96, 1: 0, 2: 128}
OS = 32
SLOTS = 4


def permutation():
    cols = [NS + 3 * c + 1 for c in range(NV)] + list(range(NS))
    cols += [NS + 3 * c for c in range(NV)] + [NS + 3 * c + 2 for c in range(NV)]
    return np.array(cols)


def build(nc, t, out):
    import concourse.bass as bass
    from concourse import mybir
    from contextlib import ExitStack

    F32, BF16, I32, U32 = mybir.dt.float32, mybir.dt.bfloat16, mybir.dt.int32, mybir.dt.uint32
    ALU = mybir.AluOpType
    ACT = mybir.ActivationFunctionType
    ds = bass.ds

    top = ExitStack()

    def sb(scope, name, shape, dt=F32):
        return scope.enter_context(nc.sbuf_tensor(name, shape, dt))

    def ps(scope, name, shape, dt=F32):
        return scope.enter_context(nc.psum_tensor(name, shape, dt))

    def wait(eng, sem, value):
        if not (isinstance(value, int) and value <= 0):
            eng.wait_ge(sem, value)

    def steps(eng, count, unroll, body, tail=0):
        for i in range(unroll):
            body(i, i, 0)
        turns = (count - tail) // unroll
        with eng.Fori(1, turns) as it:
            for k in range(unroll):
                body(it * unroll + k, k, it)
        for i in range(turns * unroll, count):
            body(i, i % unroll, i // unroll)

    rec_s = nc.dram_tensor("rec_s", (P * T + EJ, WS), F32, kind="Internal").ap()
    rec_d = nc.dram_tensor("rec_d", (P * T + EJ, WD), F32, kind="Internal").ap()
    h_dram = nc.dram_tensor("h_rows", (NT * P, C), F32, kind="Internal").ap()

    with top:
        in_use = []

        def sem(name):
            in_use.append(nc.alloc_semaphore(name))
            return in_use[-1]

        def stand(eng, sem_):
            eng.sem_inc(sem_, 1)

        def end_stage():
            nc.clear_and_free_semaphores(in_use)
            in_use.clear()
            nc.all_engine_barrier()

        x = sb(top, "x", [P, NT, C])
        attr = sb(top, "attr", [P, NT])
        iota = sb(top, "iota", [P, P])
        ident = sb(top, "ident", [P, P])
        identb = sb(top, "identb", [P, P], BF16)
        sel2 = sb(top, "sel2", [96, 16, P], BF16)
        sel4 = sb(top, "sel4", [96, 8, P], BF16)
        gtile = {"s": sb(top, "gtile_s", [1, NG], I32), "d": sb(top, "gtile_d", [1, NG], I32)}
        loc = {k: sb(top, f"loc_{k}", [P, EJ]) for k in "sd"}
        pos = {k: sb(top, f"pos_{k}", [P, EJ], I32) for k in "sd"}
        key_i = {k: sb(top, f"key_{k}", [P, EJ], I32) for k in "sd"}
        nidx = sb(top, "nidx", [P, 1])
        k31 = sb(top, "k31", [P, 1])
        pidx_i = sb(top, "pidx_i", [P, 2], I32)
        tri = sb(top, "tri", [P, P])
        ones_sq = sb(top, "ones_sq", [P, P])
        bval = sb(top, "bval", [P, NT + 1])

        with ExitStack() as sc:
            ramp_i = sb(sc, "ramp_i", [P, P], I32)
            sel2_i = sb(sc, "sel2_i", [96, 16 * P], I32)
            sel4_i = sb(sc, "sel4_i", [96, 8 * P], I32)
            empty_s = sb(sc, "empty_s", [P, T, WS])
            EMPTY = 22
            empty_d = sb(sc, "empty_d", [P, EMPTY, WD])
            const_ints = sem("const_ints")
            empties = sem("empties")
            empty_zero = sem("empty_zero")
            loads = sem("loads")
            cleared = sem("cleared")
            written = sem("empty_written")
            dve_step = sem("const_step")
            with nc.Block() as block:
                @block.gpsimd
                def _(pool):
                    nc.gpsimd.iota(ramp_i[:], [[1, P]], base=0, channel_multiplier=0).then_inc(const_ints, 1)
                    nc.gpsimd.iota(pidx_i[:, 0:1], [[1, 1]], base=0, channel_multiplier=1).then_inc(const_ints, 1)
                    nc.gpsimd.iota(sel2_i[:], [[2, 16], [1, 2], [0, 64]], base=0, channel_multiplier=0).then_inc(const_ints, 1)
                    nc.gpsimd.iota(sel4_i[:], [[4, 8], [1, 4], [0, 32]], base=0, channel_multiplier=0).then_inc(const_ints, 1)
                    nc.gpsimd.memset(empty_s[:], 0.0).then_inc(empty_zero, 1)
                    nc.gpsimd.memset(empty_d[:], 0.0).then_inc(empty_zero, 1)
                    pool.wait_ge(empty_zero, 2)
                    nc.gpsimd.memset(empty_s[:, :, S_LOC:S_LOC + 1], -1.0).then_inc(empties, 1)
                    nc.gpsimd.memset(empty_d[:, :, D_LOC:D_LOC + 1], -1.0).then_inc(empties, 1)

                @block.sync
                def _(sp):
                    n = 0
                    for k in "sd":
                        src = t["src" if k == "s" else "dst"]
                        sp.dma_start(key_i[k][0:P - 1, :], src[0:(P - 1) * EJ].rearrange("(p j) -> p j", j=EJ)).then_inc(loads, 16)
                        sp.dma_start(key_i[k][P - 1:P, :], src[E - EJ:E].rearrange("(p j) -> p j", j=EJ)).then_inc(loads, 16)
                        n += 32
                    sp.wait_ge(cleared, 2)
                    sp.dma_start(x[:, 0:NFULL, :], t["x"][0:NFULL * P, :].rearrange("(t p) c -> p t c", p=P)).then_inc(loads, 16)
                    sp.dma_start(x[0:NREST, NFULL, :], t["x"][NFULL * P:N, :]).then_inc(loads, 16)
                    with nc.allow_non_contiguous_dma(reason="one word a node"):
                        sp.dma_start(attr[:, 0:NFULL], t["node_vec1"][0:NFULL * P, :].rearrange("(t p) o -> p (t o)", p=P)).then_inc(loads, 16)
                    sp.dma_start(attr[0:NREST, NFULL:NT], t["node_vec1"][NFULL * P:N, :]).then_inc(loads, 16)
                    n += 64
                    sp.wait_ge(empties, 2)
                    sp.dma_start(rec_s[0:P * T, :].rearrange("(p t) w -> p (t w)", t=T), empty_s[:].rearrange("p t w -> p (t w)")).then_inc(written, 16)
                    for i in range(T // EMPTY):
                        sp.dma_start(rec_d[0:P * T, :].rearrange("(p t) w -> p t w", t=T)[:, i * EMPTY:(i + 1) * EMPTY, :],
                                     empty_d[:]).then_inc(written, 16)
                    sp.wait_ge(written, 16 * (1 + T // EMPTY))
                    sp.wait_ge(loads, n)

                @block.vector
                def _(dve):
                    done = [0]

                    def link(ins):
                        done[0] += 1
                        ins.then_inc(dve_step, 1)
                        dve.wait_ge(dve_step, done[0])

                    nc.vector.memset(x[:, NFULL, :], 0.0).then_inc(cleared, 1)
                    nc.vector.memset(attr[:, NFULL:NT], 0.0).then_inc(cleared, 1)
                    link(nc.vector.memset(ones_sq[:], 1.0))
                    dve.wait_ge(const_ints, 4)
                    link(nc.vector.tensor_copy(iota[:], ramp_i[:]))
                    link(nc.vector.tensor_copy(bval[:], iota[:, 0:NT + 1]))
                    link(nc.vector.tensor_copy(nidx[:], pidx_i[:, 0:1]))
                    link(nc.vector.tensor_scalar(pidx_i[:, 1:2], pidx_i[:, 0:1], 31, None, ALU.bitwise_and))
                    link(nc.vector.tensor_copy(k31[:], pidx_i[:, 1:2]))
                    link(nc.vector.tensor_scalar(ident[:], iota[:], nidx[:, 0:1], None, ALU.is_equal))
                    link(nc.vector.tensor_copy(identb[:], ident[:]))
                    link(nc.vector.tensor_scalar(tri[:], iota[:], nidx[:, 0:1], None, ALU.is_gt))
                    link(nc.vector.tensor_scalar(sel2[:].rearrange("k c p -> k (c p)"), sel2_i[:], k31[0:96, 0:1], None, ALU.is_equal))
                    link(nc.vector.tensor_scalar(sel4[:].rearrange("k c p -> k (c p)"), sel4_i[:], k31[0:96, 0:1], None, ALU.is_equal))

        def order(k, row_words):
            with ExitStack() as sc:
                n = f"_{k}"
                key2 = sb(sc, "key2" + n, [P, EJ], I32)
                part_i = sb(sc, "part_i" + n, [P, EJ], I32)
                kt = sb(sc, "kt" + n, [P, EJ])
                ones = sb(sc, "ones" + n, [P, EJ])
                mask = sb(sc, "mask" + n, [P, EJ])
                cum = sb(sc, "cum" + n, [P, EJ])
                prod = sb(sc, "prod" + n, [P, EJ])
                q = sb(sc, "q" + n, [P, EJ])
                counts = sb(sc, "counts" + n, [P, NT])
                small = sb(sc, "small" + n, [P, 8, NT])
                small_i = sb(sc, "small_i" + n, [P, 2, NT], I32)
                ramp_g = sb(sc, "ramp_g" + n, [P, EJ], I32)
                ramp_f = sb(sc, "ramp_f" + n, [P, EJ])
                gt = sb(sc, "gt" + n, [1, NG])
                before = ps(sc, "before" + n, [P, NT])
                total = ps(sc, "total" + n, [P, NT])
                keys_marked = sem("keys_marked" + n)
                ramp_ready = sem("ramp_ready" + n)
                counted = sem("counted" + n)
                summed = sem("summed" + n)
                step = sem("order_step" + n)
                b_mask, b_cum, b_prod, b_q = (sem(f"{a}{n}") for a in ("b_mask", "b_cum", "b_prod", "b_q"))
                with nc.Block() as block:
                    @block.gpsimd
                    def _(pool):
                        nc.gpsimd.affine_select(out=key2[:], in_=key_i[k][:], compare_op=ALU.is_ge, fill=float(NT * P),
                                                base=(P - 1) * 1000 - EDUP, pattern=[[1, EJ]], channel_multiplier=-1000).then_inc(keys_marked, 1)
                        nc.gpsimd.iota(ramp_g[:], [[1, EJ]], base=0, channel_multiplier=0).then_inc(ramp_ready, 1)

                    @block.tensor
                    def _(pe):
                        pe.wait_ge(counted, NT)
                        nc.tensor.matmul(before[:], tri[:], counts[:], start=True, stop=True).then_inc(summed, 1)
                        nc.tensor.matmul(total[:], ones_sq[:], counts[:], start=True, stop=True).then_inc(summed, 1)

                    @block.vector
                    def _(dve):
                        done = [0]

                        def link(ins):
                            done[0] += 1
                            ins.then_inc(step, 1)
                            dve.wait_ge(step, done[0])

                        dve.wait_ge(keys_marked, 1)
                        link(nc.vector.tensor_scalar(part_i[:], key2[:], 7, None, ALU.arith_shift_right))
                        link(nc.vector.tensor_copy(kt[:], part_i[:]))
                        link(nc.vector.tensor_scalar(part_i[:], key2[:], P - 1, None, ALU.bitwise_and))
                        link(nc.vector.tensor_copy(loc[k][:], part_i[:]))
                        link(nc.vector.memset(ones[:], 1.0))
                        link(nc.vector.memset(q[:], 0.0))
                        for b in range(NT):
                            nc.vector.tensor_scalar(mask[:], kt[:], float(b), None, ALU.is_equal, ALU.add,
                                                    accum_out=counts[:, b:b + 1]).then_inc(counted, 1)
                            dve.wait_ge(counted, b + 1)
                        dve.wait_ge(summed, 2)
                        tot, grp, end, base, off = (small[:, i, :] for i in range(5))
                        link(nc.vector.tensor_scalar(tot, total[:], float(GROUP - 1), None, ALU.add))
                        link(nc.vector.tensor_copy(small_i[:, 0, :], tot))
                        link(nc.vector.tensor_scalar(small_i[:, 1, :], small_i[:, 0, :], GROUP.bit_length() - 1, None, ALU.arith_shift_right))
                        link(nc.vector.tensor_copy(grp, small_i[:, 1, :]))
                        link(nc.vector.tensor_tensor_scan(end, ones[:, 0:NT], grp, 0.0, ALU.mult, ALU.add))
                        link(nc.vector.tensor_tensor(base, end, grp, ALU.subtract))
                        link(nc.vector.tensor_scalar(base, base, float(GROUP), -1.0, ALU.mult, ALU.add))
                        link(nc.vector.tensor_tensor(off, before[:], base, ALU.add))
                        with dve.Fori(0, NT) as b:
                            nc.vector.tensor_scalar(mask[:], kt[:], bval[:, ds(b, 1)], None, ALU.is_equal).then_inc(b_mask, 1)
                            dve.wait_ge(b_mask, b + 1)
                            nc.vector.tensor_tensor_scan(cum[:], ones[:], mask[:], small[:, 4, ds(b, 1)], ALU.mult, ALU.add).then_inc(b_cum, 1)
                            dve.wait_ge(b_cum, b + 1)
                            nc.vector.tensor_tensor(prod[:], mask[:], cum[:], ALU.mult).then_inc(b_prod, 1)
                            dve.wait_ge(b_prod, b + 1)
                            nc.vector.tensor_tensor(q[:], q[:], prod[:], ALU.add).then_inc(b_q, 1)
                            dve.wait_ge(b_q, b + 1)
                        dve.wait_ge(ramp_ready, 1)
                        link(nc.vector.tensor_copy(pos[k][:], q[:]))
                        link(nc.vector.tensor_scalar(part_i[:], pos[k][:], P - 1, None, ALU.bitwise_and))
                        link(nc.vector.tensor_copy(mask[:], part_i[:]))
                        link(nc.vector.tensor_scalar(part_i[:], pos[k][:], 7, None, ALU.arith_shift_right))
                        link(nc.vector.tensor_copy(cum[:], part_i[:]))
                        link(nc.vector.scalar_tensor_tensor(q[:], mask[:], float(T), cum[:], ALU.mult, ALU.add))
                        link(nc.vector.tensor_copy(ramp_f[:], ramp_g[:]))
                        link(nc.vector.tensor_scalar(mask[:], kt[:], float(NT), None, ALU.is_equal))
                        link(nc.vector.scalar_tensor_tensor(prod[:], ramp_f[:], float(P * T), mask[:], ALU.add, ALU.mult))
                        link(nc.vector.tensor_tensor(q[:], q[:], prod[:], ALU.add))
                        link(nc.vector.tensor_copy(pos[k][:], q[:]))
                        link(nc.vector.memset(gt[:], 0.0))
                        for b in range(NT - 1):
                            link(nc.vector.scalar_tensor_tensor(gt[:], ramp_f[0:1, 0:NG], end[0:1, b:b + 1], gt[:], ALU.is_ge, ALU.add))
                        link(nc.vector.tensor_copy(gtile[k][:], gt[:]))

        def scatter(k):
            rec, words = (rec_s, WS) if k == "s" else (rec_d, WD)
            c_idx, c_loc, c_e4 = (S_IDX, S_LOC, S_E4) if k == "s" else (D_IDX, D_LOC, D_E4)
            other = key_i["d" if k == "s" else "s"]
            halves = (12, 11)
            per = sum(halves)
            turns = EJ // per
            pieces = [("edge_attr_4", c_e4, 4)]
            if k == "d":
                pieces += [("edge_attr_64", D_E64, 64), ("edge_attr_16", D_E16, 16)]
            with ExitStack() as sc:
                stage = [sb(sc, f"stage{h}_{k}", [P, halves[h], words]) for h in range(2)]
                place = [sb(sc, f"place{h}_{k}", [P, halves[h]], I32) for h in range(2)]
                loaded = [sem(f"loaded{h}_{k}") for h in range(2)]
                filled = [sem(f"filled{h}_{k}") for h in range(2)]
                sent = [sem(f"sent{h}_{k}") for h in range(2)]
                issued, turn_begun = sem(f"scatter_turn_{k}"), sem(f"turn_begun_{k}")
                with nc.Block() as block:
                    @block.sync
                    def _(sp):
                        def turn(i, h):
                            wait(sp, sent[h], i * (16 * halves[h]))
                            j0 = i * per + (halves[0] if h else 0)
                            for name, col, w in pieces:
                                src = t[name]
                                body = src[0:(P - 1) * EJ, :].rearrange("(p j) w -> p j w", j=EJ)
                                last = src[E - EJ:E, :].rearrange("(p j) w -> p j w", j=EJ)
                                sp.dma_start(stage[h][0:P - 1, :, col:col + w], body[:, ds(j0, halves[h]), :]).then_inc(loaded[h], 16)
                                sp.dma_start(stage[h][P - 1:P, :, col:col + w], last[:, ds(j0, halves[h]), :]).then_inc(loaded[h], 16)
                        for h in range(2):
                            turn(0, h)
                        with sp.Fori(1, turns) as i:
                            for h in range(2):
                                turn(i, h)

                    @block.gpsimd
                    def _(pool):
                        def turn(i, h):
                            m = halves[h]
                            j0 = i * per + (halves[0] if h else 0)
                            pool.wait_ge(loaded[h], (i + 1) * (32 * len(pieces)))
                            wait(pool, sent[h], i * (16 * m))
                            stand(pool, turn_begun)
                            nc.gpsimd.tensor_copy(stage[h][:, :, c_idx:c_idx + 1].bitcast(I32).rearrange("p m o -> p (m o)"), other[:, ds(j0, m)]).then_inc(filled[h], 1)
                            nc.gpsimd.tensor_copy(stage[h][:, :, c_loc:c_loc + 1].rearrange("p m o -> p (m o)"), loc[k][:, ds(j0, m)]).then_inc(filled[h], 1)
                            nc.gpsimd.tensor_copy(place[h][:], pos[k][:, ds(j0, m)]).then_inc(filled[h], 1)
                            pool.wait_ge(filled[h], (i + 1) * 3)
                            stand(pool, issued)
                            for c in range(m):
                                pool.indirect_dma_start(rec, bass.IndirectOffsetOnAxis(place[h][:, c:c + 1].bitcast(U32), 0),
                                                        stage[h][:, c, :], None).then_inc(sent[h], 16)
                        for h in range(2):
                            turn(0, h)
                        with pool.Fori(1, turns) as i:
                            for h in range(2):
                                turn(i, h)
                        for h in range(2):
                            pool.wait_ge(sent[h], 16 * halves[h] * turns)

        end_stage()
        order("s", WS)
        scatter("s")
        order("d", WD)
        scatter("d")
        end_stage()

        def node_rows(dram):
            return dram.rearrange("(t p) c -> p t c", p=P)

        def one(ap):
            return ap.rearrange("p o c -> p (o c)")

        def layernorm(n, to_output=False):
            with ExitStack() as sc:
                stats = sb(sc, f"stats_{n}", [P, NT, 6])
                mv = sb(sc, f"mv_{n}", [P, NT, 2])
                rstd = sb(sc, f"rstd_{n}", [P, NT])
                stats_ready, mv_ready, eps_added = sem(f"stats_ready_{n}"), sem(f"mv_ready_{n}"), sem(f"eps_added_{n}")
                rooted, inverted, normed = sem(f"rooted_{n}"), sem(f"inverted_{n}"), sem(f"normed_{n}")
                x_out = sem(f"x_out_{n}")
                with nc.Block() as block:
                    @block.vector
                    def _(dve):
                        with dve.Fori(0, NT) as nt:
                            nc.vector.bn_stats(one(stats[:, ds(nt, 1), :]), one(x[:, ds(nt, 1), :])).then_inc(stats_ready, 1)
                        dve.wait_ge(stats_ready, NT)
                        for nt in range(NT):
                            nc.vector.bn_aggr(mv[:, nt, :], stats[:, nt, :]).then_inc(mv_ready, 1)
                        dve.wait_ge(mv_ready, NT)
                        nc.vector.tensor_scalar(rstd[:].unsqueeze(2), mv[:, :, 1:2], 1e-5, None, ALU.add).then_inc(eps_added, 1)
                        dve.wait_ge(rooted, 1)
                        nc.vector.reciprocal(rstd[:], rstd[:]).then_inc(inverted, 1)
                        dve.wait_ge(inverted, 1)
                        for nt in range(NT):
                            nc.vector.tensor_scalar(x[:, nt, :], x[:, nt, :], mv[:, nt, 0:1], rstd[:, nt:nt + 1],
                                                    ALU.subtract, ALU.mult).then_inc(normed, 1)

                    @block.scalar
                    def _(act):
                        act.wait_ge(eps_added, 1)
                        nc.scalar.activation(rstd[:], rstd[:], ACT.Sqrt).then_inc(rooted, 1)

                    @block.sync
                    def _(sp):
                        sp.wait_ge(normed, NT)
                        if to_output:
                            sp.dma_start(node_rows(out[0:NFULL * P, :]), x[:, 0:NFULL, :]).then_inc(x_out, 16)
                            sp.dma_start(out[NFULL * P:N, :], x[0:NREST, NFULL, :]).then_inc(x_out, 16)
                            sp.wait_ge(x_out, 32)
                        else:
                            sp.dma_start(node_rows(h_dram), x[:]).then_inc(x_out, 16)
                            sp.wait_ge(x_out, 16)

        A_T, A_W = 512, 544

        def product_layer(n, rows, w, scales):
            rec = rec_s[0:P * T, :].rearrange("(p t) w -> p t w", t=T)
            layer = ExitStack()
            with layer:
                acc = sb(layer, f"acc_{n}", [P, NT, A_W])
                raw0 = sb(layer, f"raw0_{n}", [P, NS])
                rawt = sb(layer, f"rawt_{n}", [NV, NS])
                raw1 = sb(layer, f"raw1_{n}", [P, NV])
                w0 = sb(layer, f"w0_{n}", [P, 2, NS])
                wt = sb(layer, f"wt_{n}", [NV, 2, NS])
                w1 = sb(layer, f"w1_{n}", [P, 4, NV])
                wss = sb(layer, f"wss_{n}", [P, 32, NS])
                wvv = sb(layer, f"wvv_{n}", [P, 8, NS])
                wsv = sb(layer, f"wsv_{n}", [P, 16, NV])
                wvs = sb(layer, f"wvs_{n}", [P, 16, NV])
                lus = sb(layer, f"lus_{n}", [NS, NS])
                luv = sb(layer, f"luv_{n}", [NV, NV])
                w_in, w_scaled = sem(f"weights_in_{n}"), sem(f"weights_scaled_{n}")

                with ExitStack() as sc:
                    recb = [sb(sc, f"recb{i}_{n}", [P, TPG, WS]) for i in range(SLOTS)]
                    rowb = [sb(sc, f"rowb{i}_{n}", [P, TPG, C]) for i in range(SLOTS)]
                    oh = [sb(sc, f"oh{i}_{n}", [P, TPG, 5, P]) for i in range(2)]
                    psa = [ps(sc, f"psa{i}_{n}", [P, 512]) for i in range(2)]
                    psb = [ps(sc, f"psb{i}_{n}", [P, 512]) for i in range(2)]
                    rec_in = [sem(f"rec_in{i}_{n}") for i in range(SLOTS)]
                    rows_in = [sem(f"rows_in{i}_{n}") for i in range(SLOTS)]
                    acc_zero, oh_ready, agg_done, evac_done = (sem(f"{a}_{n}") for a in ("acc_zero", "oh_ready", "agg_done", "evac_done"))
                    gather_turn = sem(f"gather_turn_{n}")
                    with nc.Block() as block:
                        @block.sync
                        def _(sp):
                            def body(g, slot, turn):
                                wait(sp, agg_done, g - (SLOTS - 1))
                                sp.dma_start(recb[slot][:], rec[:, ds(TPG * g, TPG), :]).then_inc(rec_in[slot], 16)
                            steps(sp, NG, SLOTS, body)

                        @block.scalar
                        def _(act):
                            nw = 0
                            for dst, src in (
                                    (raw0[0:64, :], w["lm_s"]), (raw0[64:128, :], w["wm_ss"]), (rawt[:], w["wm_vv"]),
                                    (raw1[0:64, :], w["wm_sv"]), (raw1[64:96, :], w["lm_v"]), (raw1[96:128, :], w["wm_vs"]),
                                    (lus[:], w["lu_s"]), (luv[:], w["lu_v"]),
                                    (wss[:], w["wu_ss"].rearrange("u v w -> (u v) w").rearrange("(c p) w -> p c w", p=P)),
                                    (wvv[:], w["wu_vv"].rearrange("u v w -> (u v) w").rearrange("(c p) w -> p c w", p=P)),
                                    (wsv[:], w["wu_sv"].rearrange("u v w -> (u v) w").rearrange("(c p) w -> p c w", p=P)),
                                    (wvs[:], w["wu_vs"].rearrange("u v w -> (u v) w").rearrange("(c p) w -> p c w", p=P))):
                                act.dma_start(dst, src).then_inc(w_in, 16)
                                nw += 16
                            act.wait_ge(w_in, nw)
                            for r in range(2):
                                nc.scalar.mul(w0[0:64, r, :], raw0[0:64, :], scales["lm_s"])
                                nc.scalar.mul(w0[64:128, r, :], raw0[64:128, :], scales["wm_ss"])
                                nc.scalar.mul(wt[:, r, :], rawt[:], scales["wm_vv"])
                            for r in range(4):
                                nc.scalar.mul(w1[0:64, r, :], raw1[0:64, :], scales["wm_sv"])
                                nc.scalar.mul(w1[64:96, r, :], raw1[64:96, :], scales["lm_v"])
                                nc.scalar.mul(w1[96:128, r, :], raw1[96:128, :], scales["wm_vs"])
                            for a, s in ((wss, "wu_ss"), (wvv, "wu_vv"), (wsv, "wu_sv"), (wvs, "wu_vs")):
                                nc.scalar.mul(a[:], a[:], scales[s])
                            nc.scalar.mul(lus[:], lus[:], scales["lu_s"])
                            nc.scalar.mul(luv[:], luv[:], scales["lu_v"]).then_inc(w_scaled, 1)

                        @block.gpsimd
                        def _(pool):
                            def body(g, slot, turn):
                                pool.wait_ge(rec_in[slot], (turn + 1) * 16)
                                wait(pool, agg_done, g - (SLOTS - 1))
                                stand(pool, gather_turn)
                                for k in range(TPG):
                                    pool.indirect_dma_start(rowb[slot][:, k, :], None, rows,
                                                            bass.IndirectOffsetOnAxis(recb[slot][:, k, S_IDX:S_IDX + 1].bitcast(U32), 0)).then_inc(rows_in[slot], 16)
                            steps(pool, NG, SLOTS, body)

                        @block.vector
                        def _(dve):
                            def build(g, slot, turn):
                                dve.wait_ge(rec_in[slot], (turn + 1) * 16)
                                wait(dve, agg_done, g - 1)
                                for k in range(TPG):
                                    where = recb[slot][:, k, S_LOC:S_LOC + 1]
                                    nc.vector.tensor_scalar(oh[slot % 2][:, k, 4, :], iota[:], where, None, ALU.is_equal)
                                    for c in range(4):
                                        last = nc.vector.tensor_scalar(oh[slot % 2][:, k, c, :], iota[:], where,
                                                                       recb[slot][:, k, S_E4 + c:S_E4 + c + 1], ALU.is_equal, ALU.mult)
                                last.then_inc(oh_ready, 1)

                            def body(g, slot, turn):
                                if not (isinstance(g, int) and g == NG - 1):
                                    build(g + 1, (slot + 1) % SLOTS, turn + (slot == SLOTS - 1))
                                tile = dve.value_load(gtile["s"][0:1, ds(g, 1)], min_val=0, max_val=NT - 1)
                                dve.wait_ge(agg_done, g + 1)
                                wait(dve, evac_done, g)
                                a = one(acc[:, ds(tile, 1), :])
                                pa, pb = psa[slot % 2], psb[slot % 2]
                                two = pa[:, 0:2 * C].rearrange("p (a c) -> p a c", a=2)
                                vec = a[:, P:A_T].rearrange("p (i c) -> p i c", i=3)

                                def add(dst, src):
                                    return nc.vector.tensor_tensor(dst, src, dst, ALU.add)
                                add(a[:, 0:P].rearrange("p (a c) -> p a c", a=2), two[:, :, OS:OS + NS])
                                add(vec[:, 1, NS:P].rearrange("p (a c) -> p a c", a=2), two[:, :, 0:NV])
                                add(vec[:, 0:3:2, NS:P].rearrange("p i (a c) -> p i a c", a=2),
                                    two[:, :, OV[0]:C].rearrange("p a (i c) -> p i a c", i=2))
                                add(vec[:, 1:3, 0:NS], pb[:, 96:224].rearrange("p (i c) -> p i c", i=2))
                                add(vec[:, 0, 0:NS], pb[:, 0:64])
                                add(a[:, A_T:A_W], pb[:, 64:96]).then_inc(evac_done, 1)

                            nc.vector.memset(acc[:], 0.0).then_inc(acc_zero, 1)
                            build(0, 0, 0)
                            dve.wait_ge(acc_zero, 1)
                            steps(dve, NG, SLOTS, body, tail=1)

                        @block.tensor
                        def _(pe):
                            def body(g, slot, turn):
                                pe.wait_ge(oh_ready, g + 1)
                                pe.wait_ge(rows_in[slot], (turn + 1) * (16 * TPG))
                                wait(pe, evac_done, g - 1)
                                pa, pb = psa[slot % 2], psb[slot % 2]
                                for k in range(TPG):
                                    o, r, first, last = oh[slot % 2][:, k], rowb[slot][:, k, :], k == 0, k == TPG - 1

                                    def mm(dst, coef, cols, start=False, stop=False):
                                        return nc.tensor.matmul(dst, o[:, coef, :], cols, start=start, stop=stop, skip_group_check=True)
                                    mm(pa[:, 0:C], 4, r[:], first, False)
                                    mm(pa[:, C:2 * C], w["dist"], r[:], False, last)
                                    rx, ry, rz = w["r"]
                                    mm(pb[:, 0:96], rx, r[:, OS:OS + 96], first, False)
                                    mm(pb[:, 64:160], ry, r[:, 0:96], False, False)
                                    mm(pb[:, 160:224], rz, r[:, OS:OS + NS], False, False)
                                    end = mm(pb[:, 64:96], rz, r[:, OV[2]:OV[2] + NV], False, last)
                                end.then_inc(agg_done, 1)
                            steps(pe, NG, SLOTS, body)

                items = []
                for gp in (1, 2):
                    for q in range(4):
                        items.append((sel2, 4 * q, gp, 0, 1, wss, 16 * (gp - 1) + 4 * q, [(OS, NS)]))
                group_of = {0: 3, 1: 0, 2: 4}
                for i in range(3):
                    for q in range(2):
                        items.append((sel4, 4 * q, group_of[i], 1 + i, 1, wvv, 4 * q, [(OS, NS)]))
                for gp in (1, 2):
                    for q in range(2):
                        items.append((sel4, 4 * q, gp, 1, 3, wsv, 8 * (gp - 1) + 4 * q, [(OV[i], NV) for i in range(3)]))
                for i in range(3):
                    for q in range(4):
                        items.append((sel2, 4 * q, group_of[i], 0, 1, wvs, 4 * q, [(OV[i], NV)]))
                NI = len(items)
                T_AT, B_AT = NI // 3, 2 * NI // 3

                with ExitStack() as sc:
                    stg = [sb(sc, f"stg{i}_{n}", [P, A_W]) for i in range(2)]
                    xst = [sb(sc, f"xst{i}_{n}", [P, C]) for i in range(2)]
                    xsp = [sb(sc, f"xsp{i}_{n}", [P, 5, 3, NV], BF16) for i in range(2)]
                    rest = [sb(sc, f"rest{i}_{n}", [P, 2, C]) for i in range(2)]
                    cT = [sb(sc, f"cT{i}_{n}", [P, 512]) for i in range(2)]
                    tT = [sb(sc, f"tT{i}_{n}", [NV, P]) for i in range(2)]
                    xsT = [sb(sc, f"xsT{i}_{n}", [NS, P]) for i in range(2)]
                    xvT = [sb(sc, f"xvT{i}_{n}", [NV, 3 * P]) for i in range(2)]
                    xpT = [sb(sc, f"xpT{i}_{n}", [96, 5, P], BF16) for i in range(2)]
                    aT = [sb(sc, f"aT{i}_{n}", [P, 4, P]) for i in range(2)]
                    zb = [sb(sc, f"zb{i}_{n}", [P, 12 * P]) for i in range(2)]
                    ps_c = ps(sc, f"ps_c_{n}", [P, 512])
                    ps_s = ps(sc, f"ps_s_{n}", [P, 512])
                    ps_v = ps(sc, f"ps_v_{n}", [P, 512])
                    ps_x = ps(sc, f"ps_x_{n}", [P, 1024], BF16)
                    ps_a = ps(sc, f"ps_a_{n}", [P, 512])
                    bc = [ps(sc, f"bc{i}_{n}", [P, 4, P]) for i in range(2)]
                    ps_u = ps(sc, f"ps_u_{n}", [P, 512])
                    (staged, split, split_a, split_b, split_c, split_d, transposed, tcopied, a_done, a_ready,
                     spread, paired, used, y_done) = (sem(f"{a}_{n}") for a in (
                        "staged", "split", "split_a", "split_b", "split_c", "split_d", "transposed", "tcopied", "a_done",
                        "a_ready", "spread", "paired", "used", "y_done"))
                    split_turn = sem(f"split_turn_{n}")
                    with nc.Block() as block:
                        @block.scalar
                        def _(act):
                            def body(t_, slot, turn):
                                wait(act, transposed, t_ - 1)
                                wait(act, split, t_ - 1)
                                nc.scalar.copy(stg[slot][:], one(acc[:, ds(t_, 1), :]))
                                nc.scalar.copy(xst[slot][:], one(x[:, ds(t_, 1), :])).then_inc(staged, 1)
                                act.wait_ge(transposed, t_ + 1)
                                wait(act, used, (t_ - 1) * NI)
                                nc.scalar.copy(cT[slot][:], ps_c[:])
                                nc.scalar.copy(tT[slot][:], ps_s[0:NV, 0:P])
                                nc.scalar.copy(xsT[slot][:], ps_s[0:NS, P:2 * P])
                                nc.scalar.copy(xvT[slot][:], ps_v[0:NV, 0:3 * P])
                                nc.scalar.copy(xpT[slot][:], ps_x[0:96, 0:5 * P].rearrange("k (g p) -> k g p", g=5)).then_inc(tcopied, 1)
                                act.wait_ge(a_done, t_ + 1)
                                nc.scalar.copy(aT[slot][:], ps_a[:].rearrange("p (i q) -> p i q", i=4)).then_inc(a_ready, 1)
                            steps(act, NT, 2, body)

                        @block.gpsimd
                        def _(pool):
                            def body(t_, slot, turn):
                                pool.wait_ge(staged, t_ + 1)
                                wait(pool, transposed, t_ - 1)
                                stand(pool, split_turn)
                                src = xst[slot][:].rearrange("p (g c) -> p g c", g=5)
                                part = xsp[slot]
                                r1 = rest[slot][:, 0, :].rearrange("p (g c) -> p g c", g=5)
                                r2 = rest[slot][:, 1, :].rearrange("p (g c) -> p g c", g=5)
                                nc.gpsimd.tensor_copy(part[:, :, 0, :], src).then_inc(split_a, 1)
                                pool.wait_ge(split_a, t_ + 1)
                                stand(pool, split_turn)
                                nc.gpsimd.tensor_tensor(r1, src, part[:, :, 0, :], ALU.subtract).then_inc(split_b, 1)
                                pool.wait_ge(split_b, t_ + 1)
                                stand(pool, split_turn)
                                nc.gpsimd.tensor_copy(part[:, :, 1, :], r1).then_inc(split_c, 1)
                                pool.wait_ge(split_c, t_ + 1)
                                stand(pool, split_turn)
                                nc.gpsimd.tensor_tensor(r2, r1, part[:, :, 1, :], ALU.subtract).then_inc(split_d, 1)
                                pool.wait_ge(split_d, t_ + 1)
                                stand(pool, split_turn)
                                nc.gpsimd.tensor_copy(part[:, :, 2, :], r2).then_inc(split, 1)
                            steps(pool, NT, 2, body)

                        @block.vector
                        def _(dve):
                            def body(t_, slot, turn):
                                dve.wait_ge(a_ready, t_ + 1)
                                for q, (sel, c0, gp, ai, comps, wu, wc, dst) in enumerate(items):
                                    at = t_ * NI + q
                                    b = q % 2
                                    dve.wait_ge(spread, at + 1)
                                    wait(dve, used, at - 1)
                                    if comps == 1:
                                        z = zb[b][:, 0:4 * P].rearrange("p (c q) -> p c q", c=4)
                                        ins = nc.vector.tensor_tensor(z, bc[b][:], aT[slot][:, ai:ai + 1, :].broadcast_to([P, 4, P]), ALU.mult)
                                    else:
                                        z = zb[b][:].rearrange("p (i c q) -> p i c q", i=3, c=4)
                                        ins = nc.vector.tensor_tensor(z, bc[b][:].unsqueeze(1).broadcast_to([P, 3, 4, P]),
                                                                      aT[slot][:, 1:4, :].unsqueeze(2).broadcast_to([P, 3, 4, P]), ALU.mult)
                                    ins.then_inc(paired, 1)
                                dve.wait_ge(used, (t_ + 1) * NI)
                                row = one(x[:, ds(t_, 1), :])
                                nc.vector.scalar_tensor_tensor(row, row, 2.0, ps_u[:, 0:C], ALU.mult, ALU.add).then_inc(y_done, 1)
                            steps(dve, NT, 2, body)

                        @block.tensor
                        def _(pe):
                            def transposes(t_, slot):
                                pe.wait_ge(staged, t_ + 1)
                                pe.wait_ge(split, t_ + 1)
                                wait(pe, tcopied, t_)
                                for i in range(4):
                                    nc.tensor.transpose(ps_c[:, i * P:(i + 1) * P], stg[slot][:, i * P:(i + 1) * P], ident[:])
                                nc.tensor.transpose(ps_s[0:NV, 0:P], stg[slot][:, A_T:A_W], ident[:])
                                nc.tensor.transpose(ps_s[0:NS, P:2 * P], xst[slot][:, OS:OS + NS], ident[:])
                                for i in range(3):
                                    nc.tensor.transpose(ps_v[0:NV, i * P:(i + 1) * P], xst[slot][:, OV[i]:OV[i] + NV], ident[:])
                                for i in range(5):
                                    last = nc.tensor.transpose(ps_x[0:96, i * P:(i + 1) * P], xsp[slot][:, i, :, :].rearrange("p a c -> p (a c)"), identb[:])
                                last.then_inc(transposed, 1)

                            def sums(t_, slot):
                                pe.wait_ge(tcopied, t_ + 1)
                                wait(pe, a_ready, t_)
                                nc.tensor.matmul(ps_a[:, 0:P], w0[:].rearrange("k r w -> k (r w)"), cT[slot][:, 0:P], start=True, stop=False, skip_group_check=True)
                                nc.tensor.matmul(ps_a[:, 0:P], wt[:].rearrange("k r w -> k (r w)"), tT[slot][:], start=False, stop=False, skip_group_check=True)
                                nc.tensor.matmul(ps_a[:, P:512], w1[:].rearrange("k r w -> k (r w)"), cT[slot][:, P:512], start=False, stop=True, skip_group_check=True).then_inc(a_done, 1)

                            def contract(t_, slot, q):
                                sel, c0, gp, ai, comps, wu, wc, dst = items[q]
                                pe.wait_ge(paired, t_ * NI + q + 1)
                                for i in range(comps):
                                    col, m = dst[i]
                                    for c in range(4):
                                        last = nc.tensor.matmul(ps_u[:, col:col + m], zb[q % 2][:, (4 * i + c) * P:(4 * i + c + 1) * P], wu[:, wc + c, :],
                                                                start=False, stop=(q == NI - 1 and c == 3), skip_group_check=True)
                                last.then_inc(used, 1)
                                return last

                            def body(t_, slot, turn):
                                more = not (isinstance(t_, int) and t_ == NT - 1)
                                for q, (sel, c0, gp, ai, comps, wu, wc, dst) in enumerate(items):
                                    wait(pe, paired, t_ * NI + q - 1)
                                    for c in range(4):
                                        last = nc.tensor.matmul(bc[q % 2][:, c, :], sel[:, c0 + c, :], xpT[slot][:, gp, :], start=(c == 0), stop=(c == 3), skip_group_check=True)
                                    last.then_inc(spread, 1)
                                    if q == 0:
                                        wait(pe, y_done, t_)
                                        nc.tensor.matmul(ps_u[:, OS:OS + NS], xsT[slot][:], lus[:], start=True, stop=False, skip_group_check=True)
                                        for i in range(3):
                                            nc.tensor.matmul(ps_u[:, OV[i]:OV[i] + NV], xvT[slot][:, i * P:(i + 1) * P], luv[:], start=False, stop=False, skip_group_check=True)
                                    else:
                                        contract(t_, slot, q - 1)
                                    if q == T_AT and more:
                                        transposes(t_ + 1, 1 - slot)
                                    if q == B_AT and more:
                                        sums(t_ + 1, 1 - slot)
                                contract(t_, slot, NI - 1)

                            pe.wait_ge(w_scaled, 1)
                            transposes(0, 0)
                            sums(0, 0)
                            steps(pe, NT, 2, body, tail=1)

        def filter_layer(n, f):
            rec = rec_d[0:P * T, :].rearrange("(p t) w -> p t w", t=T)
            one_l = n == 1
            K, KC = f["fc_in"], f["fc_col"]
            NW, NSC = f["nw"], f["nsc"]
            PW = 448 if one_l else 320
            WA, WB = f["wa"], f["wb"]
            layer = ExitStack()
            with layer:
                acc = sb(layer, f"acc_{n}", [P, NT, WA + WB])
                sconn = sb(layer, f"sconn_{n}", [P, NT, NSC + 96])
                ws = sb(layer, f"ws_{n}", [NS, NS + NSC])
                wv = sb(layer, f"wv_{n}", [NV, 2 * NV])
                fc1 = sb(layer, f"fc1_{n}", [K, 64])
                fc2 = sb(layer, f"fc2_{n}", [64, NW])
                NO = f["no"]
                KV = f["kv"]
                wos = sb(layer, f"wos_{n}", [96, NO])
                wov = sb(layer, f"wov_{n}", [KV, NV])
                w_in, w_scaled, h_out, h_written = (sem(f"{a}_{n}") for a in ("weights_in", "weights_scaled", "h_out", "h_written"))

                with ExitStack() as sc:
                    xst = [sb(sc, f"xst{i}_{n}", [P, C]) for i in range(2)]
                    xT = [sb(sc, f"xT{i}_{n}", [NS, 4, P]) for i in range(2)]
                    hst = [sb(sc, f"hst{i}_{n}", [P, C]) for i in range(2)]
                    pT = [ps(sc, f"pT{i}_{n}", [P, 4, P]) for i in range(2)]
                    pP = [ps(sc, f"pP{i}_{n}", [P, 512]) for i in range(2)]
                    staged, transposed, tcopied, mapped, taken = (sem(f"pre_{a}_{n}") for a in ("staged", "transposed", "tcopied", "mapped", "taken"))
                    h_sent = [sem(f"h_sent{i}_{n}") for i in range(2)]
                    turn_begun = sem(f"pre_turn_begun_{n}")
                    with nc.Block() as block:
                        @block.scalar
                        def _(act):
                            nw = 0
                            for dst, src in f["loads"](ws, wv, fc1, fc2, wos, wov):
                                act.dma_start(dst, src).then_inc(w_in, 16)
                                nw += 16
                            act.wait_ge(w_in, nw)
                            for ap, s in f["scale"](ws, wv, fc1, fc2, wos, wov):
                                last = nc.scalar.mul(ap, ap, s)
                            last.then_inc(w_scaled, 1)

                            def body(t_, slot, turn):
                                wait(act, transposed, t_ - 1)
                                nc.scalar.copy(xst[slot][:], one(x[:, ds(t_, 1), :])).then_inc(staged, 1)
                                act.wait_ge(transposed, t_ + 1)
                                wait(act, mapped, t_ - 1)
                                nc.scalar.copy(xT[slot][:, 0, :], pT[slot][0:NS, 0, :])
                                nc.scalar.copy(xT[slot][0:NV, 1:4, :], pT[slot][0:NV, 1:4, :]).then_inc(tcopied, 1)
                            steps(act, NT, 2, body)

                        @block.tensor
                        def _(pe):
                            def transposes(t_, slot):
                                pe.wait_ge(staged, t_ + 1)
                                wait(pe, tcopied, t_ - 1)
                                stand(pe, turn_begun)
                                nc.tensor.transpose(pT[slot][0:NS, 0, :], xst[slot][:, OS:OS + NS], ident[:])
                                for i in range(3):
                                    last = nc.tensor.transpose(pT[slot][0:NV, 1 + i, :], xst[slot][:, OV[i]:OV[i] + NV], ident[:])
                                last.then_inc(transposed, 1)

                            def body(t_, slot, turn):
                                if not (isinstance(t_, int) and t_ == NT - 1):
                                    transposes(t_ + 1, 1 - slot)
                                pe.wait_ge(tcopied, t_ + 1)
                                wait(pe, taken, t_ - 1)
                                nc.tensor.matmul(pP[slot][:, 0:NS + NSC], xT[slot][:, 0, :], ws[:], start=True, stop=False, skip_group_check=True)
                                for i in range(3):
                                    c0 = NS + NSC + 2 * NV * i
                                    last = nc.tensor.matmul(pP[slot][:, c0:c0 + 2 * NV], xT[slot][0:NV, 1 + i, :], wv[:], start=False, stop=(i == 2), skip_group_check=True)
                                last.then_inc(mapped, 1)
                            pe.wait_ge(w_scaled, 1)
                            transposes(0, 0)
                            steps(pe, NT, 2, body, tail=1)

                        @block.vector
                        def _(dve):
                            def body(t_, slot, turn):
                                dve.wait_ge(mapped, t_ + 1)
                                wait(dve, h_sent[slot], turn * 16)
                                a = attr[:, ds(t_, 1)]
                                p, h, s = pP[slot], hst[slot], one(sconn[:, ds(t_, 1), :])
                                vec = p[:, NS + NSC:NS + NSC + 6 * NV].rearrange("p (i c) -> p i c", i=3)
                                nc.vector.tensor_scalar(h[:, 0:NS], p[:, 0:NS], a, None, ALU.mult)
                                nc.vector.tensor_scalar(h[:, NS:C].rearrange("p (i c) -> p i c", i=3), vec[:, :, 0:NV], a, None, ALU.mult)
                                nc.vector.tensor_scalar(s[:, 0:NSC], p[:, NS:NS + NSC], a, None, ALU.mult)
                                nc.vector.tensor_scalar(s[:, NSC:NSC + 96].rearrange("p (i c) -> p i c", i=3), vec[:, :, NV:2 * NV], a, None, ALU.mult).then_inc(taken, 1)
                            steps(dve, NT, 2, body)
                            nc.vector.memset(acc[:], 0.0).then_inc(h_written, 1)

                        @block.sync
                        def _(sp):
                            def body(t_, slot, turn):
                                sp.wait_ge(taken, t_ + 1)
                                sp.dma_start(h_dram[ds(t_ * P, P), :], hst[slot][:]).then_inc(h_sent[slot], 16)
                            steps(sp, NT, 2, body)
                            sp.wait_ge(h_sent[0], 16 * ((NT + 1) // 2))
                            sp.wait_ge(h_sent[1], 16 * (NT // 2))

                with ExitStack() as sc:
                    recb = [sb(sc, f"recb{i}_{n}", [P, TPG, WD]) for i in range(SLOTS)]
                    rowb = [sb(sc, f"rowb{i}_{n}", [P, TPG, C]) for i in range(SLOTS)]
                    oh = [sb(sc, f"oh{i}_{n}", [P, TPG, 4, P]) for i in range(2)]
                    ohp = [sb(sc, f"ohp{i}_{n}", [P, TPG, P], BF16) for i in range(2)]
                    prod = [sb(sc, f"prod{i}_{n}", [P, TPG, PW]) for i in range(2)]
                    eT = sb(sc, f"eT_{n}", [K, TPG * P])
                    hid = sb(sc, f"hid_{n}", [64, TPG * P])
                    onesb = sb(sc, f"onesb_{n}", [P, 1], BF16)
                    psa = [ps(sc, f"psa{i}_{n}", [P, 512]) for i in range(2)]
                    psb = [ps(sc, f"psb{i}_{n}", [P, 512]) for i in range(2)]
                    psw = [ps(sc, f"psw{i}_{n}", [P, 512]) for i in range(2)]
                    psT = ps(sc, f"psT_{n}", [P, 512])
                    psH = ps(sc, f"psH_{n}", [P, 512])
                    rec_in = [sem(f"rec_in{i}_{n}") for i in range(SLOTS)]
                    rows_in = [sem(f"rows_in{i}_{n}") for i in range(SLOTS)]
                    (oh_ready, agg_done, evac_done, gather_turn, e_turned, eT_ready, fc1_done, hid_ready, fc2_done, prod_ready) = (
                        sem(f"{a}_{n}") for a in ("oh_ready", "agg_done", "evac_done", "gather_turn", "e_turned", "eT_ready",
                                                  "fc1_done", "hid_ready", "fc2_done", "prod_ready"))
                    ones_ready, turn_begun = sem(f"ones_ready_{n}"), sem(f"edge_turn_begun_{n}")
                    with nc.Block() as block:
                        @block.sync
                        def _(sp):
                            def body(g, slot, turn):
                                wait(sp, agg_done, g - (SLOTS - 1))
                                sp.dma_start(recb[slot][:, :, KC:WD], rec[:, ds(TPG * g, TPG), KC:WD]).then_inc(rec_in[slot], 16)
                            steps(sp, NG, SLOTS, body)

                        @block.gpsimd
                        def _(pool):
                            def body(g, slot, turn):
                                pool.wait_ge(rec_in[slot], (turn + 1) * 16)
                                wait(pool, prod_ready, g - (SLOTS - 1))
                                stand(pool, gather_turn)
                                for k in range(TPG):
                                    pool.indirect_dma_start(rowb[slot][:, k, :], None, h_dram,
                                                            bass.IndirectOffsetOnAxis(recb[slot][:, k, D_IDX:D_IDX + 1].bitcast(U32), 0)).then_inc(rows_in[slot], 16)
                            steps(pool, NG, SLOTS, body)

                        @block.scalar
                        def _(act):
                            def body(g, slot, turn):
                                act.wait_ge(e_turned, g + 1)
                                wait(act, fc1_done, g)
                                nc.scalar.copy(eT[:], psT[0:K, 0:TPG * P]).then_inc(eT_ready, 1)
                                act.wait_ge(fc1_done, g + 1)
                                wait(act, fc2_done, g)
                                nc.scalar.activation(hid[:], psH[0:64, 0:TPG * P], ACT.Silu, scale=f["silu_scale"]).then_inc(hid_ready, 1)
                            steps(act, NG, SLOTS, body)

                        @block.vector
                        def _(dve):
                            def products(g, slot, turn):
                                dve.wait_ge(rec_in[slot], (turn + 1) * 16)
                                wait(dve, agg_done, g - 1)
                                b = slot % 2
                                for k in range(TPG):
                                    where = recb[slot][:, k, D_LOC:D_LOC + 1]
                                    if not one_l:
                                        nc.vector.tensor_scalar(ohp[b][:, k, :], iota[:], where, None, ALU.is_equal)
                                    for c in range(4):
                                        nc.vector.tensor_scalar(oh[b][:, k, c, :], iota[:], where,
                                                                recb[slot][:, k, D_E4 + c:D_E4 + c + 1], ALU.is_equal, ALU.mult)
                                dve.wait_ge(rows_in[slot], (turn + 1) * (16 * TPG))
                                dve.wait_ge(fc2_done, g + 1)
                                w = psw[b][:, 0:TPG * NW].rearrange("p (k c) -> p k c", k=TPG)
                                row, pr = rowb[slot], prod[b]
                                es = row[:, :, 0:NS].unsqueeze(2).broadcast_to([P, TPG, 2, NS])
                                ev = row[:, :, NS:C].rearrange("p k (i c) -> p k i c", i=3)

                                def mul(dst, x_, wcol, m):
                                    return nc.vector.tensor_tensor(dst, w[:, :, wcol:wcol + NV].unsqueeze(2).broadcast_to([P, TPG, m, NV]), x_, ALU.mult)
                                nc.vector.tensor_tensor(pr[:, :, 0:320].rearrange("p k (a c) -> p k a c", a=2)[:, :, :, 0:NS],
                                                        w[:, :, 0:2 * NS].rearrange("p k (a c) -> p k a c", a=2), es, ALU.mult)
                                last = mul(pr[:, :, NS:C].rearrange("p k (i c) -> p k i c", i=3), ev, 2 * NS, 3)
                                if one_l:
                                    seq = pr[:, :, 224:448].rearrange("p k (b c) -> p k b c", b=7)
                                    mul(seq[:, :, 0:7:3, :], ev, 2 * NS + NV, 3)
                                    mul(seq[:, :, 1:3, :], ev[:, :, 1:3, :], 2 * NS + 2 * NV, 2)
                                    last = mul(seq[:, :, 4:6, :], ev[:, :, 0:2, :], 2 * NS + 2 * NV, 2)
                                else:
                                    last = mul(pr[:, :, 224:320].rearrange("p k (i c) -> p k i c", i=3), ev, 2 * NS + NV, 3)
                                last.then_inc(prod_ready, 1)

                            def body(g, slot, turn):
                                if not (isinstance(g, int) and g == NG - 1):
                                    products(g + 1, (slot + 1) % SLOTS, turn + (slot == SLOTS - 1))
                                tile = dve.value_load(gtile["d"][0:1, ds(g, 1)], min_val=0, max_val=NT - 1)
                                dve.wait_ge(agg_done, g + 1)
                                wait(dve, evac_done, g)
                                a = one(acc[:, ds(tile, 1), :])
                                nc.vector.tensor_tensor(a[:, 0:WA], psa[slot % 2][:, 0:WA], a[:, 0:WA], ALU.add)
                                nc.vector.tensor_tensor(a[:, WA:WA + WB], psb[slot % 2][:, 0:WB], a[:, WA:WA + WB], ALU.add).then_inc(evac_done, 1)

                            nc.vector.memset(onesb[:], 1.0).then_inc(ones_ready, 1)
                            products(0, 0, 0)
                            steps(dve, NG, SLOTS, body, tail=1)

                        @block.tensor
                        def _(pe):
                            def turn_e(g, slot, turn):
                                pe.wait_ge(rec_in[slot], (turn + 1) * 16)
                                wait(pe, eT_ready, g)
                                stand(pe, turn_begun)
                                for k in range(TPG):
                                    last = nc.tensor.transpose(psT[0:K, k * P:(k + 1) * P], recb[slot][:, k, KC:KC + K], ident[:])
                                last.then_inc(e_turned, 1)

                            def first(g):
                                pe.wait_ge(eT_ready, g + 1)
                                wait(pe, hid_ready, g)
                                stand(pe, turn_begun)
                                nc.tensor.matmul(psH[0:64, 0:TPG * P], fc1[:], eT[:], start=True, stop=True).then_inc(fc1_done, 1)

                            def second(g, slot):
                                pe.wait_ge(hid_ready, g + 1)
                                wait(pe, prod_ready, g - 1)
                                for k in range(TPG):
                                    last = nc.tensor.matmul(psw[slot % 2][:, k * NW:(k + 1) * NW], hid[:, k * P:(k + 1) * P], fc2[:],
                                                            start=(k == 0), stop=(k == TPG - 1), skip_group_check=True)
                                last.then_inc(fc2_done, 1)

                            def sums(slot, k):
                                b = slot % 2
                                o, pr, pa, pb = oh[b][:, k], prod[b][:, k, :], psa[b], psb[b]
                                st, en = k == 0, k == TPG - 1

                                def mm(dst, coef, cols, start=False, stop=False):
                                    return nc.tensor.matmul(dst, o[:, coef, :], cols, start=start, stop=stop, skip_group_check=True)
                                mm(pa[:, 0:C], 0, pr[:, 0:C], st, False)
                                if one_l:
                                    mm(pa[:, C:2 * C], 1, pr[:, C:2 * C], False, en)
                                    mm(pb[:, 0:NS], 2, pr[:, C:C + NS], st, False)
                                    mm(pb[:, NS:C], 2, pr[:, 288:384], False, False)
                                    mm(pb[:, C:C + NS], 3, pr[:, C:C + NS], False, False)
                                    return mm(pb[:, C + NS:2 * C], 3, pr[:, 352:448], False, en)
                                for i in range(3):
                                    mm(pa[:, C:C + NV], 1 + i, pr[:, 224 + NV * i:256 + NV * i], False, False)
                                    mm(pb[:, NS * i:NS * i + NS], 1 + i, pr[:, C:C + NS], st and i == 0, en and i == 2)
                                return nc.tensor.matmul(pa[:, C + NV:C + NV + 1], ohp[b][:, k, :], onesb[:], start=False, stop=en, skip_group_check=True)

                            def body(g, slot, turn):
                                ahead = not isinstance(g, int) or g + 2 < NG
                                s2, t2 = (slot + 2) % SLOTS, turn + (slot + 2) // SLOTS
                                if ahead:
                                    turn_e(g + 2, s2, t2)
                                pe.wait_ge(prod_ready, g + 1)
                                wait(pe, evac_done, g - 1)
                                sums(slot, 0)
                                if ahead:
                                    first(g + 2)
                                sums(slot, 1).then_inc(agg_done, 1)
                                if ahead:
                                    second(g + 2, s2)
                            pe.wait_ge(ones_ready, 1)
                            for g in range(2):
                                turn_e(g, g, 0)
                                first(g)
                                second(g, g)
                            steps(pe, NG, SLOTS, body, tail=2)

                with ExitStack() as sc:
                    sg = [sb(sc, f"sg{i}_{n}", [P, 96 + 3 * KV]) for i in range(2)]
                    tmp = [sb(sc, f"tmp{i}_{n}", [P, NV]) for i in range(2)]
                    sT = [sb(sc, f"sT{i}_{n}", [P, 4, P]) for i in range(2)]
                    pT = [ps(sc, f"qT{i}_{n}", [P, 4, P]) for i in range(2)]
                    pO = [ps(sc, f"pO{i}_{n}", [P, 512]) for i in range(2)]
                    factor = sb(sc, f"factor_{n}", [P, 3, NT])
                    gates = sb(sc, f"gates_{n}", [P, NT, 96]) if one_l else None
                    staged, t_summed, transposed, tcopied, mapped, taken, f_step, acted, gated, y_step = (
                        sem(f"post_{a}_{n}") for a in ("staged", "t_summed", "transposed", "tcopied", "mapped", "taken", "f_step", "acted", "gated", "y_step"))
                    with nc.Block() as block:
                        @block.vector
                        def _(dve):
                            def stage(t_, slot):
                                a = one(acc[:, ds(t_, 1), :])
                                wait(dve, transposed, t_ - 1)
                                s_ = sg[slot]
                                vec = s_[:, 96:96 + 3 * KV].rearrange("p (i c) -> p i c", i=3)
                                nc.vector.tensor_copy(s_[:, 0:NS], a[:, 0:NS])
                                nc.vector.tensor_copy(vec[:, :, NS:NS + NV], a[:, NS:C].rearrange("p (i c) -> p i c", i=3))
                                if one_l:
                                    per = a[:, C:4 * C].rearrange("p (k c) -> p k c", k=3)
                                    nc.vector.tensor_copy(vec[:, :, 0:NS], per[:, :, 0:NS])

                                    def blk(k, j):
                                        return per[:, k, NS + NV * j:NS + NV * (j + 1)]
                                    nc.vector.tensor_tensor(tmp[slot][:], blk(0, 0), blk(1, 1), ALU.add).then_inc(t_summed, 1)
                                    nc.vector.tensor_tensor(vec[:, 0, 96:128], blk(2, 1), blk(1, 0), ALU.subtract)
                                    nc.vector.tensor_tensor(vec[:, 1, 96:128], blk(0, 2), blk(2, 0), ALU.subtract)
                                    nc.vector.tensor_tensor(vec[:, 2, 96:128], blk(1, 2), blk(0, 1), ALU.subtract)
                                    dve.wait_ge(t_summed, t_ + 1)
                                    nc.vector.tensor_tensor(s_[:, NS:96], tmp[slot][:], blk(2, 2), ALU.add).then_inc(staged, 1)
                                else:
                                    nc.vector.tensor_copy(vec[:, :, 0:NS], a[:, WA:WA + WB].rearrange("p (i c) -> p i c", i=3))
                                    nc.vector.tensor_copy(s_[:, NS:96], a[:, C:C + NV]).then_inc(staged, 1)

                            def body(t_, slot, turn):
                                if not (isinstance(t_, int) and t_ == NT - 1):
                                    stage(t_ + 1, 1 - slot)
                                dve.wait_ge(mapped, t_ + 1)
                                s_ = one(sconn[:, ds(t_, 1), :])
                                if one_l:
                                    nc.vector.scalar_tensor_tensor(s_, pO[slot][:, 0:192], attr[:, ds(t_, 1)], s_, ALU.mult, ALU.add).then_inc(taken, 1)
                                else:
                                    coef = factor[:, 1, ds(t_, 1)]
                                    nc.vector.tensor_scalar(factor[:, 2, ds(t_, 1)], pO[slot][:, 0:1], coef, coef, ALU.mult, ALU.mult).then_inc(acted, 1)
                                    dve.wait_ge(acted, t_ + 1)
                                    nc.vector.scalar_tensor_tensor(s_, pO[slot][:, 1:161], factor[:, 2, ds(t_, 1)], s_, ALU.mult, ALU.add).then_inc(taken, 1)

                            if not one_l:
                                nc.vector.tensor_scalar(factor[:, 0, :].unsqueeze(2), acc[:, :, C + NV:C + NV + 1], 1.0, None, ALU.max).then_inc(f_step, 1)
                                dve.wait_ge(f_step, 1)
                                nc.vector.reciprocal(factor[:, 0, :], factor[:, 0, :]).then_inc(f_step, 1)
                                dve.wait_ge(f_step, 2)
                                nc.vector.tensor_tensor(factor[:, 1, :], factor[:, 0, :], attr[:], ALU.mult).then_inc(f_step, 1)
                                dve.wait_ge(f_step, 3)
                            stage(0, 0)
                            steps(dve, NT, 2, body, tail=1)
                            dve.wait_ge(taken, NT)
                            if one_l:
                                dve.wait_ge(gated, 1)
                                g_ = gates[:, :, NS:96].unsqueeze(2).broadcast_to([P, NT, 3, NV])
                                v_ = sconn[:, :, 96:192].rearrange("p t (i c) -> p t i c", i=3)
                                nc.vector.tensor_tensor(v_, g_, v_, ALU.mult).then_inc(y_step, 1)
                                dve.wait_ge(y_step, 1)
                                scal, v0 = gates[:, :, 0:NS], 96
                            else:
                                scal, v0 = sconn[:, :, 0:NS], NS
                            nc.vector.tensor_tensor(x[:, :, OS:OS + NS], x[:, :, OS:OS + NS], scal, ALU.add)
                            for i in range(3):
                                o = x[:, :, OV[i]:OV[i] + NV]
                                nc.vector.tensor_tensor(o, o, sconn[:, :, v0 + NV * i:v0 + NV * (i + 1)], ALU.add)

                        @block.tensor
                        def _(pe):
                            def transposes(t_, slot):
                                pe.wait_ge(staged, t_ + 1)
                                wait(pe, tcopied, t_ - 1)
                                nc.tensor.transpose(pT[slot][0:96, 0, :], sg[slot][:, 0:96], ident[:])
                                for i in range(3):
                                    last = nc.tensor.transpose(pT[slot][0:KV, 1 + i, :], sg[slot][:, 96 + KV * i:96 + KV * (i + 1)], ident[:])
                                last.then_inc(transposed, 1)

                            def body(t_, slot, turn):
                                if not (isinstance(t_, int) and t_ == NT - 1):
                                    transposes(t_ + 1, 1 - slot)
                                pe.wait_ge(tcopied, t_ + 1)
                                wait(pe, taken, t_ - 1)
                                nc.tensor.matmul(pO[slot][:, 0:NO], sT[slot][0:96, 0, :], wos[:], start=True, stop=False, skip_group_check=True)
                                for i in range(3):
                                    last = nc.tensor.matmul(pO[slot][:, NO + NV * i:NO + NV * (i + 1)], sT[slot][0:KV, 1 + i, :], wov[:], start=False, stop=(i == 2), skip_group_check=True)
                                last.then_inc(mapped, 1)
                            transposes(0, 0)
                            steps(pe, NT, 2, body, tail=1)

                        @block.scalar
                        def _(act):
                            def body(t_, slot, turn):
                                act.wait_ge(transposed, t_ + 1)
                                wait(act, mapped, t_ - 1)
                                nc.scalar.copy(sT[slot][0:96, 0, :], pT[slot][0:96, 0, :])
                                nc.scalar.copy(sT[slot][0:KV, 1:4, :], pT[slot][0:KV, 1:4, :]).then_inc(tcopied, 1)
                            steps(act, NT, 2, body)
                            if one_l:
                                act.wait_ge(taken, NT)
                                nc.scalar.activation(gates[:, :, 0:NS], sconn[:, :, 0:NS], ACT.Silu)
                                nc.scalar.activation(gates[:, :, NS:96], sconn[:, :, NS:96], ACT.Sigmoid).then_inc(gated, 1)

        inv = lambda d: float(1.0 / np.sqrt(np.float64(d)))
        r3, r32 = inv(3), inv(NV)
        p0, p3 = "L0_gnn_", "L3_gnn_"
        flat = lambda ap: ap.rearrange("u o w -> (u o) w")
        product_layer(
            0, t["x"],
            {"lm_s": t[p0 + "Lm_s"], "wm_ss": t[p0 + "Wm_ss"], "wm_vv": t[p0 + "Wm_vv"], "wm_sv": t[p0 + "Wm_sv"], "lm_v": t[p0 + "Lm_v"],
             "wm_vs": t[p0 + "Wm_vs"], "lu_s": t[p0 + "Lu_s"], "lu_v": t[p0 + "Lu_v"], "wu_ss": t[p0 + "Wu_ss"], "wu_vv": t[p0 + "Wu_vv"],
             "wu_sv": t[p0 + "Wu_sv"], "wu_vs": t[p0 + "Wu_vs"], "dist": 3, "r": (0, 1, 2)},
            {"lm_s": 1 / 8, "wm_ss": 1 / 8, "wm_vv": r3 * r32, "wm_sv": 1 / 8, "lm_v": r32, "wm_vs": r32, "lu_s": 1 / 8, "lu_v": r32,
             "wu_ss": 1 / 64, "wu_vv": r3 / 32, "wu_sv": inv(2048), "wu_vs": inv(2048)})
        end_stage()
        layernorm(0)

        p1 = "L1_gnn_"
        filter_layer(1, {
            "fc_in": 64, "fc_col": D_E64, "nw": 224, "nsc": 96, "wa": 320, "wb": 320, "no": 96, "kv": 128, "silu_scale": 1 / 8,
            "loads": lambda ws, wv, fc1, fc2, wos, wov: (
                (ws[:, 0:NS], t[p1 + "lin1_ws"]), (ws[:, NS:NS + 96], t[p1 + "sc_ws"]), (wv[:, 0:NV], t[p1 + "lin1_wv"]),
                (wv[:, NV:2 * NV], t[p1 + "sc_wv"]), (fc1[:], t[p1 + "fc_w1"]), (fc2[:], t[p1 + "fc_w2"]),
                (wos[:], t[p1 + "lin2_ws"]), (wov[:], t[p1 + "lin2_wv"])),
            "scale": lambda ws, wv, fc1, fc2, wos, wov: (
                (ws[:], 1 / 8), (wv[:], r32), (fc2[:], 1 / 8), (wos[0:NS, :], inv(96) / 4), (wos[NS:96, :], inv(96) / 4 * r3),
                (wov[0:96, :], inv(128) / 4), (wov[96:128, :], inv(128) / 4 * inv(2)))})
        end_stage()
        layernorm(1)

        p2 = "L2_gnn_"
        filter_layer(2, {
            "fc_in": 16, "fc_col": D_E16, "nw": 192, "nsc": 64, "wa": 193, "wb": 192, "no": 65, "kv": 96, "silu_scale": 1 / 4,
            "loads": lambda ws, wv, fc1, fc2, wos, wov: (
                (ws[:, 0:NS], t[p2 + "Wl1_0"]), (ws[:, NS:2 * NS], t[p2 + "Wsc0"]), (wv[:, 0:NV], t[p2 + "Wl1_1"]),
                (wv[:, NV:2 * NV], t[p2 + "Wsc1"]), (fc1[:], t[p2 + "Wfc1"]), (fc2[:], t[p2 + "Wfc2"]),
                (wos[:, 0:1], t[p2 + "Wa"]), (wos[:, 1:65], t[p2 + "Wl2_s"]), (wov[:], t[p2 + "Wl2_v"])),
            "scale": lambda ws, wv, fc1, fc2, wos, wov: (
                (ws[:], 1 / 8), (wv[:], r32), (fc2[:], 1 / 8), (wos[0:NS, :], inv(96)), (wos[NS:96, :], inv(96) * r3),
                (wov[:], inv(96)))})
        end_stage()
        layernorm(2)

        product_layer(
            3, h_dram,
            {"lm_s": t[p3 + "lm0"], "wm_ss": flat(t[p3 + "wm000"]), "wm_vv": flat(t[p3 + "wm110"]), "wm_sv": flat(t[p3 + "wm011"]),
             "lm_v": t[p3 + "lm1"], "wm_vs": flat(t[p3 + "wm101"]), "lu_s": t[p3 + "lu0"], "lu_v": t[p3 + "lu1"], "wu_ss": t[p3 + "wu000"],
             "wu_vv": t[p3 + "wu110"], "wu_sv": t[p3 + "wu011"], "wu_vs": t[p3 + "wu101"], "dist": 3, "r": (0, 1, 2)},
            {"lm_s": 1 / 8, "wm_ss": inv(96), "wm_vv": r3 * inv(96), "wm_sv": inv(96), "lm_v": r32, "wm_vs": inv(96), "lu_s": 1 / 8,
             "lu_v": r32, "wu_ss": inv(5120), "wu_vv": r3 * inv(5120), "wu_sv": 1 / 64, "wu_vs": 1 / 64})
        end_stage()
        layernorm(3, to_output=True)


_INS = ["x", "src", "dst", "edge_attr_16", "edge_attr_4", "edge_attr_64", "node_vec1"]
_INS += ["L0_gnn_" + a for a in ("Wm_ss", "Wm_vv", "Wm_sv", "Wm_vs", "Lm_s", "Lm_v", "Wu_ss", "Wu_vv", "Wu_sv", "Wu_vs", "Lu_s", "Lu_v")]
_INS += ["L1_gnn_" + a for a in ("lin1_ws", "lin1_wv", "fc_w1", "fc_w2", "sc_ws", "sc_wv", "lin2_ws", "lin2_wv")]
_INS += ["L2_gnn_" + a for a in ("Wfc1", "Wfc2", "Wsc0", "Wsc1", "Wl1_0", "Wl1_1", "Wl2_s", "Wl2_v", "Wa")]
_INS += ["L3_gnn_" + a for a in ("wm000", "wm011", "wm101", "wm110", "lm0", "lm1", "wu000", "wu011", "wu101", "wu110", "lu0", "lu1")]


def kernel(**inputs):
    import concourse.bacc as bacc
    from concourse import mybir
    from concourse.bass_utils import run_bass_kernel_spmd

    nc = bacc.Bacc("TRN2", target_bir_lowering=False, num_devices=1)
    arrays, tensors = {}, {}
    cols = permutation()
    for name in _INS:
        a = np.asarray(inputs[name])
        if name == "x":
            a = a[:, cols]
        a = np.ascontiguousarray(a)
        arrays[f"in_{name}"] = a
        tensors[name] = nc.dram_tensor(f"in_{name}", a.shape, mybir.dt.from_np(a.dtype), kind="ExternalInput").ap()
    out = nc.dram_tensor("out_rows", (N, C), mybir.dt.float32, kind="ExternalOutput").ap()
    build(nc, tensors, out)
    got = run_bass_kernel_spmd(nc, [arrays], core_ids=[0]).results[0]["out_rows"]
    back = np.empty_like(cols)
    back[cols] = np.arange(C)
    return got[:, back]
```

```python
import numpy as np

N, E, C = 3125, 50000, 160
P = 128
NS, NV = 64, 32
NT = -(-N // P)
NFULL = N // P
NREST = N - NFULL * P
GROUP = 256
TPG = GROUP // P
NG = (E + NT * (GROUP - 1)) // GROUP
T = NG * TPG
EJ = -(-E // P)
EDUP = P * EJ - E
WS, WD = 6, 86
D_E64, D_E16, D_E4, D_IDX, D_LOC = 0, 64, 80, 84, 85
S_E4, S_IDX, S_LOC = 0, 4, 5
OS = 0
OV = [NS + NV * i for i in range(3)]
BLK = 448
NB = -(-N // BLK)
SLOTS = 4


def permutation():
    cols = list(range(NS)) + [NS + 3 * c + i for i in range(3) for c in range(NV)]
    return np.array(cols)


def build(nc, t, out):
    import concourse.bass as bass
    from concourse import mybir
    from contextlib import ExitStack

    F32, BF16, I32, U32 = mybir.dt.float32, mybir.dt.bfloat16, mybir.dt.int32, mybir.dt.uint32
    ALU = mybir.AluOpType
    ACT = mybir.ActivationFunctionType
    ds = bass.ds

    top = ExitStack()

    def sb(scope, name, shape, dt=F32):
        return scope.enter_context(nc.sbuf_tensor(name, shape, dt))

    def ps(scope, name, shape, dt=F32):
        return scope.enter_context(nc.psum_tensor(name, shape, dt))

    def wait(eng, sem, value):
        if not (isinstance(value, int) and value <= 0):
            eng.wait_ge(sem, value)

    def steps(eng, count, unroll, body, tail=0):
        for i in range(unroll):
            body(i, i, 0)
        turns = (count - tail) // unroll
        with eng.Fori(1, turns) as it:
            for k in range(unroll):
                body(it * unroll + k, k, it)
        for i in range(turns * unroll, count):
            body(i, i % unroll, i // unroll)

    rec_s = nc.dram_tensor("rec_s", (P * T + EJ, WS), F32, kind="Internal").ap()
    rec_d = nc.dram_tensor("rec_d", (P * T + EJ, WD), F32, kind="Internal").ap()
    h_dram = nc.dram_tensor("h_rows", (NT * P, C), F32, kind="Internal").ap()

    with top:
        in_use = []

        def sem(name):
            in_use.append(nc.alloc_semaphore(name))
            return in_use[-1]

        def stand(eng, sem_):
            eng.sem_inc(sem_, 1)

        def end_stage(keep=()):
            nc.clear_and_free_semaphores([a for a in in_use if a not in keep])
            in_use.clear()
            nc.all_engine_barrier()

        x = sb(top, "x", [P, NT, C])
        attr = sb(top, "attr", [P, NT])
        iota = sb(top, "iota", [P, P])
        ident = sb(top, "ident", [P, P])
        identb = sb(top, "identb", [P, P], BF16)
        sel2 = sb(top, "sel2", [96, 16, P], BF16)
        sel4 = sb(top, "sel4", [96, 8, P], BF16)
        gtile = {"s": sb(top, "gtile_s", [1, NG], I32), "d": sb(top, "gtile_d", [1, NG], I32)}
        loc = {"d": sb(top, "loc_d", [P, EJ])}
        pos = {"d": sb(top, "pos_d", [P, EJ], I32)}
        key_i = {"s": sb(top, "key_s", [P, EJ], I32)}
        nidx = sb(top, "nidx", [P, 1])
        k31 = sb(top, "k31", [P, 1])
        pidx_i = sb(top, "pidx_i", [P, 2], I32)
        eye2 = sb(top, "eye2", [P, NS])
        early = ExitStack()
        loc["s"] = sb(early, "loc_s", [P, EJ])
        pos["s"] = sb(early, "pos_s", [P, EJ], I32)
        key_i["d"] = sb(early, "key_d", [P, EJ], I32)
        bval = sb(early, "bval", [P, NT + 1])
        tri = sb(early, "tri", [P, P])
        ones_sq = sb(early, "ones_sq", [P, P])

        def order_parts(k, sc):
            n = f"_{k}"
            key2 = sb(sc, "key2" + n, [P, EJ], I32)
            part_i = sb(sc, "part_i" + n, [P, EJ], I32)
            kt = sb(sc, "kt" + n, [P, EJ])
            ones = sb(sc, "ones" + n, [P, EJ])
            mask = sb(sc, "mask" + n, [P, EJ])
            cum = sb(sc, "cum" + n, [P, EJ])
            prod = sb(sc, "prod" + n, [P, EJ])
            q = sb(sc, "q" + n, [P, EJ])
            counts = sb(sc, "counts" + n, [P, NT])
            small = sb(sc, "small" + n, [P, 8, NT])
            small_i = sb(sc, "small_i" + n, [P, 2, NT], I32)
            ramp_g = sb(sc, "ramp_g" + n, [P, EJ], I32)
            ramp_f = sb(sc, "ramp_f" + n, [P, EJ])
            gt = sb(sc, "gt" + n, [1, NG])
            before = ps(sc, "before" + n, [P, NT])
            total = ps(sc, "total" + n, [P, NT])
            keys_marked = sem("keys_marked" + n)
            ramp_ready = sem("ramp_ready" + n)
            counted = sem("counted" + n)
            summed = sem("summed" + n)
            step = sem("order_step" + n)
            b_mask, b_cum, b_prod, b_q = (sem(f"{a}{n}") for a in ("b_mask", "b_cum", "b_prod", "b_q"))
            def on_gpsimd(pool):
                pool.wait_ge(keys_in, 64)
                nc.gpsimd.affine_select(out=key2[:], in_=key_i[k][:], compare_op=ALU.is_ge, fill=float(NT * P),
                                        base=(P - 1) * 1000 - EDUP, pattern=[[1, EJ]], channel_multiplier=-1000).then_inc(keys_marked, 1)
                nc.gpsimd.iota(ramp_g[:], [[1, EJ]], base=0, channel_multiplier=0).then_inc(ramp_ready, 1)

            def on_tensor(pe):
                pe.wait_ge(counted, NT)
                nc.tensor.matmul(before[:], tri[:], counts[:], start=True, stop=True).then_inc(summed, 1)
                nc.tensor.matmul(total[:], ones_sq[:], counts[:], start=True, stop=True).then_inc(summed, 1)

            def on_vector(dve):
                done = [0]

                def link(ins):
                    done[0] += 1
                    ins.then_inc(step, 1)
                    dve.wait_ge(step, done[0])

                dve.wait_ge(keys_marked, 1)
                link(nc.vector.tensor_scalar(part_i[:], key2[:], 7, None, ALU.arith_shift_right))
                link(nc.vector.tensor_copy(kt[:], part_i[:]))
                link(nc.vector.tensor_scalar(part_i[:], key2[:], P - 1, None, ALU.bitwise_and))
                link(nc.vector.tensor_copy(loc[k][:], part_i[:]))
                link(nc.vector.memset(ones[:], 1.0))
                link(nc.vector.memset(q[:], 0.0))
                for b in range(NT):
                    nc.vector.tensor_scalar(mask[:], kt[:], float(b), None, ALU.is_equal, ALU.add,
                                            accum_out=counts[:, b:b + 1]).then_inc(counted, 1)
                    dve.wait_ge(counted, b + 1)
                dve.wait_ge(summed, 2)
                tot, grp, end, base, off = (small[:, i, :] for i in range(5))
                link(nc.vector.tensor_scalar(tot, total[:], float(GROUP - 1), None, ALU.add))
                link(nc.vector.tensor_copy(small_i[:, 0, :], tot))
                link(nc.vector.tensor_scalar(small_i[:, 1, :], small_i[:, 0, :], GROUP.bit_length() - 1, None, ALU.arith_shift_right))
                link(nc.vector.tensor_copy(grp, small_i[:, 1, :]))
                link(nc.vector.tensor_tensor_scan(end, ones[:, 0:NT], grp, 0.0, ALU.mult, ALU.add))
                link(nc.vector.tensor_tensor(base, end, grp, ALU.subtract))
                link(nc.vector.tensor_scalar(base, base, float(GROUP), -1.0, ALU.mult, ALU.add))
                link(nc.vector.tensor_tensor(off, before[:], base, ALU.add))
                with dve.Fori(0, NT) as b:
                    nc.vector.tensor_scalar(mask[:], kt[:], bval[:, ds(b, 1)], None, ALU.is_equal).then_inc(b_mask, 1)
                    dve.wait_ge(b_mask, b + 1)
                    nc.vector.tensor_tensor_scan(cum[:], ones[:], mask[:], small[:, 4, ds(b, 1)], ALU.mult, ALU.add).then_inc(b_cum, 1)
                    dve.wait_ge(b_cum, b + 1)
                    nc.vector.tensor_tensor(prod[:], mask[:], cum[:], ALU.mult).then_inc(b_prod, 1)
                    dve.wait_ge(b_prod, b + 1)
                    nc.vector.tensor_tensor(q[:], q[:], prod[:], ALU.add).then_inc(b_q, 1)
                    dve.wait_ge(b_q, b + 1)
                dve.wait_ge(ramp_ready, 1)
                link(nc.vector.tensor_copy(pos[k][:], q[:]))
                link(nc.vector.tensor_scalar(part_i[:], pos[k][:], P - 1, None, ALU.bitwise_and))
                link(nc.vector.tensor_copy(mask[:], part_i[:]))
                link(nc.vector.tensor_scalar(part_i[:], pos[k][:], 7, None, ALU.arith_shift_right))
                link(nc.vector.tensor_copy(cum[:], part_i[:]))
                link(nc.vector.scalar_tensor_tensor(q[:], mask[:], float(T), cum[:], ALU.mult, ALU.add))
                link(nc.vector.tensor_copy(ramp_f[:], ramp_g[:]))
                link(nc.vector.tensor_scalar(mask[:], kt[:], float(NT), None, ALU.is_equal))
                link(nc.vector.scalar_tensor_tensor(prod[:], ramp_f[:], float(P * T), mask[:], ALU.add, ALU.mult))
                link(nc.vector.tensor_tensor(q[:], q[:], prod[:], ALU.add))
                link(nc.vector.tensor_copy(pos[k][:], q[:]))
                link(nc.vector.memset(gt[:], 0.0))
                for b in range(NT - 1):
                    link(nc.vector.scalar_tensor_tensor(gt[:], ramp_f[0:1, 0:NG], end[0:1, b:b + 1], gt[:], ALU.is_ge, ALU.add))
                link(nc.vector.tensor_copy(gtile[k][:], gt[:]))
            return on_gpsimd, on_tensor, on_vector

        def scatter_parts(k, sc):
            rec, words = (rec_s, WS) if k == "s" else (rec_d, WD)
            c_idx, c_loc, c_e4 = (S_IDX, S_LOC, S_E4) if k == "s" else (D_IDX, D_LOC, D_E4)
            other = key_i["d" if k == "s" else "s"]
            halves = (12, 11)
            per = sum(halves)
            turns = EJ // per
            pieces = [("edge_attr_4", c_e4, 4)]
            if k == "d":
                pieces += [("edge_attr_64", D_E64, 64), ("edge_attr_16", D_E16, 16)]
            stage = [sb(sc, f"stage{h}_{k}", [P, halves[h], words]) for h in range(2)]
            place = [sb(sc, f"place{h}_{k}", [P, halves[h]], I32) for h in range(2)]
            loaded = [sem(f"loaded{h}_{k}") for h in range(2)]
            filled = [sem(f"filled{h}_{k}") for h in range(2)]
            sent = [sem(f"sent{h}_{k}") for h in range(2)]
            issued, turn_begun = sem(f"scatter_turn_{k}"), sem(f"turn_begun_{k}")
            def on_sync(sp):
                def turn(i, h):
                    wait(sp, sent[h], i * (16 * halves[h]))
                    j0 = i * per + (halves[0] if h else 0)
                    for name, col, w in pieces:
                        src = t[name]
                        body = src[0:(P - 1) * EJ, :].rearrange("(p j) w -> p j w", j=EJ)
                        last = src[E - EJ:E, :].rearrange("(p j) w -> p j w", j=EJ)
                        sp.dma_start(stage[h][0:P - 1, :, col:col + w], body[:, ds(j0, halves[h]), :]).then_inc(loaded[h], 16)
                        sp.dma_start(stage[h][P - 1:P, :, col:col + w], last[:, ds(j0, halves[h]), :]).then_inc(loaded[h], 16)
                for h in range(2):
                    turn(0, h)
                with sp.Fori(1, turns) as i:
                    for h in range(2):
                        turn(i, h)

            def on_gpsimd(pool):
                def turn(i, h):
                    m = halves[h]
                    j0 = i * per + (halves[0] if h else 0)
                    pool.wait_ge(loaded[h], (i + 1) * (32 * len(pieces)))
                    wait(pool, sent[h], i * (16 * m))
                    stand(pool, turn_begun)
                    nc.gpsimd.tensor_copy(stage[h][:, :, c_idx:c_idx + 1].bitcast(I32).rearrange("p m o -> p (m o)"), other[:, ds(j0, m)]).then_inc(filled[h], 1)
                    nc.gpsimd.tensor_copy(stage[h][:, :, c_loc:c_loc + 1].rearrange("p m o -> p (m o)"), loc[k][:, ds(j0, m)]).then_inc(filled[h], 1)
                    nc.gpsimd.tensor_copy(place[h][:], pos[k][:, ds(j0, m)]).then_inc(filled[h], 1)
                    pool.wait_ge(filled[h], (i + 1) * 3)
                    stand(pool, issued)
                    for c in range(m):
                        pool.indirect_dma_start(rec, bass.IndirectOffsetOnAxis(place[h][:, c:c + 1].bitcast(U32), 0),
                                                stage[h][:, c, :], None).then_inc(sent[h], 16)
                for h in range(2):
                    turn(0, h)
                with pool.Fori(1, turns) as i:
                    for h in range(2):
                        turn(i, h)
                for h in range(2):
                    pool.wait_ge(sent[h], 16 * halves[h] * turns)
            return on_sync, on_gpsimd

        keys_in = sem("keys_in")
        with ExitStack() as sc:
            ramp_i = sb(sc, "ramp_i", [P, P], I32)
            sel2_i = sb(sc, "sel2_i", [96, 16 * P], I32)
            sel4_i = sb(sc, "sel4_i", [96, 8 * P], I32)
            empty_s = sb(sc, "empty_s", [P, T, WS])
            EMPTY = 22
            empty_d = sb(sc, "empty_d", [P, EMPTY, WD])
            const_ints = sem("const_ints")
            empties = sem("empties")
            empty_zero = sem("empty_zero")
            loads = sem("loads")
            cleared = sem("cleared")
            written = sem("empty_written")
            dve_step = sem("const_step")
            order_pool, order_pe, order_dve = order_parts("s", sc)
            with nc.Block() as block:
                @block.gpsimd
                def _(pool):
                    nc.gpsimd.iota(ramp_i[:], [[1, P]], base=0, channel_multiplier=0).then_inc(const_ints, 1)
                    nc.gpsimd.iota(pidx_i[:, 0:1], [[1, 1]], base=0, channel_multiplier=1).then_inc(const_ints, 1)
                    nc.gpsimd.iota(sel2_i[:], [[2, 16], [1, 2], [0, 64]], base=0, channel_multiplier=0).then_inc(const_ints, 1)
                    nc.gpsimd.iota(sel4_i[:], [[4, 8], [1, 4], [0, 32]], base=0, channel_multiplier=0).then_inc(const_ints, 1)
                    nc.gpsimd.memset(empty_s[:], 0.0).then_inc(empty_zero, 1)
                    nc.gpsimd.memset(empty_d[:], 0.0).then_inc(empty_zero, 1)
                    pool.wait_ge(empty_zero, 2)
                    nc.gpsimd.memset(empty_s[:, :, S_LOC:S_LOC + 1], -1.0).then_inc(empties, 1)
                    nc.gpsimd.memset(empty_d[:, :, D_LOC:D_LOC + 1], -1.0).then_inc(empties, 1)
                    order_pool(pool)

                @block.tensor
                def _(pe):
                    order_pe(pe)

                @block.sync
                def _(sp):
                    n = 0
                    for k in "sd":
                        src = t["src" if k == "s" else "dst"]
                        sp.dma_start(key_i[k][0:P - 1, :], src[0:(P - 1) * EJ].rearrange("(p j) -> p j", j=EJ)).then_inc(keys_in, 16)
                        sp.dma_start(key_i[k][P - 1:P, :], src[E - EJ:E].rearrange("(p j) -> p j", j=EJ)).then_inc(keys_in, 16)
                    sp.wait_ge(cleared, 2)
                    sp.dma_start(x[:, 0:NFULL, :], t["x"][0:NFULL * P, :].rearrange("(t p) c -> p t c", p=P)).then_inc(loads, 16)
                    sp.dma_start(x[0:NREST, NFULL, :], t["x"][NFULL * P:N, :]).then_inc(loads, 16)
                    with nc.allow_non_contiguous_dma(reason="one word a node"):
                        sp.dma_start(attr[:, 0:NFULL], t["node_vec1"][0:NFULL * P, :].rearrange("(t p) o -> p (t o)", p=P)).then_inc(loads, 16)
                    sp.dma_start(attr[0:NREST, NFULL:NT], t["node_vec1"][NFULL * P:N, :]).then_inc(loads, 16)
                    n += 64
                    sp.wait_ge(empties, 2)
                    sp.dma_start(rec_s[0:P * T, :].rearrange("(p t) w -> p (t w)", t=T), empty_s[:].rearrange("p t w -> p (t w)")).then_inc(written, 16)
                    for i in range(T // EMPTY):
                        sp.dma_start(rec_d[0:P * T, :].rearrange("(p t) w -> p t w", t=T)[:, i * EMPTY:(i + 1) * EMPTY, :],
                                     empty_d[:]).then_inc(written, 16)
                    sp.wait_ge(written, 16 * (1 + T // EMPTY))
                    sp.wait_ge(loads, n)

                @block.vector
                def _(dve):
                    done = [0]

                    def link(ins):
                        done[0] += 1
                        ins.then_inc(dve_step, 1)
                        dve.wait_ge(dve_step, done[0])

                    nc.vector.memset(x[:, NFULL, :], 0.0).then_inc(cleared, 1)
                    nc.vector.memset(attr[:, NFULL:NT], 0.0).then_inc(cleared, 1)
                    link(nc.vector.memset(ones_sq[:], 1.0))
                    dve.wait_ge(const_ints, 4)
                    link(nc.vector.tensor_copy(iota[:], ramp_i[:]))
                    link(nc.vector.tensor_copy(bval[:], iota[:, 0:NT + 1]))
                    link(nc.vector.tensor_copy(nidx[:], pidx_i[:, 0:1]))
                    link(nc.vector.tensor_scalar(pidx_i[:, 1:2], pidx_i[:, 0:1], 31, None, ALU.bitwise_and))
                    link(nc.vector.tensor_copy(k31[:], pidx_i[:, 1:2]))
                    link(nc.vector.tensor_scalar(ident[:], iota[:], nidx[:, 0:1], None, ALU.is_equal))
                    link(nc.vector.tensor_copy(identb[:], ident[:]))
                    link(nc.vector.tensor_scalar(tri[:], iota[:], nidx[:, 0:1], None, ALU.is_gt))
                    link(nc.vector.tensor_scalar(sel2[:].rearrange("k c p -> k (c p)"), sel2_i[:], k31[0:96, 0:1], None, ALU.is_equal))
                    link(nc.vector.tensor_scalar(sel4[:].rearrange("k c p -> k (c p)"), sel4_i[:], k31[0:96, 0:1], None, ALU.is_equal))
                    link(nc.vector.tensor_tensor(eye2[:], ident[:, 0:NS], ident[:, NS:P], ALU.add))
                    order_dve(dve)

        with ExitStack() as sc:
            order_pool, order_pe, order_dve = order_parts("d", sc)
            scatter_sp, scatter_pool = scatter_parts("s", sc)
            with nc.Block() as block:
                @block.sync
                def _(sp):
                    scatter_sp(sp)

                @block.gpsimd
                def _(pool):
                    order_pool(pool)
                    scatter_pool(pool)

                @block.tensor
                def _(pe):
                    order_pe(pe)

                @block.vector
                def _(dve):
                    order_dve(dve)
        early.close()
        end_stage()

        def node_rows(dram):
            return dram.rearrange("(t p) c -> p t c", p=P)

        def one(ap):
            return ap.rearrange("p o c -> p (o c)")

        def layernorm(n, to_output=False):
            with ExitStack() as sc:
                stats = sb(sc, f"stats_{n}", [P, NT, 6])
                mv = sb(sc, f"mv_{n}", [P, NT, 2])
                rstd = sb(sc, f"rstd_{n}", [P, NT])
                stats_ready, mv_ready, eps_added = sem(f"stats_ready_{n}"), sem(f"mv_ready_{n}"), sem(f"eps_added_{n}")
                rooted, inverted, normed = sem(f"rooted_{n}"), sem(f"inverted_{n}"), sem(f"normed_{n}")
                x_out = sem(f"x_out_{n}")
                with nc.Block() as block:
                    @block.vector
                    def _(dve):
                        with dve.Fori(0, NT) as nt:
                            nc.vector.bn_stats(one(stats[:, ds(nt, 1), :]), one(x[:, ds(nt, 1), :])).then_inc(stats_ready, 1)
                        dve.wait_ge(stats_ready, NT)
                        for nt in range(NT):
                            nc.vector.bn_aggr(mv[:, nt, :], stats[:, nt, :]).then_inc(mv_ready, 1)
                        dve.wait_ge(mv_ready, NT)
                        nc.vector.tensor_scalar(rstd[:].unsqueeze(2), mv[:, :, 1:2], 1e-5, None, ALU.add).then_inc(eps_added, 1)
                        dve.wait_ge(rooted, 1)
                        nc.vector.reciprocal(rstd[:], rstd[:]).then_inc(inverted, 1)
                        dve.wait_ge(inverted, 1)
                        for nt in range(NT):
                            nc.vector.tensor_scalar(x[:, nt, :], x[:, nt, :], mv[:, nt, 0:1], rstd[:, nt:nt + 1],
                                                    ALU.subtract, ALU.mult).then_inc(normed, 1)

                    @block.scalar
                    def _(act):
                        act.wait_ge(eps_added, 1)
                        nc.scalar.activation(rstd[:], rstd[:], ACT.Sqrt).then_inc(rooted, 1)

                    @block.sync
                    def _(sp):
                        sp.wait_ge(normed, NT)
                        if to_output:
                            sp.dma_start(node_rows(out[0:NFULL * P, :]), x[:, 0:NFULL, :]).then_inc(x_out, 16)
                            sp.dma_start(out[NFULL * P:N, :], x[0:NREST, NFULL, :]).then_inc(x_out, 16)
                            sp.wait_ge(x_out, 32)
                        else:
                            sp.dma_start(node_rows(h_dram), x[:]).then_inc(x_out, 16)
                            sp.wait_ge(x_out, 16)

        A_D, A_RS, A_RV, A_W = C, 2 * C, 2 * C + 3 * NS, 2 * C + 3 * NS + 3 * NV

        def product_layer(n, rows, scatter_beside, w, scales):
            rec = rec_s[0:P * T, :].rearrange("(p t) w -> p t w", t=T)
            layer = ExitStack()
            with layer:
                raw0 = sb(layer, f"raw0_{n}", [P, NS])
                rawt = sb(layer, f"rawt_{n}", [3 * NV, NS])
                raw1 = sb(layer, f"raw1_{n}", [P, NV])
                w0 = sb(layer, f"w0_{n}", [P, 2, NS])
                wt = sb(layer, f"wt_{n}", [3 * NV, 2, NS])
                w1 = sb(layer, f"w1_{n}", [P, 4, NV])
                wss = sb(layer, f"wss_{n}", [P, 32, NS])
                wvv = sb(layer, f"wvv_{n}", [P, 8, NS])
                wsv = sb(layer, f"wsv_{n}", [P, 16, NV])
                wvs = sb(layer, f"wvs_{n}", [P, 16, NV])
                lus = sb(layer, f"lus_{n}", [NS, NS])
                luv = sb(layer, f"luv_{n}", [NV, NV])
                aT = sb(layer, f"aT_{n}", [P, 4, NT * P])
                xpT = sb(layer, f"xpT_{n}", [96, 5, NT * P], BF16)
                w_in, w_scaled = sem(f"weights_in_{n}"), sem(f"weights_scaled_{n}")

                sums_scope = ExitStack()
                with sums_scope:
                    acc = sb(sums_scope, f"acc_{n}", [P, NT, A_W])

                    with ExitStack() as sc:
                        recb = [sb(sc, f"recb{i}_{n}", [P, TPG, WS]) for i in range(SLOTS)]
                        rowb = [sb(sc, f"rowb{i}_{n}", [P, TPG, C]) for i in range(SLOTS)]
                        spare = aT[:].rearrange("p i q -> p (i q)")
                        w_oh, w_msg = TPG * P, TPG * (A_W - C)
                        oh = [spare[:, i * w_oh:(i + 1) * w_oh].rearrange("p (k q) -> p k q", k=TPG) for i in range(SLOTS)]
                        spare = spare[:, SLOTS * w_oh:SLOTS * (w_oh + w_msg)]
                        msg = [spare[:, i * w_msg:(i + 1) * w_msg].rearrange("p (k q) -> p k q", k=TPG) for i in range(SLOTS)]
                        psa = [ps(sc, f"psa{i}_{n}", [P, 512]) for i in range(2)]
                        psb = [ps(sc, f"psb{i}_{n}", [P, 512]) for i in range(2)]
                        rec_in = [sem(f"rec_in{i}_{n}") for i in range(SLOTS)]
                        rows_in = [sem(f"rows_in{i}_{n}") for i in range(SLOTS)]
                        acc_zero, msg_ready, dist_ready, agg_done, evac_done = (sem(f"{a}_{n}") for a in (
                            "acc_zero", "msg_ready", "dist_ready", "agg_done", "evac_done"))
                        gather_turn = sem(f"gather_turn_{n}")
                        with nc.Block() as block:
                            @block.sync
                            def _(sp):
                                nw = 0
                                for dst, src in (
                                        (raw0[0:64, :], w["lm_s"]), (raw0[64:128, :], w["wm_ss"]), (rawt[0:32, :], w["wm_vv"]),
                                        (rawt[32:64, :], w["wm_vv"]), (rawt[64:96, :], w["wm_vv"]),
                                        (raw1[0:64, :], w["wm_sv"]), (raw1[64:96, :], w["lm_v"]), (raw1[96:128, :], w["wm_vs"]),
                                        (lus[:], w["lu_s"]), (luv[:], w["lu_v"]),
                                        (wss[:], w["wu_ss"].rearrange("u v w -> (u v) w").rearrange("(c p) w -> p c w", p=P)),
                                        (wvv[:], w["wu_vv"].rearrange("u v w -> (u v) w").rearrange("(c p) w -> p c w", p=P)),
                                        (wsv[:], w["wu_sv"].rearrange("u v w -> (u v) w").rearrange("(c p) w -> p c w", p=P)),
                                        (wvs[:], w["wu_vs"].rearrange("u v w -> (u v) w").rearrange("(c p) w -> p c w", p=P))):
                                    sp.dma_start(dst, src).then_inc(w_in, 16)
                                    nw += 16

                                def body(g, slot, turn):
                                    wait(sp, agg_done, g - (SLOTS - 1))
                                    sp.dma_start(recb[slot][:], rec[:, ds(TPG * g, TPG), :]).then_inc(rec_in[slot], 16)
                                steps(sp, NG, SLOTS, body)

                            @block.gpsimd
                            def _(pool):
                                def body(g, slot, turn):
                                    pool.wait_ge(rec_in[slot], (turn + 1) * 16)
                                    wait(pool, agg_done, g - (SLOTS - 1))
                                    stand(pool, gather_turn)
                                    for k in range(TPG):
                                        pool.indirect_dma_start(rowb[slot][:, k, :], None, rows,
                                                                bass.IndirectOffsetOnAxis(recb[slot][:, k, S_IDX:S_IDX + 1].bitcast(U32), 0)).then_inc(rows_in[slot], 16)
                                steps(pool, NG, SLOTS, body)

                            @block.scalar
                            def _(act):
                                def body(g, slot, turn):
                                    act.wait_ge(rows_in[slot], (turn + 1) * (16 * TPG))
                                    wait(act, agg_done, g - (SLOTS - 1))
                                    for k in range(TPG):
                                        last = nc.scalar.activation(msg[slot][:, k, 0:C], rowb[slot][:, k, :], ACT.Copy,
                                                                    scale=recb[slot][:, k, S_E4 + 3:S_E4 + 4])
                                    last.then_inc(dist_ready, 1)
                                steps(act, NG, SLOTS, body)
                                act.wait_ge(w_in, 16 * 14)
                                for r in range(2):
                                    nc.scalar.mul(w0[0:64, r, :], raw0[0:64, :], scales["lm_s"])
                                    nc.scalar.mul(w0[64:128, r, :], raw0[64:128, :], scales["wm_ss"])
                                    nc.scalar.mul(wt[:, r, :], rawt[:], scales["wm_vv"])
                                for r in range(4):
                                    nc.scalar.mul(w1[0:64, r, :], raw1[0:64, :], scales["wm_sv"])
                                    nc.scalar.mul(w1[64:96, r, :], raw1[64:96, :], scales["lm_v"])
                                    nc.scalar.mul(w1[96:128, r, :], raw1[96:128, :], scales["wm_vs"])
                                for a, f in ((wss, "wu_ss"), (wvv, "wu_vv"), (wsv, "wu_sv"), (wvs, "wu_vs")):
                                    nc.scalar.mul(a[:], a[:], scales[f])
                                nc.scalar.mul(lus[:], lus[:], scales["lu_s"])
                                nc.scalar.mul(luv[:], luv[:], scales["lu_v"]).then_inc(w_scaled, 1)

                            @block.vector
                            def _(dve):
                                def build(g, slot, turn):
                                    dve.wait_ge(rec_in[slot], (turn + 1) * 16)
                                    wait(dve, agg_done, g - (SLOTS - 1))
                                    rb, row, m = recb[slot], rowb[slot], msg[slot]
                                    nc.vector.tensor_tensor(oh[slot], iota[:].unsqueeze(1).broadcast_to([P, TPG, P]),
                                                            rb[:, :, S_LOC:S_LOC + 1].broadcast_to([P, TPG, P]), ALU.is_equal)
                                    dve.wait_ge(rows_in[slot], (turn + 1) * (16 * TPG))
                                    r = rb[:, :, S_E4:S_E4 + 3].unsqueeze(3)
                                    nc.vector.tensor_tensor(m[:, :, A_RS - C:A_RV - C].rearrange("p k (i c) -> p k i c", i=3),
                                                            row[:, :, 0:NS].unsqueeze(2).broadcast_to([P, TPG, 3, NS]),
                                                            r.broadcast_to([P, TPG, 3, NS]), ALU.mult)
                                    nc.vector.tensor_tensor(m[:, :, A_RV - C:A_W - C].rearrange("p k (i c) -> p k i c", i=3),
                                                            row[:, :, NS:C].rearrange("p k (i c) -> p k i c", i=3),
                                                            r.broadcast_to([P, TPG, 3, NV]), ALU.mult).then_inc(msg_ready, 1)

                                def body(g, slot, turn):
                                    if not isinstance(g, int) or g + 2 < NG:
                                        build(g + 2, (slot + 2) % SLOTS, turn + (slot + 2) // SLOTS)
                                    tile = dve.value_load(gtile["s"][0:1, ds(g, 1)], min_val=0, max_val=NT - 1)
                                    dve.wait_ge(agg_done, g + 1)
                                    wait(dve, evac_done, g)
                                    a = one(acc[:, ds(tile, 1), :])
                                    nc.vector.tensor_tensor(a[:, 0:C], psa[slot % 2][:, 0:C], a[:, 0:C], ALU.add)
                                    nc.vector.tensor_tensor(a[:, C:A_W], psb[slot % 2][:, 0:A_W - C], a[:, C:A_W], ALU.add).then_inc(evac_done, 1)

                                nc.vector.memset(acc[:], 0.0).then_inc(acc_zero, 1)
                                build(0, 0, 0)
                                build(1, 1, 0)
                                dve.wait_ge(acc_zero, 1)
                                steps(dve, NG, SLOTS, body, tail=2)

                            @block.tensor
                            def _(pe):
                                def body(g, slot, turn):
                                    pe.wait_ge(msg_ready, g + 1)
                                    pe.wait_ge(rows_in[slot], (turn + 1) * (16 * TPG))
                                    wait(pe, evac_done, g - 1)
                                    b = slot % 2
                                    for k in range(TPG):
                                        nc.tensor.matmul(psa[b][:, 0:C], oh[slot][:, k, :], rowb[slot][:, k, :], start=(k == 0), stop=(k == TPG - 1))
                                    pe.wait_ge(dist_ready, g + 1)
                                    for k in range(TPG):
                                        last = nc.tensor.matmul(psb[b][:, 0:A_W - C], oh[slot][:, k, :], msg[slot][:, k, :], start=(k == 0), stop=(k == TPG - 1))
                                    last.then_inc(agg_done, 1)
                                steps(pe, NG, SLOTS, body)

                    with ExitStack() as sc:
                        SG = 4 * P + 3 * NV
                        stg = [sb(sc, f"stg{i}_{n}", [P, SG]) for i in range(2)]
                        xst = [sb(sc, f"xst{i}_{n}", [P, C]) for i in range(2)]
                        xsp = [sb(sc, f"xsp{i}_{n}", [P, 5, 3, NV], BF16) for i in range(2)]
                        rest = sb(sc, f"rest_{n}", [P, 2, C])
                        cT = [sb(sc, f"cT{i}_{n}", [P, 512]) for i in range(2)]
                        rT = [sb(sc, f"rT{i}_{n}", [3 * NV, P]) for i in range(2)]
                        xT = [sb(sc, f"xT{i}_{n}", [NS, 4, P]) for i in range(2)]
                        ps_c = ps(sc, f"ps_c_{n}", [P, 512])
                        ps_r = ps(sc, f"ps_r_{n}", [P, 512])
                        ps_v = ps(sc, f"ps_v_{n}", [P, 4, P])
                        ps_x = ps(sc, f"ps_x_{n}", [P, 1024], BF16)
                        ps_a = ps(sc, f"ps_a_{n}", [P, 4, P])
                        ps_d = ps(sc, f"ps_d_{n}", [P, 512])
                        (staged, split, split_a, split_b, split_c, split_d, split_turn, turned, sums_copied, x_copied, a_done, a_copied, x_done) = (
                            sem(f"{a}_{n}") for a in ("staged", "split", "split_a", "split_b", "split_c", "split_d", "split_turn",
                                                      "turned", "sums_copied", "x_copied", "a_done", "a_copied", "x_done"))
                        with nc.Block() as block:
                            @block.scalar
                            def _(act):
                                def stage(t_, slot):
                                    wait(act, turned, t_ - 1)
                                    wait(act, split, t_ - 1)
                                    a = one(acc[:, ds(t_, 1), :])
                                    pair = a[:, 0:2 * C].rearrange("p (a c) -> p a c", a=2)
                                    nc.scalar.copy(stg[slot][:, 0:P].rearrange("p (a c) -> p a c", a=2), pair[:, :, 0:NS])
                                    vec = stg[slot][:, P:4 * P].rearrange("p (i c) -> p i c", i=3)
                                    nc.scalar.copy(vec[:, :, 0:NS], a[:, A_RS:A_RV].rearrange("p (i c) -> p i c", i=3))
                                    for k in range(2):
                                        nc.scalar.copy(vec[:, :, NS + NV * k:NS + NV * (k + 1)], pair[:, k, NS:C].rearrange("p (i c) -> p i c", i=3))
                                    nc.scalar.copy(stg[slot][:, 4 * P:SG], a[:, A_RV:A_W])
                                    nc.scalar.copy(xst[slot][:], one(x[:, ds(t_, 1), :])).then_inc(staged, 1)

                                def body(t_, slot, turn):
                                    if not (isinstance(t_, int) and t_ == NT - 1):
                                        stage(t_ + 1, 1 - slot)
                                    act.wait_ge(turned, t_ + 1)
                                    wait(act, x_done, t_ - 1)
                                    nc.scalar.copy(xT[slot][:, 0, :], ps_v[0:NS, 0, :])
                                    nc.scalar.copy(xT[slot][0:NV, 1:4, :], ps_v[0:NV, 1:4, :])
                                    nc.scalar.copy(xpT[:, :, ds(t_ * P, P)], ps_x[0:96, 0:5 * P].rearrange("k (g p) -> k g p", g=5)).then_inc(x_copied, 1)
                                stage(0, 0)
                                steps(act, NT, 2, body, tail=1)

                            @block.gpsimd
                            def _(pool):
                                def body(t_, slot, turn):
                                    pool.wait_ge(staged, t_ + 1)
                                    wait(pool, turned, t_ - 1)
                                    stand(pool, split_turn)
                                    src = xst[slot][:].rearrange("p (g c) -> p g c", g=5)
                                    part = xsp[slot]
                                    r1 = rest[:, 0, :].rearrange("p (g c) -> p g c", g=5)
                                    r2 = rest[:, 1, :].rearrange("p (g c) -> p g c", g=5)
                                    nc.gpsimd.tensor_copy(part[:, :, 0, :], src).then_inc(split_a, 1)
                                    pool.wait_ge(split_a, t_ + 1)
                                    stand(pool, split_turn)
                                    nc.gpsimd.tensor_tensor(r1, src, part[:, :, 0, :], ALU.subtract).then_inc(split_b, 1)
                                    pool.wait_ge(split_b, t_ + 1)
                                    stand(pool, split_turn)
                                    nc.gpsimd.tensor_copy(part[:, :, 1, :], r1).then_inc(split_c, 1)
                                    pool.wait_ge(split_c, t_ + 1)
                                    stand(pool, split_turn)
                                    nc.gpsimd.tensor_tensor(r2, r1, part[:, :, 1, :], ALU.subtract).then_inc(split_d, 1)
                                    pool.wait_ge(split_d, t_ + 1)
                                    stand(pool, split_turn)
                                    nc.gpsimd.tensor_copy(part[:, :, 2, :], r2).then_inc(split, 1)
                                steps(pool, NT, 2, body)

                            @block.vector
                            def _(dve):
                                def body(t_, slot, turn):
                                    dve.wait_ge(turned, t_ + 1)
                                    wait(dve, a_done, t_ - 1)
                                    nc.vector.tensor_copy(cT[slot][:], ps_c[:])
                                    nc.vector.tensor_copy(rT[slot][:], ps_r[0:3 * NV, 0:P]).then_inc(sums_copied, 1)
                                    dve.wait_ge(x_done, t_ + 1)
                                    row = one(x[:, ds(t_, 1), :])
                                    nc.vector.scalar_tensor_tensor(row, row, 2.0, ps_d[:, 0:C], ALU.mult, ALU.add)
                                    dve.wait_ge(a_done, t_ + 1)
                                    nc.vector.tensor_copy(aT[:, :, ds(t_ * P, P)], ps_a[:]).then_inc(a_copied, 1)
                                steps(dve, NT, 2, body)

                            @block.tensor
                            def _(pe):
                                def turn_over(t_, slot):
                                    pe.wait_ge(staged, t_ + 1)
                                    wait(pe, sums_copied, t_)
                                    wait(pe, x_copied, t_)
                                    for i in range(4):
                                        nc.tensor.transpose(ps_c[:, i * P:(i + 1) * P], stg[slot][:, i * P:(i + 1) * P], ident[:])
                                    nc.tensor.transpose(ps_r[0:3 * NV, 0:P], stg[slot][:, 4 * P:SG], ident[:])
                                    nc.tensor.transpose(ps_v[0:NS, 0, :], xst[slot][:, 0:NS], ident[:])
                                    for i in range(3):
                                        nc.tensor.transpose(ps_v[0:NV, 1 + i, :], xst[slot][:, OV[i]:OV[i] + NV], ident[:])
                                    pe.wait_ge(split, t_ + 1)
                                    for i in range(5):
                                        last = nc.tensor.transpose(ps_x[0:96, i * P:(i + 1) * P], xsp[slot][:, i, :, :].rearrange("p a c -> p (a c)"), identb[:])
                                    last.then_inc(turned, 1)

                                def body(t_, slot, turn):
                                    if not (isinstance(t_, int) and t_ == NT - 1):
                                        turn_over(t_ + 1, 1 - slot)
                                    pe.wait_ge(x_copied, t_ + 1)
                                    wait(pe, a_copied, t_)
                                    nc.tensor.matmul(ps_d[:, 0:NS], xT[slot][:, 0, :], lus[:], start=True, stop=False, skip_group_check=True)
                                    for i in range(3):
                                        last = nc.tensor.matmul(ps_d[:, OV[i]:OV[i] + NV], xT[slot][0:NV, 1 + i, :], luv[:], start=False, stop=(i == 2), skip_group_check=True)
                                    last.then_inc(x_done, 1)
                                    pe.wait_ge(sums_copied, t_ + 1)
                                    nc.tensor.matmul(ps_a[:, 0, :], w0[:].rearrange("k r w -> k (r w)"), cT[slot][:, 0:P], start=True, stop=False, skip_group_check=True)
                                    nc.tensor.matmul(ps_a[:, 0, :], wt[:].rearrange("k r w -> k (r w)"), rT[slot][:], start=False, stop=False, skip_group_check=True)
                                    nc.tensor.matmul(ps_a[:, 1:4, :], w1[:].rearrange("k r w -> k (r w)"), cT[slot][:, P:512], start=False, stop=True, skip_group_check=True).then_inc(a_done, 1)
                                pe.wait_ge(w_scaled, 1)
                                turn_over(0, 0)
                                steps(pe, NT, 2, body, tail=1)

                S_LO, S_HI, VEC = 0, NS, 2 * NS
                chunks = []
                for gp in (0, 1):
                    for c in range(16):
                        chunks.append((sel2, c, gp, [(0, wss, 16 * gp + c, S_HI if c % 2 else S_LO)]))
                for i in range(3):
                    for c in range(8):
                        chunks.append((sel4, c, 2 + i, [(1 + i, wvv, c, S_HI if c % 2 else S_LO)]))
                for c in range(16):
                    for i in range(3):
                        chunks.append((sel2, c, 2 + i, [(0, wvs, c, VEC + NV * i)]))
                for gp in (0, 1):
                    for c in range(8):
                        chunks.append((sel4, c, gp, [(1 + i, wsv, 8 * gp + c, VEC + NV * i) for i in range(3)]))
                BATCH = 4
                NBATCH = len(chunks) // BATCH
                starts, ends = {}, {}
                for q, ch in enumerate(chunks):
                    for part in ch[3]:
                        starts.setdefault(part[3], q)
                        ends[part[3]] = q
                with ExitStack() as sc:
                    uS = sb(sc, f"uS_{n}", [P, NT * P])
                    uV = sb(sc, f"uV_{n}", [3 * NV, NT * P])
                    with ExitStack() as sc2:
                        xb = [sb(sc2, f"xb{i}_{n}", [96, 5, BLK], BF16) for i in range(2)]
                        zb = [sb(sc2, f"zb{i}_{n}", [P, 3, BLK]) for i in range(BATCH + 1)]
                        bc = [ps(sc2, f"bc{i}_{n}", [P, 512]) for i in range(BATCH)]
                        ps_s = [ps(sc2, f"ps_s{i}_{n}", [P, 512]) for i in range(2)]
                        ps_w = [ps(sc2, f"ps_w{i}_{n}", [P, 512]) for i in range(2)]
                        xb_ready, spread, paired, used, u_copied, tail_zero = (sem(f"{a}_{n}") for a in (
                            "xb_ready", "spread", "paired", "used", "u_copied", "tail_zero"))
                        NCH = len(chunks)
                        NZ = len(zb)
                        if scatter_beside:
                            scatter_sp, scatter_pool = scatter_parts(scatter_beside, sc2)
                        with nc.Block() as block:
                            if scatter_beside:
                                @block.sync
                                def _(sp):
                                    scatter_sp(sp)

                                @block.gpsimd
                                def _(pool):
                                    scatter_pool(pool)

                            @block.scalar
                            def _(act):
                                def body(b, slot, turn):
                                    if not (isinstance(b, int) and b == NB - 1):
                                        wait(act, spread, b * NCH)
                                        nc.scalar.copy(xb[1 - slot][:], xpT[:, :, ds((b + 1) * BLK, BLK)]).then_inc(xb_ready, 1)
                                    act.wait_ge(used, (b + 1) * NCH)
                                    nc.scalar.copy(uS[:, ds(b * BLK, BLK)], ps_s[slot][:, 0:BLK])
                                    nc.scalar.copy(uV[:, ds(b * BLK, BLK)], ps_w[slot][0:3 * NV, 0:BLK]).then_inc(u_copied, 1)
                                nc.scalar.copy(xb[0][:], xpT[:, :, 0:BLK]).then_inc(xb_ready, 1)
                                steps(act, NB, 2, body, tail=1)

                            @block.vector
                            def _(dve):
                                def body(b, slot, turn):
                                    for q, (sel, c, gp, parts) in enumerate(chunks):
                                        at = b * NCH + q
                                        z = zb[(slot * NCH + q) % NZ]
                                        dve.wait_ge(spread, at + 1)
                                        wait(dve, used, at + 1 - NZ)
                                        m = len(parts)
                                        a0 = parts[0][0]
                                        nc.vector.tensor_tensor(z[:, 0:m, :], bc[q % BATCH][:, 0:BLK].unsqueeze(1).broadcast_to([P, m, BLK]),
                                                                aT[:, a0:a0 + m, ds(b * BLK, BLK)], ALU.mult).then_inc(paired, 1)
                                nc.vector.memset(uS[:, NB * BLK:NT * P], 0.0).then_inc(tail_zero, 1)
                                nc.vector.memset(uV[:, NB * BLK:NT * P], 0.0).then_inc(tail_zero, 1)
                                steps(dve, NB, 2, body, tail=1)

                            @block.tensor
                            def _(pe):
                                def contract(b, slot, q):
                                    sel, c, gp, parts = chunks[q]
                                    pe.wait_ge(paired, b * NCH + q + 1)
                                    for j, (a0, wu, wc, at) in enumerate(parts):
                                        dst, m = (ps_w[slot], NV) if at >= VEC else (ps_s[slot], NS)
                                        row = at - VEC if at >= VEC else at
                                        last = nc.tensor.matmul(dst[row:row + m, 0:BLK], wu[:, wc, :], zb[(slot * NCH + q) % NZ][:, j, :],
                                                                start=(starts[at] == q), stop=(ends[at] == q), skip_group_check=True)
                                    last.then_inc(used, 1)

                                def body(b, slot, turn):
                                    pe.wait_ge(xb_ready, b + 1)
                                    wait(pe, u_copied, b - 1)
                                    for batch in range(NBATCH + 1):
                                        for q in range(batch * BATCH, min((batch + 1) * BATCH, NCH)):
                                            sel, c, gp, parts = chunks[q]
                                            wait(pe, paired, b * NCH + q + 1 - BATCH)
                                            nc.tensor.matmul(bc[q % BATCH][:, 0:BLK], sel[:, c, :], xb[slot][:, gp, :], start=True, stop=True).then_inc(spread, 1)
                                        for q in range((batch - 1) * BATCH, batch * BATCH):
                                            if q >= 0:
                                                contract(b, slot, q)
                                steps(pe, NB, 2, body, tail=1)

                    with ExitStack() as sc2:
                        back = [ps(sc2, f"back{i}_{n}", [P, 512]) for i in range(4)]
                        turned_back, added = sem(f"turned_back_{n}"), sem(f"added_{n}")
                        with nc.Block() as block:
                            @block.tensor
                            def _(pe):
                                for t_ in range(NT):
                                    wait(pe, added, t_ - 3)
                                    nc.tensor.matmul(back[t_ % 4][:, 0:NS], uS[:, t_ * P:(t_ + 1) * P], eye2[:], start=True, stop=False, skip_group_check=True)
                                    nc.tensor.matmul(back[t_ % 4][:, NS:C], uV[:, t_ * P:(t_ + 1) * P], ident[0:96, 0:96], start=False, stop=True, skip_group_check=True).then_inc(turned_back, 1)

                            @block.vector
                            def _(dve):
                                for t_ in range(NT):
                                    dve.wait_ge(turned_back, t_ + 1)
                                    nc.vector.tensor_tensor(x[:, t_, :], x[:, t_, :], back[t_ % 4][:, 0:C], ALU.add).then_inc(added, 1)

        def filter_layer(n, f):
            rec = rec_d[0:P * T, :].rearrange("(p t) w -> p t w", t=T)
            one_l = n == 1
            K, KC = f["fc_in"], f["fc_col"]
            NW, NSC = f["nw"], f["nsc"]
            PW = 448 if one_l else 320
            MW = f["wa"] + f["wb"]
            WA, WB = f["wa"], f["wb"]
            layer = ExitStack()
            with layer:
                acc = sb(layer, f"acc_{n}", [P, NT, WA + WB])
                sconn = sb(layer, f"sconn_{n}", [P, NT, NSC + 96])
                ws = sb(layer, f"ws_{n}", [NS, NS + NSC])
                wv = sb(layer, f"wv_{n}", [NV, 2 * NV])
                fc1 = sb(layer, f"fc1_{n}", [K, 64])
                fc2 = sb(layer, f"fc2_{n}", [64, NW])
                NO = f["no"]
                KV = f["kv"]
                wos = sb(layer, f"wos_{n}", [96, NO])
                wov = sb(layer, f"wov_{n}", [KV, NV])
                w_in, w_scaled, h_out, h_written = (sem(f"{a}_{n}") for a in ("weights_in", "weights_scaled", "h_out", "h_written"))

                with ExitStack() as sc:
                    xst = [sb(sc, f"xst{i}_{n}", [P, C]) for i in range(2)]
                    xT = [sb(sc, f"xT{i}_{n}", [NS, 4, P]) for i in range(2)]
                    hst = [sb(sc, f"hst{i}_{n}", [P, C]) for i in range(2)]
                    pT = [ps(sc, f"pT{i}_{n}", [P, 4, P]) for i in range(2)]
                    pP = [ps(sc, f"pP{i}_{n}", [P, 512]) for i in range(2)]
                    staged, transposed, tcopied, mapped, taken = (sem(f"pre_{a}_{n}") for a in ("staged", "transposed", "tcopied", "mapped", "taken"))
                    h_sent = [sem(f"h_sent{i}_{n}") for i in range(2)]
                    turn_begun = sem(f"pre_turn_begun_{n}")
                    with nc.Block() as block:
                        @block.scalar
                        def _(act):
                            nw = 0
                            for dst, src in f["loads"](ws, wv, fc1, fc2, wos, wov):
                                act.dma_start(dst, src).then_inc(w_in, 16)
                                nw += 16
                            act.wait_ge(w_in, nw)
                            for ap, s in f["scale"](ws, wv, fc1, fc2, wos, wov):
                                last = nc.scalar.mul(ap, ap, s)
                            last.then_inc(w_scaled, 1)

                            def body(t_, slot, turn):
                                wait(act, transposed, t_ - 1)
                                nc.scalar.copy(xst[slot][:], one(x[:, ds(t_, 1), :])).then_inc(staged, 1)
                                act.wait_ge(transposed, t_ + 1)
                                wait(act, mapped, t_ - 1)
                                nc.scalar.copy(xT[slot][:, 0, :], pT[slot][0:NS, 0, :])
                                nc.scalar.copy(xT[slot][0:NV, 1:4, :], pT[slot][0:NV, 1:4, :]).then_inc(tcopied, 1)
                            steps(act, NT, 2, body)

                        @block.tensor
                        def _(pe):
                            def transposes(t_, slot):
                                pe.wait_ge(staged, t_ + 1)
                                wait(pe, tcopied, t_ - 1)
                                stand(pe, turn_begun)
                                nc.tensor.transpose(pT[slot][0:NS, 0, :], xst[slot][:, OS:OS + NS], ident[:])
                                for i in range(3):
                                    last = nc.tensor.transpose(pT[slot][0:NV, 1 + i, :], xst[slot][:, OV[i]:OV[i] + NV], ident[:])
                                last.then_inc(transposed, 1)

                            def body(t_, slot, turn):
                                if not (isinstance(t_, int) and t_ == NT - 1):
                                    transposes(t_ + 1, 1 - slot)
                                pe.wait_ge(tcopied, t_ + 1)
                                wait(pe, taken, t_ - 1)
                                nc.tensor.matmul(pP[slot][:, 0:NS + NSC], xT[slot][:, 0, :], ws[:], start=True, stop=False, skip_group_check=True)
                                for i in range(3):
                                    c0 = NS + NSC + 2 * NV * i
                                    last = nc.tensor.matmul(pP[slot][:, c0:c0 + 2 * NV], xT[slot][0:NV, 1 + i, :], wv[:], start=False, stop=(i == 2), skip_group_check=True)
                                last.then_inc(mapped, 1)
                            pe.wait_ge(w_scaled, 1)
                            transposes(0, 0)
                            steps(pe, NT, 2, body, tail=1)

                        @block.vector
                        def _(dve):
                            def body(t_, slot, turn):
                                dve.wait_ge(mapped, t_ + 1)
                                wait(dve, h_sent[slot], turn * 16)
                                a = attr[:, ds(t_, 1)]
                                p, h, s = pP[slot], hst[slot], one(sconn[:, ds(t_, 1), :])
                                vec = p[:, NS + NSC:NS + NSC + 6 * NV].rearrange("p (i c) -> p i c", i=3)
                                nc.vector.tensor_scalar(h[:, 0:NS], p[:, 0:NS], a, None, ALU.mult)
                                nc.vector.tensor_scalar(h[:, NS:C].rearrange("p (i c) -> p i c", i=3), vec[:, :, 0:NV], a, None, ALU.mult)
                                nc.vector.tensor_scalar(s[:, 0:NSC], p[:, NS:NS + NSC], a, None, ALU.mult)
                                nc.vector.tensor_scalar(s[:, NSC:NSC + 96].rearrange("p (i c) -> p i c", i=3), vec[:, :, NV:2 * NV], a, None, ALU.mult).then_inc(taken, 1)
                            steps(dve, NT, 2, body)
                            nc.vector.memset(acc[:], 0.0).then_inc(h_written, 1)

                        @block.sync
                        def _(sp):
                            def body(t_, slot, turn):
                                sp.wait_ge(taken, t_ + 1)
                                sp.dma_start(h_dram[ds(t_ * P, P), :], hst[slot][:]).then_inc(h_sent[slot], 16)
                            steps(sp, NT, 2, body)
                            sp.wait_ge(h_sent[0], 16 * ((NT + 1) // 2))
                            sp.wait_ge(h_sent[1], 16 * (NT // 2))

                with ExitStack() as sc:
                    recb = [sb(sc, f"recb{i}_{n}", [P, TPG, WD]) for i in range(SLOTS)]
                    rowb = [sb(sc, f"rowb{i}_{n}", [P, TPG, C]) for i in range(SLOTS)]
                    oh = [sb(sc, f"oh{i}_{n}", [P, TPG, P]) for i in range(SLOTS)]
                    prod = [sb(sc, f"prod{i}_{n}", [P, TPG, PW]) for i in range(SLOTS)]
                    msg = [sb(sc, f"msg{i}_{n}", [P, TPG, MW]) for i in range(SLOTS)]
                    eT = sb(sc, f"eT_{n}", [K, TPG * P])
                    hid = sb(sc, f"hid_{n}", [64, TPG * P])
                    psa = [ps(sc, f"psa{i}_{n}", [P, 512]) for i in range(2)]
                    psb = [ps(sc, f"psb{i}_{n}", [P, 512]) for i in range(2)]
                    psw = [ps(sc, f"psw{i}_{n}", [P, 512]) for i in range(2)]
                    psT = ps(sc, f"psT_{n}", [P, 512])
                    psH = ps(sc, f"psH_{n}", [P, 512])
                    rec_in = [sem(f"rec_in{i}_{n}") for i in range(SLOTS)]
                    rows_in = [sem(f"rows_in{i}_{n}") for i in range(SLOTS)]
                    (oh_ready, agg_done, evac_done, gather_turn, e_turned, eT_ready, fc1_done, hid_ready, fc2_done, prod_ready) = (
                        sem(f"{a}_{n}") for a in ("oh_ready", "agg_done", "evac_done", "gather_turn", "e_turned", "eT_ready",
                                                  "fc1_done", "hid_ready", "fc2_done", "prod_ready"))
                    scaled, msg_ready = sem(f"scaled_{n}"), sem(f"msg_ready_{n}")
                    ones_ready, turn_begun = sem(f"ones_ready_{n}"), sem(f"edge_turn_begun_{n}")
                    with nc.Block() as block:
                        @block.sync
                        def _(sp):
                            def body(g, slot, turn):
                                wait(sp, agg_done, g - (SLOTS - 1))
                                sp.dma_start(recb[slot][:, :, KC:WD], rec[:, ds(TPG * g, TPG), KC:WD]).then_inc(rec_in[slot], 16)
                            steps(sp, NG, SLOTS, body)

                        @block.gpsimd
                        def _(pool):
                            def body(g, slot, turn):
                                pool.wait_ge(rec_in[slot], (turn + 1) * 16)
                                wait(pool, prod_ready, g - (SLOTS - 1))
                                stand(pool, gather_turn)
                                for k in range(TPG):
                                    pool.indirect_dma_start(rowb[slot][:, k, :], None, h_dram,
                                                            bass.IndirectOffsetOnAxis(recb[slot][:, k, D_IDX:D_IDX + 1].bitcast(U32), 0)).then_inc(rows_in[slot], 16)
                            steps(pool, NG, SLOTS, body)

                        @block.scalar
                        def _(act):
                            def turned(g):
                                act.wait_ge(e_turned, g + 1)
                                wait(act, fc1_done, g)
                                nc.scalar.copy(eT[:], psT[0:K, 0:TPG * P]).then_inc(eT_ready, 1)

                            def hidden(g):
                                act.wait_ge(fc1_done, g + 1)
                                wait(act, fc2_done, g)
                                nc.scalar.activation(hid[:], psH[0:64, 0:TPG * P], ACT.Silu, scale=f["silu_scale"]).then_inc(hid_ready, 1)

                            def scale(g, slot, k):
                                act.wait_ge(prod_ready, g + 1)
                                wait(act, agg_done, g - (SLOTS - 1))
                                rb, pr, m = recb[slot], prod[slot], msg[slot]
                                last = nc.scalar.activation(m[:, k, 0:C], pr[:, k, 0:C], ACT.Copy, scale=rb[:, k, D_E4:D_E4 + 1])
                                for i in range(3 if one_l else 0):
                                    last = nc.scalar.activation(m[:, k, 352 + 96 * i:448 + 96 * i], pr[:, k, 224 + 2 * NV * i:320 + 2 * NV * i],
                                                                ACT.Copy, scale=rb[:, k, D_E4 + 1 + i:D_E4 + 2 + i])
                                last.then_inc(scaled, 1)

                            def body(g, slot, turn):
                                if not isinstance(g, int) or g + 2 < NG:
                                    turned(g + 2)
                                if not isinstance(g, int) or g + 1 < NG:
                                    scale(g + 1, (slot + 1) % SLOTS, 0)
                                if not isinstance(g, int) or g + 2 < NG:
                                    hidden(g + 2)
                                if not isinstance(g, int) or g + 1 < NG:
                                    scale(g + 1, (slot + 1) % SLOTS, 1)
                            for g in range(2):
                                turned(g)
                                hidden(g)
                            for k in range(TPG):
                                scale(0, 0, k)
                            steps(act, NG, SLOTS, body, tail=2)

                        @block.vector
                        def _(dve):
                            def products(g, slot, turn):
                                dve.wait_ge(rec_in[slot], (turn + 1) * 16)
                                wait(dve, agg_done, g - (SLOTS - 1))
                                wait(dve, scaled, (g - (SLOTS - 1)) * TPG)
                                b = slot
                                nc.vector.tensor_tensor(oh[b][:], iota[:].unsqueeze(1).broadcast_to([P, TPG, P]),
                                                        recb[slot][:, :, D_LOC:D_LOC + 1].broadcast_to([P, TPG, P]), ALU.is_equal)
                                dve.wait_ge(rows_in[slot], (turn + 1) * (16 * TPG))
                                dve.wait_ge(fc2_done, g + 1)
                                w = psw[slot % 2][:, 0:TPG * NW].rearrange("p (k c) -> p k c", k=TPG)
                                row, pr = rowb[slot], prod[b]
                                es = row[:, :, 0:NS].unsqueeze(2).broadcast_to([P, TPG, 2, NS])
                                ev = row[:, :, NS:C].rearrange("p k (i c) -> p k i c", i=3)

                                def mul(dst, x_, wcol, m):
                                    return nc.vector.tensor_tensor(dst, w[:, :, wcol:wcol + NV].unsqueeze(2).broadcast_to([P, TPG, m, NV]), x_, ALU.mult)
                                nc.vector.tensor_tensor(pr[:, :, 0:320].rearrange("p k (a c) -> p k a c", a=2)[:, :, :, 0:NS],
                                                        w[:, :, 0:2 * NS].rearrange("p k (a c) -> p k a c", a=2), es, ALU.mult)
                                last = mul(pr[:, :, NS:C].rearrange("p k (i c) -> p k i c", i=3), ev, 2 * NS, 3)
                                if one_l:
                                    seq = pr[:, :, 224:448].rearrange("p k (b c) -> p k b c", b=7)
                                    mul(seq[:, :, 0:7:3, :], ev, 2 * NS + NV, 3)
                                    mul(seq[:, :, 1:3, :], ev[:, :, 1:3, :], 2 * NS + 2 * NV, 2)
                                    last = mul(seq[:, :, 4:6, :], ev[:, :, 0:2, :], 2 * NS + 2 * NV, 2)
                                else:
                                    last = mul(pr[:, :, 224:320].rearrange("p k (i c) -> p k i c", i=3), ev, 2 * NS + NV, 3)
                                last.then_inc(prod_ready, 1)
                                dve.wait_ge(prod_ready, g + 1)
                                m = msg[b]
                                e1 = recb[slot][:, :, D_E4 + 1:D_E4 + 4].unsqueeze(3)
                                last = nc.vector.tensor_tensor(m[:, :, C:352].rearrange("p k (i c) -> p k i c", i=3),
                                                               pr[:, :, C:C + NS].unsqueeze(2).broadcast_to([P, TPG, 3, NS]),
                                                               e1.broadcast_to([P, TPG, 3, NS]), ALU.mult)
                                if not one_l:
                                    last = nc.vector.tensor_tensor(m[:, :, 352:448].rearrange("p k (i c) -> p k i c", i=3),
                                                                   pr[:, :, 224:320].rearrange("p k (i c) -> p k i c", i=3),
                                                                   e1.broadcast_to([P, TPG, 3, NV]), ALU.mult)
                                last.then_inc(msg_ready, 1)

                            def body(g, slot, turn):
                                if not isinstance(g, int) or g + 2 < NG:
                                    products(g + 2, (slot + 2) % SLOTS, turn + (slot + 2) // SLOTS)
                                tile = dve.value_load(gtile["d"][0:1, ds(g, 1)], min_val=0, max_val=NT - 1)
                                dve.wait_ge(agg_done, g + 1)
                                wait(dve, evac_done, g)
                                a = one(acc[:, ds(tile, 1), :])
                                last = nc.vector.tensor_tensor(a[:, 0:WA], psa[slot % 2][:, 0:WA], a[:, 0:WA], ALU.add)
                                if WB:
                                    last = nc.vector.tensor_tensor(a[:, WA:WA + WB], psb[slot % 2][:, 0:WB], a[:, WA:WA + WB], ALU.add)
                                last.then_inc(evac_done, 1)

                            for b in range(SLOTS):
                                nc.vector.memset(msg[b][:, :, MW - 1:MW], 1.0).then_inc(ones_ready, 1)
                            products(0, 0, 0)
                            products(1, 1, 0)
                            steps(dve, NG, SLOTS, body, tail=2)

                        @block.tensor
                        def _(pe):
                            def turn_e(g, slot, turn):
                                pe.wait_ge(rec_in[slot], (turn + 1) * 16)
                                wait(pe, eT_ready, g)
                                stand(pe, turn_begun)
                                for k in range(TPG):
                                    last = nc.tensor.transpose(psT[0:K, k * P:(k + 1) * P], recb[slot][:, k, KC:KC + K], ident[:])
                                last.then_inc(e_turned, 1)

                            def first(g):
                                pe.wait_ge(eT_ready, g + 1)
                                wait(pe, hid_ready, g)
                                stand(pe, turn_begun)
                                nc.tensor.matmul(psH[0:64, 0:TPG * P], fc1[:], eT[:], start=True, stop=True).then_inc(fc1_done, 1)

                            def second(g, slot):
                                pe.wait_ge(hid_ready, g + 1)
                                wait(pe, prod_ready, g - 1)
                                for k in range(TPG):
                                    last = nc.tensor.matmul(psw[slot % 2][:, k * NW:(k + 1) * NW], hid[:, k * P:(k + 1) * P], fc2[:],
                                                            start=(k == 0), stop=(k == TPG - 1), skip_group_check=True)
                                last.then_inc(fc2_done, 1)

                            def sums(slot, k):
                                b, st, en = slot % 2, k == 0, k == TPG - 1
                                last = nc.tensor.matmul(psa[b][:, 0:WA], oh[slot][:, k, :], msg[slot][:, k, 0:WA], start=st, stop=en)
                                if WB:
                                    last = nc.tensor.matmul(psb[b][:, 0:WB], oh[slot][:, k, :], msg[slot][:, k, WA:MW], start=st, stop=en)
                                return last

                            def body(g, slot, turn):
                                ahead = not isinstance(g, int) or g + 2 < NG
                                s2, t2 = (slot + 2) % SLOTS, turn + (slot + 2) // SLOTS
                                if ahead:
                                    turn_e(g + 2, s2, t2)
                                pe.wait_ge(msg_ready, g + 1)
                                pe.wait_ge(scaled, (g + 1) * TPG)
                                wait(pe, evac_done, g - 1)
                                sums(slot, 0)
                                if ahead:
                                    first(g + 2)
                                sums(slot, 1).then_inc(agg_done, 1)
                                if ahead:
                                    second(g + 2, s2)
                            pe.wait_ge(ones_ready, SLOTS)
                            for g in range(2):
                                turn_e(g, g, 0)
                                first(g)
                                second(g, g)
                            steps(pe, NG, SLOTS, body, tail=2)

                with ExitStack() as sc:
                    sg = [sb(sc, f"sg{i}_{n}", [P, 96 + 3 * KV]) for i in range(2)]
                    tmp = [sb(sc, f"tmp{i}_{n}", [P, NV]) for i in range(2)]
                    sT = [sb(sc, f"sT{i}_{n}", [P, 4, P]) for i in range(2)]
                    pT = [ps(sc, f"qT{i}_{n}", [P, 4, P]) for i in range(2)]
                    pO = [ps(sc, f"pO{i}_{n}", [P, 512]) for i in range(2)]
                    factor = sb(sc, f"factor_{n}", [P, 3, NT])
                    gates = sb(sc, f"gates_{n}", [P, NT, 96]) if one_l else None
                    staged, t_summed, transposed, tcopied, mapped, taken, f_step, acted, gated, y_step = (
                        sem(f"post_{a}_{n}") for a in ("staged", "t_summed", "transposed", "tcopied", "mapped", "taken", "f_step", "acted", "gated", "y_step"))
                    with nc.Block() as block:
                        @block.vector
                        def _(dve):
                            def stage(t_, slot):
                                a = one(acc[:, ds(t_, 1), :])
                                wait(dve, transposed, t_ - 1)
                                s_ = sg[slot]
                                vec = s_[:, 96:96 + 3 * KV].rearrange("p (i c) -> p i c", i=3)
                                nc.vector.tensor_copy(s_[:, 0:NS], a[:, 0:NS])
                                nc.vector.tensor_copy(vec[:, :, NS:NS + NV], a[:, NS:C].rearrange("p (i c) -> p i c", i=3))
                                nc.vector.tensor_copy(vec[:, :, 0:NS], a[:, C:352].rearrange("p (i c) -> p i c", i=3))
                                if one_l:
                                    def blk(k, j):
                                        c0 = 352 + 96 * k + NV * j
                                        return a[:, c0:c0 + NV]
                                    nc.vector.tensor_tensor(tmp[slot][:], blk(0, 0), blk(1, 1), ALU.add).then_inc(t_summed, 1)
                                    nc.vector.tensor_tensor(vec[:, 0, 96:128], blk(2, 1), blk(1, 0), ALU.subtract)
                                    nc.vector.tensor_tensor(vec[:, 1, 96:128], blk(0, 2), blk(2, 0), ALU.subtract)
                                    nc.vector.tensor_tensor(vec[:, 2, 96:128], blk(1, 2), blk(0, 1), ALU.subtract)
                                    dve.wait_ge(t_summed, t_ + 1)
                                    nc.vector.tensor_tensor(s_[:, NS:96], tmp[slot][:], blk(2, 2), ALU.add).then_inc(staged, 1)
                                else:
                                    nc.vector.tensor_tensor(tmp[slot][:], a[:, 352:384], a[:, 384:416], ALU.add).then_inc(t_summed, 1)
                                    dve.wait_ge(t_summed, t_ + 1)
                                    nc.vector.tensor_tensor(s_[:, NS:96], tmp[slot][:], a[:, 416:448], ALU.add).then_inc(staged, 1)

                            def body(t_, slot, turn):
                                if not (isinstance(t_, int) and t_ == NT - 1):
                                    stage(t_ + 1, 1 - slot)
                                dve.wait_ge(mapped, t_ + 1)
                                s_ = one(sconn[:, ds(t_, 1), :])
                                if one_l:
                                    nc.vector.scalar_tensor_tensor(s_, pO[slot][:, 0:192], attr[:, ds(t_, 1)], s_, ALU.mult, ALU.add).then_inc(taken, 1)
                                else:
                                    coef = factor[:, 1, ds(t_, 1)]
                                    nc.vector.tensor_scalar(factor[:, 2, ds(t_, 1)], pO[slot][:, 0:1], coef, coef, ALU.mult, ALU.mult).then_inc(acted, 1)
                                    dve.wait_ge(acted, t_ + 1)
                                    nc.vector.scalar_tensor_tensor(s_, pO[slot][:, 1:161], factor[:, 2, ds(t_, 1)], s_, ALU.mult, ALU.add).then_inc(taken, 1)

                            if not one_l:
                                nc.vector.tensor_scalar(factor[:, 0, :].unsqueeze(2), acc[:, :, MW - 1:MW], 1.0, None, ALU.max).then_inc(f_step, 1)
                                dve.wait_ge(f_step, 1)
                                nc.vector.reciprocal(factor[:, 0, :], factor[:, 0, :]).then_inc(f_step, 1)
                                dve.wait_ge(f_step, 2)
                                nc.vector.tensor_tensor(factor[:, 1, :], factor[:, 0, :], attr[:], ALU.mult).then_inc(f_step, 1)
                                dve.wait_ge(f_step, 3)
                            stage(0, 0)
                            steps(dve, NT, 2, body, tail=1)
                            dve.wait_ge(taken, NT)
                            if one_l:
                                dve.wait_ge(gated, 1)
                                g_ = gates[:, :, NS:96].unsqueeze(2).broadcast_to([P, NT, 3, NV])
                                v_ = sconn[:, :, 96:192].rearrange("p t (i c) -> p t i c", i=3)
                                nc.vector.tensor_tensor(v_, g_, v_, ALU.mult).then_inc(y_step, 1)
                                dve.wait_ge(y_step, 1)
                                scal, v0 = gates[:, :, 0:NS], 96
                            else:
                                scal, v0 = sconn[:, :, 0:NS], NS
                            nc.vector.tensor_tensor(x[:, :, OS:OS + NS], x[:, :, OS:OS + NS], scal, ALU.add)
                            for i in range(3):
                                o = x[:, :, OV[i]:OV[i] + NV]
                                nc.vector.tensor_tensor(o, o, sconn[:, :, v0 + NV * i:v0 + NV * (i + 1)], ALU.add)

                        @block.tensor
                        def _(pe):
                            def transposes(t_, slot):
                                pe.wait_ge(staged, t_ + 1)
                                wait(pe, tcopied, t_ - 1)
                                nc.tensor.transpose(pT[slot][0:96, 0, :], sg[slot][:, 0:96], ident[:])
                                for i in range(3):
                                    last = nc.tensor.transpose(pT[slot][0:KV, 1 + i, :], sg[slot][:, 96 + KV * i:96 + KV * (i + 1)], ident[:])
                                last.then_inc(transposed, 1)

                            def body(t_, slot, turn):
                                if not (isinstance(t_, int) and t_ == NT - 1):
                                    transposes(t_ + 1, 1 - slot)
                                pe.wait_ge(tcopied, t_ + 1)
                                wait(pe, taken, t_ - 1)
                                nc.tensor.matmul(pO[slot][:, 0:NO], sT[slot][0:96, 0, :], wos[:], start=True, stop=False, skip_group_check=True)
                                for i in range(3):
                                    last = nc.tensor.matmul(pO[slot][:, NO + NV * i:NO + NV * (i + 1)], sT[slot][0:KV, 1 + i, :], wov[:], start=False, stop=(i == 2), skip_group_check=True)
                                last.then_inc(mapped, 1)
                            transposes(0, 0)
                            steps(pe, NT, 2, body, tail=1)

                        @block.scalar
                        def _(act):
                            def body(t_, slot, turn):
                                act.wait_ge(transposed, t_ + 1)
                                wait(act, mapped, t_ - 1)
                                nc.scalar.copy(sT[slot][0:96, 0, :], pT[slot][0:96, 0, :])
                                nc.scalar.copy(sT[slot][0:KV, 1:4, :], pT[slot][0:KV, 1:4, :]).then_inc(tcopied, 1)
                            steps(act, NT, 2, body)
                            if one_l:
                                act.wait_ge(taken, NT)
                                nc.scalar.activation(gates[:, :, 0:NS], sconn[:, :, 0:NS], ACT.Silu)
                                nc.scalar.activation(gates[:, :, NS:96], sconn[:, :, NS:96], ACT.Sigmoid).then_inc(gated, 1)

        inv = lambda d: float(1.0 / np.sqrt(np.float64(d)))
        r3, r32 = inv(3), inv(NV)
        p0, p3 = "L0_gnn_", "L3_gnn_"
        flat = lambda ap: ap.rearrange("u o w -> (u o) w")
        product_layer(
            0, t["x"], "d",
            {"lm_s": t[p0 + "Lm_s"], "wm_ss": t[p0 + "Wm_ss"], "wm_vv": t[p0 + "Wm_vv"], "wm_sv": t[p0 + "Wm_sv"], "lm_v": t[p0 + "Lm_v"],
             "wm_vs": t[p0 + "Wm_vs"], "lu_s": t[p0 + "Lu_s"], "lu_v": t[p0 + "Lu_v"], "wu_ss": t[p0 + "Wu_ss"], "wu_vv": t[p0 + "Wu_vv"],
             "wu_sv": t[p0 + "Wu_sv"], "wu_vs": t[p0 + "Wu_vs"], "dist": 3, "r": (0, 1, 2)},
            {"lm_s": 1 / 8, "wm_ss": 1 / 8, "wm_vv": r3 * r32, "wm_sv": 1 / 8, "lm_v": r32, "wm_vs": r32, "lu_s": 1 / 8, "lu_v": r32,
             "wu_ss": 1 / 64, "wu_vv": r3 / 32, "wu_sv": inv(2048), "wu_vs": inv(2048)})
        end_stage()
        layernorm(0)

        p1 = "L1_gnn_"
        filter_layer(1, {
            "fc_in": 64, "fc_col": D_E64, "nw": 224, "nsc": 96, "wa": 320, "wb": 320, "no": 96, "kv": 128, "silu_scale": 1 / 8,
            "loads": lambda ws, wv, fc1, fc2, wos, wov: (
                (ws[:, 0:NS], t[p1 + "lin1_ws"]), (ws[:, NS:NS + 96], t[p1 + "sc_ws"]), (wv[:, 0:NV], t[p1 + "lin1_wv"]),
                (wv[:, NV:2 * NV], t[p1 + "sc_wv"]), (fc1[:], t[p1 + "fc_w1"]), (fc2[:], t[p1 + "fc_w2"]),
                (wos[:], t[p1 + "lin2_ws"]), (wov[:], t[p1 + "lin2_wv"])),
            "scale": lambda ws, wv, fc1, fc2, wos, wov: (
                (ws[:], 1 / 8), (wv[:], r32), (fc2[:], 1 / 8), (wos[0:NS, :], inv(96) / 4), (wos[NS:96, :], inv(96) / 4 * r3),
                (wov[0:96, :], inv(128) / 4), (wov[96:128, :], inv(128) / 4 * inv(2)))})
        end_stage()
        layernorm(1)

        p2 = "L2_gnn_"
        filter_layer(2, {
            "fc_in": 16, "fc_col": D_E16, "nw": 192, "nsc": 64, "wa": 449, "wb": 0, "no": 65, "kv": 96, "silu_scale": 1 / 4,
            "loads": lambda ws, wv, fc1, fc2, wos, wov: (
                (ws[:, 0:NS], t[p2 + "Wl1_0"]), (ws[:, NS:2 * NS], t[p2 + "Wsc0"]), (wv[:, 0:NV], t[p2 + "Wl1_1"]),
                (wv[:, NV:2 * NV], t[p2 + "Wsc1"]), (fc1[:], t[p2 + "Wfc1"]), (fc2[:], t[p2 + "Wfc2"]),
                (wos[:, 0:1], t[p2 + "Wa"]), (wos[:, 1:65], t[p2 + "Wl2_s"]), (wov[:], t[p2 + "Wl2_v"])),
            "scale": lambda ws, wv, fc1, fc2, wos, wov: (
                (ws[:], 1 / 8), (wv[:], r32), (fc2[:], 1 / 8), (wos[0:NS, :], inv(96)), (wos[NS:96, :], inv(96) * r3),
                (wov[:], inv(96)))})
        end_stage()
        layernorm(2)

        product_layer(
            3, h_dram, None,
            {"lm_s": t[p3 + "lm0"], "wm_ss": flat(t[p3 + "wm000"]), "wm_vv": flat(t[p3 + "wm110"]), "wm_sv": flat(t[p3 + "wm011"]),
             "lm_v": t[p3 + "lm1"], "wm_vs": flat(t[p3 + "wm101"]), "lu_s": t[p3 + "lu0"], "lu_v": t[p3 + "lu1"], "wu_ss": t[p3 + "wu000"],
             "wu_vv": t[p3 + "wu110"], "wu_sv": t[p3 + "wu011"], "wu_vs": t[p3 + "wu101"], "dist": 3, "r": (0, 1, 2)},
            {"lm_s": 1 / 8, "wm_ss": inv(96), "wm_vv": r3 * inv(96), "wm_sv": inv(96), "lm_v": r32, "wm_vs": inv(96), "lu_s": 1 / 8,
             "lu_v": r32, "wu_ss": inv(5120), "wu_vv": r3 * inv(5120), "wu_sv": 1 / 64, "wu_vs": 1 / 64})
        end_stage()
        layernorm(3, to_output=True)


_INS = ["x", "src", "dst", "edge_attr_16", "edge_attr_4", "edge_attr_64", "node_vec1"]
_INS += ["L0_gnn_" + a for a in ("Wm_ss", "Wm_vv", "Wm_sv", "Wm_vs", "Lm_s", "Lm_v", "Wu_ss", "Wu_vv", "Wu_sv", "Wu_vs", "Lu_s", "Lu_v")]
_INS += ["L1_gnn_" + a for a in ("lin1_ws", "lin1_wv", "fc_w1", "fc_w2", "sc_ws", "sc_wv", "lin2_ws", "lin2_wv")]
_INS += ["L2_gnn_" + a for a in ("Wfc1", "Wfc2", "Wsc0", "Wsc1", "Wl1_0", "Wl1_1", "Wl2_s", "Wl2_v", "Wa")]
_INS += ["L3_gnn_" + a for a in ("wm000", "wm011", "wm101", "wm110", "lm0", "lm1", "wu000", "wu011", "wu101", "wu110", "lu0", "lu1")]


def kernel(**inputs):
    import concourse.bacc as bacc
    from concourse import mybir
    from concourse.bass_utils import run_bass_kernel_spmd

    nc = bacc.Bacc("TRN2", target_bir_lowering=False, num_devices=1)
    arrays, tensors = {}, {}
    cols = permutation()
    for name in _INS:
        a = np.asarray(inputs[name])
        if name == "x":
            a = a[:, cols]
        a = np.ascontiguousarray(a)
        arrays[f"in_{name}"] = a
        tensors[name] = nc.dram_tensor(f"in_{name}", a.shape, mybir.dt.from_np(a.dtype), kind="ExternalInput").ap()
    out = nc.dram_tensor("out_rows", (N, C), mybir.dt.float32, kind="ExternalOutput").ap()
    build(nc, tensors, out)
    got = run_bass_kernel_spmd(nc, [arrays], core_ids=[0]).results[0]["out_rows"]
    back = np.empty_like(cols)
    back[cols] = np.arange(C)
    return got[:, back]
```

```python
import numpy as np

N, E, C = 3125, 50000, 160
P = 128
NS, NV = 64, 32
NT = -(-N // P)
NFULL = N // P
NREST = N - NFULL * P
GROUP = 256
TPG = GROUP // P
NG = (E + NT * (GROUP - 1)) // GROUP
T = NG * TPG
EJ = -(-E // P)
EDUP = P * EJ - E
WS, WD = 6, 86
D_E64, D_E16, D_E4, D_IDX, D_LOC = 0, 64, 80, 84, 85
S_E4, S_IDX, S_LOC = 0, 4, 5
OS = 0
OV = [NS + NV * i for i in range(3)]
BLK = 448
NB = -(-N // BLK)
SLOTS = 4
LEAD = 4
RSLOTS = 8


def permutation():
    cols = list(range(NS)) + [NS + 3 * c + i for i in range(3) for c in range(NV)]
    return np.array(cols)


def build(nc, t, out):
    import concourse.bass as bass
    from concourse import mybir
    from contextlib import ExitStack

    F32, BF16, I32, U32 = mybir.dt.float32, mybir.dt.bfloat16, mybir.dt.int32, mybir.dt.uint32
    ALU = mybir.AluOpType
    ACT = mybir.ActivationFunctionType
    ds = bass.ds

    top = ExitStack()

    def sb(scope, name, shape, dt=F32):
        return scope.enter_context(nc.sbuf_tensor(name, shape, dt))

    def ps(scope, name, shape, dt=F32):
        return scope.enter_context(nc.psum_tensor(name, shape, dt))

    def wait(eng, sem, value):
        if not (isinstance(value, int) and value <= 0):
            eng.wait_ge(sem, value)

    def steps(eng, count, unroll, body, tail=0):
        for i in range(unroll):
            body(i, i, 0)
        turns = (count - tail) // unroll
        with eng.Fori(1, turns) as it:
            for k in range(unroll):
                body(it * unroll + k, k, it)
        for i in range(turns * unroll, count):
            body(i, i % unroll, i // unroll)

    rec_s = nc.dram_tensor("rec_s", (P * T + EJ, WS), F32, kind="Internal").ap()
    rec_d = nc.dram_tensor("rec_d", (P * T + EJ, WD), F32, kind="Internal").ap()
    h_dram = nc.dram_tensor("h_rows", (NT * P, C), F32, kind="Internal").ap()

    with top:
        in_use = []

        def sem(name):
            in_use.append(nc.alloc_semaphore(name))
            return in_use[-1]

        def stand(eng, sem_):
            eng.sem_inc(sem_, 1)

        def end_stage(keep=()):
            nc.clear_and_free_semaphores([a for a in in_use if a not in keep])
            in_use.clear()
            nc.all_engine_barrier()

        x = sb(top, "x", [P, NT, C])
        attr = sb(top, "attr", [P, NT])
        iota = sb(top, "iota", [P, P])
        ident = sb(top, "ident", [P, P])
        identb = sb(top, "identb", [P, P], BF16)
        sel2 = sb(top, "sel2", [96, 16, P], BF16)
        sel4 = sb(top, "sel4", [96, 8, P], BF16)
        gtile = {"s": sb(top, "gtile_s", [1, NG], I32), "d": sb(top, "gtile_d", [1, NG], I32)}
        loc = {"d": sb(top, "loc_d", [P, EJ])}
        pos = {"d": sb(top, "pos_d", [P, EJ], I32)}
        key_i = {"s": sb(top, "key_s", [P, EJ], I32)}
        nidx = sb(top, "nidx", [P, 1])
        k31 = sb(top, "k31", [P, 1])
        pidx_i = sb(top, "pidx_i", [P, 2], I32)
        eye2 = sb(top, "eye2", [P, NS])
        early = ExitStack()
        loc["s"] = sb(early, "loc_s", [P, EJ])
        pos["s"] = sb(early, "pos_s", [P, EJ], I32)
        key_i["d"] = sb(early, "key_d", [P, EJ], I32)
        bval = sb(early, "bval", [P, NT + 1])
        tri = sb(early, "tri", [P, P])
        ones_sq = sb(early, "ones_sq", [P, P])

        def order_parts(k, sc):
            n = f"_{k}"
            key2 = sb(sc, "key2" + n, [P, EJ], I32)
            part_i = sb(sc, "part_i" + n, [P, EJ], I32)
            kt = sb(sc, "kt" + n, [P, EJ])
            ones = sb(sc, "ones" + n, [P, EJ])
            masks = [sb(sc, f"mask{i}{n}", [P, EJ]) for i in range(2)]
            cums = [sb(sc, f"cum{i}{n}", [P, EJ]) for i in range(2)]
            mask, cum = masks[0], cums[0]
            prod = sb(sc, "prod" + n, [P, EJ])
            q = sb(sc, "q" + n, [P, EJ])
            counts = sb(sc, "counts" + n, [P, NT])
            small = sb(sc, "small" + n, [P, 8, NT])
            small_i = sb(sc, "small_i" + n, [P, 2, NT], I32)
            ramp_g = sb(sc, "ramp_g" + n, [P, EJ], I32)
            ramp_f = sb(sc, "ramp_f" + n, [P, EJ])
            gt = sb(sc, "gt" + n, [1, NG])
            before = ps(sc, "before" + n, [P, NT])
            total = ps(sc, "total" + n, [P, NT])
            keys_marked = sem("keys_marked" + n)
            ramp_ready = sem("ramp_ready" + n)
            counted = sem("counted" + n)
            summed = sem("summed" + n)
            step, group_step = sem("order_step" + n), sem("group_step" + n)
            b_mask, b_cum, b_prod, b_q = (sem(f"{a}{n}") for a in ("b_mask", "b_cum", "b_prod", "b_q"))
            def on_gpsimd(pool):
                pool.wait_ge(keys_in, 64)
                nc.gpsimd.affine_select(out=key2[:], in_=key_i[k][:], compare_op=ALU.is_ge, fill=float(NT * P),
                                        base=(P - 1) * 1000 - EDUP, pattern=[[1, EJ]], channel_multiplier=-1000).then_inc(keys_marked, 1)
                nc.gpsimd.iota(ramp_g[:], [[1, EJ]], base=0, channel_multiplier=0).then_inc(ramp_ready, 1)

            def on_tensor(pe):
                pe.wait_ge(counted, NT)
                nc.tensor.matmul(before[:], tri[:], counts[:], start=True, stop=True).then_inc(summed, 1)
                nc.tensor.matmul(total[:], ones_sq[:], counts[:], start=True, stop=True).then_inc(summed, 1)

            def on_vector(dve):
                done = [0]

                def link(ins):
                    done[0] += 1
                    ins.then_inc(step, 1)
                    dve.wait_ge(step, done[0])

                dve.wait_ge(keys_marked, 1)
                link(nc.vector.tensor_scalar(part_i[:], key2[:], 7, None, ALU.arith_shift_right))
                link(nc.vector.tensor_copy(kt[:], part_i[:]))
                link(nc.vector.tensor_scalar(part_i[:], key2[:], P - 1, None, ALU.bitwise_and))
                link(nc.vector.tensor_copy(loc[k][:], part_i[:]))
                link(nc.vector.memset(ones[:], 1.0))
                link(nc.vector.memset(q[:], 0.0))
                for b in range(NT):
                    wait(dve, counted, b - 1)
                    nc.vector.tensor_scalar(masks[b % 2][:], kt[:], float(b), None, ALU.is_equal, ALU.add,
                                            accum_out=counts[:, b:b + 1]).then_inc(counted, 1)
                dve.wait_ge(counted, NT)
                dve.wait_ge(summed, 2)
                tot, grp, end, base, off = (small[:, i, :] for i in range(5))
                link(nc.vector.tensor_scalar(tot, total[:], float(GROUP - 1), None, ALU.add))
                link(nc.vector.tensor_copy(small_i[:, 0, :], tot))
                link(nc.vector.tensor_scalar(small_i[:, 1, :], small_i[:, 0, :], GROUP.bit_length() - 1, None, ALU.arith_shift_right))
                link(nc.vector.tensor_copy(grp, small_i[:, 1, :]))
                link(nc.vector.tensor_tensor_scan(end, ones[:, 0:NT], grp, 0.0, ALU.mult, ALU.add))
                link(nc.vector.tensor_tensor(base, end, grp, ALU.subtract))
                link(nc.vector.tensor_scalar(base, base, float(GROUP), -1.0, ALU.mult, ALU.add))
                link(nc.vector.tensor_tensor(off, before[:], base, ALU.add))
                def mark(b, slot):
                    wait(dve, b_cum, b - 1)
                    wait(dve, b_prod, b - 1)
                    nc.vector.tensor_scalar(masks[slot][:], kt[:], bval[:, ds(b, 1)], None, ALU.is_equal).then_inc(b_mask, 1)

                def count(b, slot):
                    dve.wait_ge(b_mask, b + 1)
                    nc.vector.tensor_tensor_scan(cums[slot][:], ones[:], masks[slot][:], small[:, 4, ds(b, 1)], ALU.mult, ALU.add).then_inc(b_cum, 1)

                def body(b, slot, turn):
                    more = not (isinstance(b, int) and b == NT - 1)
                    if more:
                        mark(b + 1, (slot + 1) % 2)
                    dve.wait_ge(b_cum, b + 1)
                    wait(dve, b_q, b)
                    nc.vector.tensor_tensor(prod[:], masks[slot % 2][:], cums[slot % 2][:], ALU.mult).then_inc(b_prod, 1)
                    if more:
                        count(b + 1, (slot + 1) % 2)
                    dve.wait_ge(b_prod, b + 1)
                    nc.vector.tensor_tensor(q[:], q[:], prod[:], ALU.add).then_inc(b_q, 1)
                mark(0, 0)
                count(0, 0)
                steps(dve, NT, 6, body, tail=1)
                dve.wait_ge(b_q, NT)
                dve.wait_ge(ramp_ready, 1)
                link(nc.vector.tensor_copy(pos[k][:], q[:]))
                link(nc.vector.tensor_scalar(part_i[:], pos[k][:], P - 1, None, ALU.bitwise_and))
                link(nc.vector.tensor_copy(mask[:], part_i[:]))
                link(nc.vector.tensor_scalar(part_i[:], pos[k][:], 7, None, ALU.arith_shift_right))
                link(nc.vector.tensor_copy(cum[:], part_i[:]))
                link(nc.vector.scalar_tensor_tensor(q[:], mask[:], float(T), cum[:], ALU.mult, ALU.add))
                link(nc.vector.tensor_copy(ramp_f[:], ramp_g[:]))
                link(nc.vector.tensor_scalar(mask[:], kt[:], float(NT), None, ALU.is_equal))
                link(nc.vector.scalar_tensor_tensor(prod[:], ramp_f[:], float(P * T), mask[:], ALU.add, ALU.mult))
                link(nc.vector.tensor_tensor(q[:], q[:], prod[:], ALU.add))
                link(nc.vector.tensor_copy(pos[k][:], q[:]))

            def groups_on_vector(dve):
                done = [0]

                def link(ins):
                    done[0] += 1
                    ins.then_inc(group_step, 1)
                    dve.wait_ge(group_step, done[0])

                end = small[:, 2, :]
                link(nc.vector.memset(gt[:], 0.0))
                for b in range(NT - 1):
                    link(nc.vector.scalar_tensor_tensor(gt[:], ramp_f[0:1, 0:NG], end[0:1, b:b + 1], gt[:], ALU.is_ge, ALU.add))
                link(nc.vector.tensor_copy(gtile[k][:], gt[:]))
            return on_gpsimd, on_tensor, on_vector, groups_on_vector

        def scatter_parts(k, sc):
            rec, words = (rec_s, WS) if k == "s" else (rec_d, WD)
            c_idx, c_loc, c_e4 = (S_IDX, S_LOC, S_E4) if k == "s" else (D_IDX, D_LOC, D_E4)
            other = key_i["d" if k == "s" else "s"]
            halves = (12, 11)
            per = sum(halves)
            turns = EJ // per
            pieces = [("edge_attr_4", c_e4, 4)]
            if k == "d":
                pieces += [("edge_attr_64", D_E64, 64), ("edge_attr_16", D_E16, 16)]
            stage = [sb(sc, f"stage{h}_{k}", [P, halves[h], words]) for h in range(2)]
            place = [sb(sc, f"place{h}_{k}", [P, halves[h]], I32) for h in range(2)]
            loaded = [sem(f"loaded{h}_{k}") for h in range(2)]
            filled = [sem(f"filled{h}_{k}") for h in range(2)]
            sent = [sem(f"sent{h}_{k}") for h in range(2)]
            issued, turn_begun = sem(f"scatter_turn_{k}"), sem(f"turn_begun_{k}")
            def on_sync(sp):
                def turn(i, h):
                    wait(sp, sent[h], i * (16 * halves[h]))
                    j0 = i * per + (halves[0] if h else 0)
                    for name, col, w in pieces:
                        src = t[name]
                        body = src[0:(P - 1) * EJ, :].rearrange("(p j) w -> p j w", j=EJ)
                        last = src[E - EJ:E, :].rearrange("(p j) w -> p j w", j=EJ)
                        sp.dma_start(stage[h][0:P - 1, :, col:col + w], body[:, ds(j0, halves[h]), :]).then_inc(loaded[h], 16)
                        sp.dma_start(stage[h][P - 1:P, :, col:col + w], last[:, ds(j0, halves[h]), :]).then_inc(loaded[h], 16)
                for h in range(2):
                    turn(0, h)
                with sp.Fori(1, turns) as i:
                    for h in range(2):
                        turn(i, h)

            def on_gpsimd(pool):
                def turn(i, h):
                    m = halves[h]
                    j0 = i * per + (halves[0] if h else 0)
                    pool.wait_ge(loaded[h], (i + 1) * (32 * len(pieces)))
                    wait(pool, sent[h], i * (16 * m))
                    stand(pool, turn_begun)
                    nc.gpsimd.tensor_copy(stage[h][:, :, c_idx:c_idx + 1].bitcast(I32).rearrange("p m o -> p (m o)"), other[:, ds(j0, m)]).then_inc(filled[h], 1)
                    nc.gpsimd.tensor_copy(stage[h][:, :, c_loc:c_loc + 1].rearrange("p m o -> p (m o)"), loc[k][:, ds(j0, m)]).then_inc(filled[h], 1)
                    nc.gpsimd.tensor_copy(place[h][:], pos[k][:, ds(j0, m)]).then_inc(filled[h], 1)
                    pool.wait_ge(filled[h], (i + 1) * 3)
                    stand(pool, issued)
                    for c in range(m):
                        pool.indirect_dma_start(rec, bass.IndirectOffsetOnAxis(place[h][:, c:c + 1].bitcast(U32), 0),
                                                stage[h][:, c, :], None).then_inc(sent[h], 16)
                for h in range(2):
                    turn(0, h)
                with pool.Fori(1, turns) as i:
                    for h in range(2):
                        turn(i, h)
                for h in range(2):
                    pool.wait_ge(sent[h], 16 * halves[h] * turns)
            return on_sync, on_gpsimd

        keys_in = sem("keys_in")
        with ExitStack() as sc:
            ramp_i = sb(early, "ramp_i", [P, P], I32)
            empty_s = sb(early, "empty_s", [P, T, WS])
            EMPTY = 22
            empty_d = sb(early, "empty_d", [P, EMPTY, WD])
            sel2_i = sb(early, "sel2_i", [96, 16 * P], I32)
            sel4_i = sb(early, "sel4_i", [96, 8 * P], I32)
            const_ints = sem("const_ints")
            empties = sem("empties")
            empty_zero = sem("empty_zero")
            loads = sem("loads")
            cleared = sem("cleared")
            sel_ints = sem("sel_ints")
            written, written_d = sem("empty_written_s"), sem("empty_written_d")
            dve_step = sem("const_step")
            order_pool, order_pe, order_dve, groups_s = order_parts("s", early)
            with nc.Block() as block:
                @block.gpsimd
                def _(pool):
                    nc.gpsimd.iota(ramp_i[:], [[1, P]], base=0, channel_multiplier=0).then_inc(const_ints, 1)
                    nc.gpsimd.iota(pidx_i[:, 0:1], [[1, 1]], base=0, channel_multiplier=1).then_inc(const_ints, 1)
                    order_pool(pool)
                    nc.gpsimd.memset(empty_s[:], 0.0).then_inc(empty_zero, 1)
                    nc.gpsimd.memset(empty_d[:], 0.0).then_inc(empty_zero, 1)
                    pool.wait_ge(empty_zero, 2)
                    nc.gpsimd.memset(empty_s[:, :, S_LOC:S_LOC + 1], -1.0).then_inc(empties, 1)
                    nc.gpsimd.memset(empty_d[:, :, D_LOC:D_LOC + 1], -1.0).then_inc(empties, 1)
                    nc.gpsimd.iota(sel2_i[:], [[2, 16], [1, 2], [0, 64]], base=0, channel_multiplier=0).then_inc(sel_ints, 1)
                    nc.gpsimd.iota(sel4_i[:], [[4, 8], [1, 4], [0, 32]], base=0, channel_multiplier=0).then_inc(sel_ints, 1)

                @block.tensor
                def _(pe):
                    order_pe(pe)

                @block.sync
                def _(sp):
                    n = 0
                    for k in "sd":
                        src = t["src" if k == "s" else "dst"]
                        sp.dma_start(key_i[k][0:P - 1, :], src[0:(P - 1) * EJ].rearrange("(p j) -> p j", j=EJ)).then_inc(keys_in, 16)
                        sp.dma_start(key_i[k][P - 1:P, :], src[E - EJ:E].rearrange("(p j) -> p j", j=EJ)).then_inc(keys_in, 16)
                    sp.wait_ge(cleared, 2)
                    sp.dma_start(x[:, 0:NFULL, :], t["x"][0:NFULL * P, :].rearrange("(t p) c -> p t c", p=P)).then_inc(loads, 16)
                    sp.dma_start(x[0:NREST, NFULL, :], t["x"][NFULL * P:N, :]).then_inc(loads, 16)
                    with nc.allow_non_contiguous_dma(reason="one word a node"):
                        sp.dma_start(attr[:, 0:NFULL], t["node_vec1"][0:NFULL * P, :].rearrange("(t p) o -> p (t o)", p=P)).then_inc(loads, 16)
                    sp.dma_start(attr[0:NREST, NFULL:NT], t["node_vec1"][NFULL * P:N, :]).then_inc(loads, 16)
                    n += 64
                    sp.wait_ge(empties, 2)
                    sp.dma_start(rec_s[0:P * T, :].rearrange("(p t) w -> p (t w)", t=T), empty_s[:].rearrange("p t w -> p (t w)")).then_inc(written, 16)
                    for i in range(T // EMPTY):
                        sp.dma_start(rec_d[0:P * T, :].rearrange("(p t) w -> p t w", t=T)[:, i * EMPTY:(i + 1) * EMPTY, :],
                                     empty_d[:]).then_inc(written_d, 16)
                    sp.wait_ge(written, 16)
                    sp.wait_ge(loads, n)

                @block.vector
                def _(dve):
                    done = [0]

                    def link(ins):
                        done[0] += 1
                        ins.then_inc(dve_step, 1)
                        dve.wait_ge(dve_step, done[0])

                    nc.vector.memset(x[:, NFULL, :], 0.0).then_inc(cleared, 1)
                    nc.vector.memset(attr[:, NFULL:NT], 0.0).then_inc(cleared, 1)
                    link(nc.vector.memset(ones_sq[:], 1.0))
                    dve.wait_ge(const_ints, 2)
                    link(nc.vector.tensor_copy(iota[:], ramp_i[:]))
                    link(nc.vector.tensor_copy(bval[:], iota[:, 0:NT + 1]))
                    link(nc.vector.tensor_copy(nidx[:], pidx_i[:, 0:1]))
                    link(nc.vector.tensor_scalar(tri[:], iota[:], nidx[:, 0:1], None, ALU.is_gt))
                    order_dve(dve)

        with ExitStack() as sc:
            order_pool, order_pe, order_dve, groups_d = order_parts("d", sc)
            late_step = sem("const_step_late")
            scatter_sp, scatter_pool = scatter_parts("s", sc)
            with nc.Block() as block:
                @block.sync
                def _(sp):
                    scatter_sp(sp)
                    sp.wait_ge(written_d, 16 * (T // EMPTY))

                @block.gpsimd
                def _(pool):
                    order_pool(pool)
                    scatter_pool(pool)

                @block.tensor
                def _(pe):
                    order_pe(pe)

                @block.vector
                def _(dve):
                    done = [0]

                    def link(ins):
                        done[0] += 1
                        ins.then_inc(late_step, 1)
                        dve.wait_ge(late_step, done[0])

                    groups_s(dve)
                    order_dve(dve)
                    groups_d(dve)
                    link(nc.vector.tensor_scalar(pidx_i[:, 1:2], pidx_i[:, 0:1], 31, None, ALU.bitwise_and))
                    link(nc.vector.tensor_copy(k31[:], pidx_i[:, 1:2]))
                    link(nc.vector.tensor_scalar(ident[:], iota[:], nidx[:, 0:1], None, ALU.is_equal))
                    link(nc.vector.tensor_copy(identb[:], ident[:]))
                    dve.wait_ge(sel_ints, 2)
                    link(nc.vector.tensor_scalar(sel2[:].rearrange("k c p -> k (c p)"), sel2_i[:], k31[0:96, 0:1], None, ALU.is_equal))
                    link(nc.vector.tensor_scalar(sel4[:].rearrange("k c p -> k (c p)"), sel4_i[:], k31[0:96, 0:1], None, ALU.is_equal))
                    link(nc.vector.tensor_tensor(eye2[:], ident[:, 0:NS], ident[:, NS:P], ALU.add))
        early.close()
        end_stage()

        def node_rows(dram):
            return dram.rearrange("(t p) c -> p t c", p=P)

        def one(ap):
            return ap.rearrange("p o c -> p (o c)")

        def layernorm(n, to_output=False, gathered=False, clear=None):
            with ExitStack() as sc:
                stats = sb(sc, f"stats_{n}", [P, NT, 6])
                mv = sb(sc, f"mv_{n}", [P, NT, 2])
                rstd = sb(sc, f"rstd_{n}", [P, NT])
                stats_ready, mv_ready, eps_added = sem(f"stats_ready_{n}"), sem(f"mv_ready_{n}"), sem(f"eps_added_{n}")
                rooted, inverted, normed = sem(f"rooted_{n}"), sem(f"inverted_{n}"), sem(f"normed_{n}")
                x_out, cleared_beside = sem(f"x_out_{n}"), sem(f"cleared_beside_{n}")
                with nc.Block() as block:
                    @block.vector
                    def _(dve):
                        def tile_stats(nt, slot, turn):
                            nc.vector.bn_stats(one(stats[:, ds(nt, 1), :]), one(x[:, ds(nt, 1), :])).then_inc(stats_ready, 1)
                        steps(dve, NT, 6, tile_stats)
                        dve.wait_ge(stats_ready, NT)
                        for nt in range(NT):
                            nc.vector.bn_aggr(mv[:, nt, :], stats[:, nt, :]).then_inc(mv_ready, 1)
                        dve.wait_ge(mv_ready, NT)
                        nc.vector.tensor_scalar(rstd[:].unsqueeze(2), mv[:, :, 1:2], 1e-5, None, ALU.add).then_inc(eps_added, 1)
                        dve.wait_ge(rooted, 1)
                        nc.vector.reciprocal(rstd[:], rstd[:]).then_inc(inverted, 1)
                        dve.wait_ge(inverted, 1)
                        for nt in range(NT):
                            nc.vector.tensor_scalar(x[:, nt, :], x[:, nt, :], mv[:, nt, 0:1], rstd[:, nt:nt + 1],
                                                    ALU.subtract, ALU.mult).then_inc(normed, 1)

                    if clear is not None:
                        @block.gpsimd
                        def _(pool):
                            nc.gpsimd.memset(clear, 0.0).then_inc(cleared_beside, 1)
                            pool.wait_ge(cleared_beside, 1)

                    @block.scalar
                    def _(act):
                        act.wait_ge(eps_added, 1)
                        nc.scalar.activation(rstd[:], rstd[:], ACT.Sqrt).then_inc(rooted, 1)

                    @block.sync
                    def _(sp):
                        sp.wait_ge(normed, NT)
                        if to_output:
                            sp.dma_start(node_rows(out[0:NFULL * P, :]), x[:, 0:NFULL, :]).then_inc(x_out, 16)
                            sp.dma_start(out[NFULL * P:N, :], x[0:NREST, NFULL, :]).then_inc(x_out, 16)
                            sp.wait_ge(x_out, 32)
                        elif gathered:
                            sp.dma_start(node_rows(h_dram), x[:]).then_inc(x_out, 16)
                            sp.wait_ge(x_out, 16)

        A_D, A_RS, A_RV, A_W = C, 2 * C, 2 * C + 3 * NS, 2 * C + 3 * NS + 3 * NV

        def product_layer(n, rows, scatter_beside, w, scales, before=None):
            rec = rec_s[0:P * T, :].rearrange("(p t) w -> p t w", t=T)
            layer = ExitStack()
            with layer:
                raw0 = sb(layer, f"raw0_{n}", [P, NS])
                rawt = sb(layer, f"rawt_{n}", [P, NS])
                raw1 = sb(layer, f"raw1_{n}", [P, NV])
                w0 = sb(layer, f"w0_{n}", [P, 2, NS])
                wt = sb(layer, f"wt_{n}", [P, 2, NS])
                w1 = sb(layer, f"w1_{n}", [P, 4, NV])
                wss = sb(layer, f"wss_{n}", [P, 32, NS])
                wvv = sb(layer, f"wvv_{n}", [P, 8, NS])
                wsv = sb(layer, f"wsv_{n}", [P, 16, NV])
                wvs = sb(layer, f"wvs_{n}", [P, 16, NV])
                lu = sb(layer, f"lu_{n}", [P, C])
                aT = sb(layer, f"aT_{n}", [P, 4, NT * P])
                xpT = sb(layer, f"xpT_{n}", [96, 5, NT * P], BF16)
                w_in, w_scaled = sem(f"weights_in_{n}"), sem(f"weights_scaled_{n}")

                sums_scope = ExitStack()
                with sums_scope:
                    acc = sb(sums_scope, f"acc_{n}", [P, NT, A_W])
                    if before:
                        before(acc[:])

                    with ExitStack() as sc:
                        recb = [sb(sc, f"recb{i}_{n}", [P, TPG, WS]) for i in range(RSLOTS)]
                        rowb = [sb(sc, f"rowb{i}_{n}", [P, TPG, C]) for i in range(RSLOTS)]
                        spare = aT[:].rearrange("p i q -> p (i q)")
                        w_oh, w_msg = TPG * P, TPG * (A_W - C)
                        oh = [spare[:, i * w_oh:(i + 1) * w_oh].rearrange("p (k q) -> p k q", k=TPG) for i in range(SLOTS)]
                        spare = spare[:, SLOTS * w_oh:SLOTS * (w_oh + w_msg)]
                        msg = [spare[:, i * w_msg:(i + 1) * w_msg].rearrange("p (k q) -> p k q", k=TPG) for i in range(SLOTS)]
                        psa = [ps(sc, f"psa{i}_{n}", [P, 512]) for i in range(2)]
                        psb = [ps(sc, f"psb{i}_{n}", [P, 512]) for i in range(2)]
                        rec_in = [sem(f"rec_in{i}_{n}") for i in range(RSLOTS)]
                        rows_in = [sem(f"rows_in{i}_{n}") for i in range(RSLOTS)]
                        acc_zero, msg_ready, dist_ready, agg_done, evac_done = (sem(f"{a}_{n}") for a in (
                            "acc_zero", "msg_ready", "dist_ready", "agg_done", "evac_done"))
                        gather_turn, blocks_zero = sem(f"gather_turn_{n}"), sem(f"blocks_zero_{n}")
                        with nc.Block() as block:
                            @block.sync
                            def _(sp):
                                nw = 0
                                sp.wait_ge(blocks_zero, 2)
                                for dst, src in (
                                        (raw0[0:64, :], w["lm_s"]), (raw0[64:128, :], w["wm_ss"]), (rawt[0:32, :], w["wm_vv"]),
                                        (rawt[32:64, :], w["wm_vv"]), (rawt[64:96, :], w["wm_vv"]),
                                        (raw1[0:64, :], w["wm_sv"]), (raw1[64:96, :], w["lm_v"]), (raw1[96:128, :], w["wm_vs"]),
                                        (lu[0:64, 0:64], w["lu_s"]), (lu[64:96, 64:96], w["lu_v"]),
                                        (lu[96:128, 96:128], w["lu_v"]), (lu[96:128, 128:160], w["lu_v"]),
                                        (wss[:], w["wu_ss"].rearrange("u v w -> (u v) w").rearrange("(c p) w -> p c w", p=P)),
                                        (wvv[:], w["wu_vv"].rearrange("u v w -> (u v) w").rearrange("(c p) w -> p c w", p=P)),
                                        (wsv[:], w["wu_sv"].rearrange("u v w -> (u v) w").rearrange("(c p) w -> p c w", p=P)),
                                        (wvs[:], w["wu_vs"].rearrange("u v w -> (u v) w").rearrange("(c p) w -> p c w", p=P))):
                                    sp.dma_start(dst, src).then_inc(w_in, 16)
                                    nw += 16

                                def body(g, slot, turn):
                                    wait(sp, agg_done, g - (RSLOTS - 1))
                                    sp.dma_start(recb[slot][:], rec[:, ds(TPG * g, TPG), :]).then_inc(rec_in[slot], 16)
                                steps(sp, NG, RSLOTS, body)

                            @block.gpsimd
                            def _(pool):
                                def body(g, slot, turn):
                                    pool.wait_ge(rec_in[slot], (turn + 1) * 16)
                                    wait(pool, agg_done, g - (RSLOTS - 1))
                                    stand(pool, gather_turn)
                                    for k in range(TPG):
                                        pool.indirect_dma_start(rowb[slot][:, k, :], None, rows,
                                                                bass.IndirectOffsetOnAxis(recb[slot][:, k, S_IDX:S_IDX + 1].bitcast(U32), 0)).then_inc(rows_in[slot], 16)
                                steps(pool, NG, RSLOTS, body)

                            @block.scalar
                            def _(act):
                                def body(g, slot, turn):
                                    act.wait_ge(rows_in[slot], (turn + 1) * (16 * TPG))
                                    wait(act, agg_done, g - (SLOTS - 1))
                                    for k in range(TPG):
                                        last = nc.scalar.activation(msg[slot % SLOTS][:, k, 0:C], rowb[slot][:, k, :], ACT.Copy,
                                                                    scale=recb[slot][:, k, S_E4 + 3:S_E4 + 4])
                                    last.then_inc(dist_ready, 1)
                                steps(act, NG, RSLOTS, body)
                                act.wait_ge(w_in, 16 * 16)
                                for r in range(2):
                                    nc.scalar.mul(w0[0:64, r, :], raw0[0:64, :], scales["lm_s"])
                                    nc.scalar.mul(w0[64:128, r, :], raw0[64:128, :], scales["wm_ss"])
                                    nc.scalar.mul(wt[:, r, :], rawt[:], scales["wm_vv"])
                                for r in range(4):
                                    nc.scalar.mul(w1[0:64, r, :], raw1[0:64, :], scales["wm_sv"])
                                    nc.scalar.mul(w1[64:96, r, :], raw1[64:96, :], scales["lm_v"])
                                    nc.scalar.mul(w1[96:128, r, :], raw1[96:128, :], scales["wm_vs"])
                                for a, f in ((wss, "wu_ss"), (wvv, "wu_vv"), (wsv, "wu_sv"), (wvs, "wu_vs")):
                                    nc.scalar.mul(a[:], a[:], scales[f])
                                nc.scalar.mul(lu[0:64, :], lu[0:64, :], scales["lu_s"])
                                nc.scalar.mul(lu[64:128, :], lu[64:128, :], scales["lu_v"]).then_inc(w_scaled, 1)

                            @block.vector
                            def _(dve):
                                def build(g, slot, turn):
                                    dve.wait_ge(rec_in[slot], (turn + 1) * 16)
                                    wait(dve, agg_done, g - (SLOTS - 1))
                                    rb, row, m = recb[slot], rowb[slot], msg[slot % SLOTS]
                                    nc.vector.tensor_tensor(oh[slot % SLOTS], iota[:].unsqueeze(1).broadcast_to([P, TPG, P]),
                                                            rb[:, :, S_LOC:S_LOC + 1].broadcast_to([P, TPG, P]), ALU.is_equal)
                                    dve.wait_ge(rows_in[slot], (turn + 1) * (16 * TPG))
                                    r = rb[:, :, S_E4:S_E4 + 3].unsqueeze(3)
                                    nc.vector.tensor_tensor(m[:, :, A_RS - C:A_RV - C].rearrange("p k (i c) -> p k i c", i=3),
                                                            row[:, :, 0:NS].unsqueeze(2).broadcast_to([P, TPG, 3, NS]),
                                                            r.broadcast_to([P, TPG, 3, NS]), ALU.mult)
                                    nc.vector.tensor_tensor(m[:, :, A_RV - C:A_W - C].rearrange("p k (i c) -> p k i c", i=3),
                                                            row[:, :, NS:C].rearrange("p k (i c) -> p k i c", i=3),
                                                            r.broadcast_to([P, TPG, 3, NV]), ALU.mult).then_inc(msg_ready, 1)

                                def body(g, slot, turn):
                                    tile = dve.value_load(gtile["s"][0:1, ds(g, 1)], min_val=0, max_val=NT - 1)
                                    if not isinstance(g, int) or g + 2 < NG:
                                        build(g + 2, (slot + 2) % RSLOTS, turn + (slot + 2) // RSLOTS)
                                    dve.wait_ge(agg_done, g + 1)
                                    wait(dve, evac_done, g)
                                    a = one(acc[:, ds(tile, 1), :])
                                    nc.vector.tensor_tensor(a[:, 0:C], psa[slot % 2][:, 0:C], a[:, 0:C], ALU.add)
                                    nc.vector.tensor_tensor(a[:, C:A_W], psb[slot % 2][:, 0:A_W - C], a[:, C:A_W], ALU.add).then_inc(evac_done, 1)

                                nc.vector.memset(rawt[:], 0.0).then_inc(blocks_zero, 1)
                                nc.vector.memset(lu[:], 0.0).then_inc(blocks_zero, 1)
                                if not before:
                                    nc.vector.memset(acc[:], 0.0).then_inc(acc_zero, 1)
                                build(0, 0, 0)
                                build(1, 1, 0)
                                if not before:
                                    dve.wait_ge(acc_zero, 1)
                                steps(dve, NG, RSLOTS, body, tail=2)

                            @block.tensor
                            def _(pe):
                                def body(g, slot, turn):
                                    pe.wait_ge(msg_ready, g + 1)
                                    pe.wait_ge(rows_in[slot], (turn + 1) * (16 * TPG))
                                    wait(pe, evac_done, g - 1)
                                    b = slot % 2
                                    for k in range(TPG):
                                        nc.tensor.matmul(psa[b][:, 0:C], oh[slot % SLOTS][:, k, :], rowb[slot][:, k, :], start=(k == 0), stop=(k == TPG - 1))
                                    pe.wait_ge(dist_ready, g + 1)
                                    for k in range(TPG):
                                        last = nc.tensor.matmul(psb[b][:, 0:A_W - C], oh[slot % SLOTS][:, k, :], msg[slot % SLOTS][:, k, :], start=(k == 0), stop=(k == TPG - 1))
                                    last.then_inc(agg_done, 1)
                                steps(pe, NG, RSLOTS, body)

                    with ExitStack() as sc:
                        AHEAD = 3
                        stg = [sb(sc, f"stg{i}_{n}", [P, 5 * P]) for i in range(AHEAD)]
                        xst = [sb(sc, f"xst{i}_{n}", [P, C]) for i in range(AHEAD)]
                        xsp = [sb(sc, f"xsp{i}_{n}", [P, 5, 3, NV], BF16) for i in range(AHEAD)]
                        rest1 = [sb(sc, f"rest1_{i}_{n}", [P, C]) for i in range(AHEAD)]
                        rest2 = sb(sc, f"rest2_{n}", [P, C])
                        cT = [sb(sc, f"cT{i}_{n}", [P, 512]) for i in range(2)]
                        rxT = [sb(sc, f"rxT{i}_{n}", [P, 2 * P]) for i in range(2)]
                        ps_c = [ps(sc, f"ps_c{i}_{n}", [P, 512]) for i in range(2)]
                        ps_r = [ps(sc, f"ps_r{i}_{n}", [P, 512]) for i in range(2)]
                        ps_x = [ps(sc, f"ps_x{i}_{n}", [P, 1024], BF16) for i in range(2)]
                        ps_a = ps(sc, f"ps_a_{n}", [P, 4, P])
                        ps_d = ps(sc, f"ps_d_{n}", [P, 512])
                        (staged, split, split_a, split_b, split_c, split_d, split_turn, turned, sums_copied, x_copied, a_done, a_copied, x_done) = (
                            sem(f"{a}_{n}") for a in ("staged", "split", "split_a", "split_b", "split_c", "split_d", "split_turn",
                                                      "turned", "sums_copied", "x_copied", "a_done", "a_copied", "x_done"))
                        with nc.Block() as block:
                            @block.scalar
                            def _(act):
                                def stage(t_, slot):
                                    slot = slot % AHEAD
                                    wait(act, turned, t_ - (AHEAD - 1))
                                    wait(act, split, t_ - (AHEAD - 1))
                                    a = one(acc[:, ds(t_, 1), :])
                                    pair = a[:, 0:2 * C].rearrange("p (a c) -> p a c", a=2)
                                    row = one(x[:, ds(t_, 1), :])
                                    nc.scalar.copy(xst[slot][:], row)
                                    nc.scalar.copy(stg[slot][:, 0:P].rearrange("p (a c) -> p a c", a=2), pair[:, :, 0:NS])
                                    vec = stg[slot][:, P:4 * P].rearrange("p (i c) -> p i c", i=3)
                                    nc.scalar.copy(vec[:, :, 0:NS], a[:, A_RS:A_RV].rearrange("p (i c) -> p i c", i=3))
                                    for k in range(2):
                                        nc.scalar.copy(vec[:, :, NS + NV * k:NS + NV * (k + 1)], pair[:, k, NS:C].rearrange("p (i c) -> p i c", i=3))
                                    nc.scalar.copy(stg[slot][:, 4 * P:4 * P + 3 * NV], a[:, A_RV:A_W])
                                    nc.scalar.copy(stg[slot][:, 4 * P + 3 * NV:5 * P], row[:, OV[2]:C]).then_inc(staged, 1)

                                def body(t_, slot, turn):
                                    if not isinstance(t_, int) or t_ + 2 < NT:
                                        stage(t_ + 2, slot + 2)
                                    act.wait_ge(turned, t_ + 1)
                                    nc.scalar.copy(xpT[:, :, ds(t_ * P, P)], ps_x[slot % 2][0:96, 0:5 * P].rearrange("k (g p) -> k g p", g=5)).then_inc(x_copied, 1)
                                stage(0, 0)
                                stage(1, 1)
                                steps(act, NT, 2 * AHEAD, body, tail=2)

                            def by_group(ap):
                                return ap.rearrange("p (g c) -> p g c", g=5)

                            @block.gpsimd
                            def _(pool):
                                def body(t_, slot, turn):
                                    r1, r2, part = by_group(rest1[slot % AHEAD][:]), by_group(rest2[:]), xsp[slot % AHEAD]
                                    pool.wait_ge(split_b, t_ + 1)
                                    stand(pool, split_turn)
                                    nc.gpsimd.tensor_copy(part[:, :, 1, :], r1).then_inc(split_c, 1)
                                    pool.wait_ge(split_c, t_ + 1)
                                    wait(pool, split, t_)
                                    stand(pool, split_turn)
                                    nc.gpsimd.tensor_tensor(r2, r1, part[:, :, 1, :], ALU.subtract).then_inc(split_d, 1)
                                    pool.wait_ge(split_d, t_ + 1)
                                    stand(pool, split_turn)
                                    nc.gpsimd.tensor_copy(part[:, :, 2, :], r2).then_inc(split, 1)
                                steps(pool, NT, 2 * AHEAD, body)

                            @block.vector
                            def _(dve):
                                def first_part(t_, slot):
                                    dve.wait_ge(staged, t_ + 1)
                                    wait(dve, turned, t_ - (AHEAD - 1))
                                    nc.vector.tensor_copy(xsp[slot][:, :, 0, :], by_group(xst[slot][:])).then_inc(split_a, 1)

                                def remainder(t_, slot):
                                    dve.wait_ge(split_a, t_ + 1)
                                    wait(dve, split, t_ - (AHEAD - 1))
                                    nc.vector.tensor_tensor(by_group(rest1[slot][:]), by_group(xst[slot][:]), xsp[slot][:, :, 0, :],
                                                            ALU.subtract).then_inc(split_b, 1)

                                def body(t_, slot, turn):
                                    more = not isinstance(t_, int) or t_ + 2 < NT
                                    if more:
                                        first_part(t_ + 2, (slot + 2) % AHEAD)
                                    dve.wait_ge(turned, t_ + 1)
                                    wait(dve, a_done, t_ - 1)
                                    wait(dve, x_done, t_ - 1)
                                    nc.vector.tensor_copy(cT[slot % 2][:], ps_c[slot % 2][:])
                                    nc.vector.tensor_copy(rxT[slot % 2][:], ps_r[slot % 2][:, 0:2 * P]).then_inc(sums_copied, 1)
                                    if more:
                                        remainder(t_ + 2, (slot + 2) % AHEAD)
                                    dve.wait_ge(x_done, t_ + 1)
                                    row = one(x[:, ds(t_, 1), :])
                                    nc.vector.scalar_tensor_tensor(row, row, 2.0, ps_d[:, 0:C], ALU.mult, ALU.add)
                                    dve.wait_ge(a_done, t_ + 1)
                                    nc.vector.tensor_copy(aT[:, :, ds(t_ * P, P)], ps_a[:]).then_inc(a_copied, 1)
                                for t_ in range(2):
                                    first_part(t_, t_)
                                    remainder(t_, t_)
                                steps(dve, NT, 2 * AHEAD, body, tail=2)

                            @block.tensor
                            def _(pe):
                                def turn_over(t_, slot):
                                    pe.wait_ge(staged, t_ + 1)
                                    wait(pe, sums_copied, t_ - 1)
                                    wait(pe, x_copied, t_ - 1)
                                    b, slot = slot % 2, slot % AHEAD
                                    for i in range(4):
                                        nc.tensor.transpose(ps_c[b][:, i * P:(i + 1) * P], stg[slot][:, i * P:(i + 1) * P], ident[:])
                                    nc.tensor.transpose(ps_r[b][:, 0:P], stg[slot][:, 4 * P:5 * P], ident[:])
                                    nc.tensor.transpose(ps_r[b][:, P:2 * P], xst[slot][:, 0:P], ident[:])
                                    pe.wait_ge(split, t_ + 1)
                                    for i in range(5):
                                        last = nc.tensor.transpose(ps_x[b][0:96, i * P:(i + 1) * P], xsp[slot][:, i, :, :].rearrange("p a c -> p (a c)"), identb[:])
                                    last.then_inc(turned, 1)

                                def body(t_, slot, turn):
                                    if not (isinstance(t_, int) and t_ == NT - 1):
                                        turn_over(t_ + 1, slot + 1)
                                    b = slot % 2
                                    pe.wait_ge(sums_copied, t_ + 1)
                                    wait(pe, a_copied, t_)
                                    nc.tensor.matmul(ps_d[:, 0:P], rxT[b][:, P:2 * P], lu[:, 0:P], start=True, stop=False, skip_group_check=True)
                                    nc.tensor.matmul(ps_d[:, P:C], rxT[b][:, 0:P], lu[:, P:C], start=False, stop=True, skip_group_check=True).then_inc(x_done, 1)
                                    nc.tensor.matmul(ps_a[:, 0, :], w0[:].rearrange("k r w -> k (r w)"), cT[b][:, 0:P], start=True, stop=False, skip_group_check=True)
                                    nc.tensor.matmul(ps_a[:, 0, :], wt[:].rearrange("k r w -> k (r w)"), rxT[b][:, 0:P], start=False, stop=False, skip_group_check=True)
                                    nc.tensor.matmul(ps_a[:, 1:4, :], w1[:].rearrange("k r w -> k (r w)"), cT[b][:, P:512], start=False, stop=True, skip_group_check=True).then_inc(a_done, 1)
                                pe.wait_ge(w_scaled, 1)
                                turn_over(0, 0)
                                steps(pe, NT, 2 * AHEAD, body, tail=1)

                S_LO, S_HI, VEC = 0, NS, 2 * NS
                chunks = []
                for gp in (0, 1):
                    for c in range(16):
                        chunks.append((sel2, c, gp, [(0, wss, 16 * gp + c, S_HI if c % 2 else S_LO)]))
                for i in range(3):
                    for c in range(8):
                        chunks.append((sel4, c, 2 + i, [(1 + i, wvv, c, S_HI if c % 2 else S_LO)]))
                for c in range(16):
                    for i in range(3):
                        chunks.append((sel2, c, 2 + i, [(0, wvs, c, VEC + NV * i)]))
                for gp in (0, 1):
                    for c in range(8):
                        chunks.append((sel4, c, gp, [(1 + i, wsv, 8 * gp + c, VEC + NV * i) for i in range(3)]))
                BATCH = 4
                NBATCH = len(chunks) // BATCH
                starts, ends = {}, {}
                for q, ch in enumerate(chunks):
                    for part in ch[3]:
                        starts.setdefault(part[3], q)
                        ends[part[3]] = q
                PLANES = 20
                plane, last_user, holder, at_plane = [], [], {}, 0
                for turn_ in range(2):
                    plane, at_plane = [], 0
                    for q, ch in enumerate(chunks):
                        m = len(ch[3])
                        if at_plane + m > PLANES:
                            at_plane = 0
                        plane.append(at_plane)
                        last_user.append(max([holder[i] for i in range(at_plane, at_plane + m) if i in holder], default=-1))
                        for i in range(at_plane, at_plane + m):
                            holder[i] = turn_ * len(chunks) + q
                        at_plane += m
                last_user = [a - len(chunks) for a in last_user[len(chunks):]]
                with ExitStack() as sc:
                    uS = sb(sc, f"uS_{n}", [P, NT * P])
                    uV = sb(sc, f"uV_{n}", [3 * NV, NT * P])
                    with ExitStack() as sc2:
                        xb = [sb(sc2, f"xb{i}_{n}", [96, 5, BLK], BF16) for i in range(2)]
                        zb = sb(sc2, f"zb_{n}", [P, PLANES, BLK])
                        bc = [ps(sc2, f"bc{i}_{n}", [P, 512]) for i in range(BATCH)]
                        ps_s = [ps(sc2, f"ps_s{i}_{n}", [P, 512]) for i in range(2)]
                        ps_w = [ps(sc2, f"ps_w{i}_{n}", [P, 512]) for i in range(2)]
                        xb_ready, spread, paired, used, u_copied, tail_zero = (sem(f"{a}_{n}") for a in (
                            "xb_ready", "spread", "paired", "used", "u_copied", "tail_zero"))
                        NCH = len(chunks)
                        if scatter_beside:
                            scatter_sp, scatter_pool = scatter_parts(scatter_beside, sc2)
                        with nc.Block() as block:
                            if scatter_beside:
                                @block.sync
                                def _(sp):
                                    scatter_sp(sp)

                                @block.gpsimd
                                def _(pool):
                                    scatter_pool(pool)

                            @block.scalar
                            def _(act):
                                def body(b, slot, turn):
                                    if not (isinstance(b, int) and b == NB - 1):
                                        wait(act, spread, b * NCH)
                                        nc.scalar.copy(xb[1 - slot][:], xpT[:, :, ds((b + 1) * BLK, BLK)]).then_inc(xb_ready, 1)
                                    act.wait_ge(used, (b + 1) * NCH)
                                    nc.scalar.copy(uS[:, ds(b * BLK, BLK)], ps_s[slot][:, 0:BLK])
                                    nc.scalar.copy(uV[:, ds(b * BLK, BLK)], ps_w[slot][0:3 * NV, 0:BLK]).then_inc(u_copied, 1)
                                nc.scalar.copy(xb[0][:], xpT[:, :, 0:BLK]).then_inc(xb_ready, 1)
                                steps(act, NB, 2, body, tail=1)

                            @block.vector
                            def _(dve):
                                def body(b, slot, turn):
                                    for q, (sel, c, gp, parts) in enumerate(chunks):
                                        at = b * NCH + q
                                        dve.wait_ge(spread, at + 1)
                                        wait(dve, used, b * NCH + last_user[q] + 1)
                                        m = len(parts)
                                        z = zb[:, plane[q]:plane[q] + m, :]
                                        a0 = parts[0][0]
                                        nc.vector.tensor_tensor(z, bc[q % BATCH][:, 0:BLK].unsqueeze(1).broadcast_to([P, m, BLK]),
                                                                aT[:, a0:a0 + m, ds(b * BLK, BLK)], ALU.mult).then_inc(paired, 1)
                                nc.vector.memset(uS[:, NB * BLK:NT * P], 0.0).then_inc(tail_zero, 1)
                                nc.vector.memset(uV[:, NB * BLK:NT * P], 0.0).then_inc(tail_zero, 1)
                                steps(dve, NB, 2, body, tail=1)

                            @block.tensor
                            def _(pe):
                                def contract(b, slot, q):
                                    sel, c, gp, parts = chunks[q]
                                    pe.wait_ge(paired, b * NCH + q + 1)
                                    for j, (a0, wu, wc, at) in enumerate(parts):
                                        dst, m = (ps_w[slot], NV) if at >= VEC else (ps_s[slot], NS)
                                        row = at - VEC if at >= VEC else at
                                        last = nc.tensor.matmul(dst[row:row + m, 0:BLK], wu[:, wc, :], zb[:, plane[q] + j, :],
                                                                start=(starts[at] == q), stop=(ends[at] == q), skip_group_check=True)
                                    last.then_inc(used, 1)

                                def body(b, slot, turn):
                                    pe.wait_ge(xb_ready, b + 1)
                                    wait(pe, u_copied, b - 1)
                                    for batch in range(NBATCH + 1):
                                        for q in range(batch * BATCH, min((batch + 1) * BATCH, NCH)):
                                            sel, c, gp, parts = chunks[q]
                                            wait(pe, paired, b * NCH + q + 1 - BATCH)
                                            nc.tensor.matmul(bc[q % BATCH][:, 0:BLK], sel[:, c, :], xb[slot][:, gp, :], start=True, stop=True).then_inc(spread, 1)
                                        for q in range((batch - 1) * BATCH, batch * BATCH):
                                            if q >= 0:
                                                contract(b, slot, q)
                                steps(pe, NB, 2, body, tail=1)

                    with ExitStack() as sc2:
                        back = [ps(sc2, f"back{i}_{n}", [P, 512]) for i in range(4)]
                        turned_back, added = sem(f"turned_back_{n}"), sem(f"added_{n}")
                        with nc.Block() as block:
                            @block.tensor
                            def _(pe):
                                for t_ in range(NT):
                                    wait(pe, added, t_ - 3)
                                    nc.tensor.matmul(back[t_ % 4][:, 0:NS], uS[:, t_ * P:(t_ + 1) * P], eye2[:], start=True, stop=False, skip_group_check=True)
                                    nc.tensor.matmul(back[t_ % 4][:, NS:C], uV[:, t_ * P:(t_ + 1) * P], ident[0:96, 0:96], start=False, stop=True, skip_group_check=True).then_inc(turned_back, 1)

                            @block.vector
                            def _(dve):
                                for t_ in range(NT):
                                    dve.wait_ge(turned_back, t_ + 1)
                                    nc.vector.tensor_tensor(x[:, t_, :], x[:, t_, :], back[t_ % 4][:, 0:C], ALU.add).then_inc(added, 1)

        def filter_layer(n, f):
            rec = rec_d[0:P * T, :].rearrange("(p t) w -> p t w", t=T)
            one_l = n == 1
            K, KC = f["fc_in"], f["fc_col"]
            KP = 32 * -(-K // 32)
            NW, NSC = f["nw"], f["nsc"]
            PW = 448 if one_l else 320
            MW = f["wa"] + f["wb"]
            WA, WB = f["wa"], f["wb"]
            layer = ExitStack()
            with layer:
                acc = sb(layer, f"acc_{n}", [P, NT, WA + WB])
                sconn = sb(layer, f"sconn_{n}", [P, NT, NSC + 96])
                ws = sb(layer, f"ws_{n}", [P, NS + NSC + 4 * NV])
                wv = sb(layer, f"wv_{n}", [NV, 2 * NV])
                fc1 = sb(layer, f"fc1_{n}", [TPG * KP, TPG * 64])
                fc2 = sb(layer, f"fc2_{n}", [TPG * 64, TPG * NW])
                NO = f["no"]
                KV = f["kv"]
                wos = sb(layer, f"wos_{n}", [96, NO])
                wov = sb(layer, f"wov_{n}", [KV, NV])
                w_in, w_scaled, acc_zero = (sem(f"{a}_{n}") for a in ("weights_in", "weights_scaled", "acc_zero"))

                with ExitStack() as sc:
                    xst = [sb(sc, f"xst{i}_{n}", [P, C]) for i in range(4)]
                    xT = [sb(sc, f"xT{i}_{n}", [P, 2, P]) for i in range(2)]
                    hst = [sb(sc, f"hst{i}_{n}", [P, C]) for i in range(2)]
                    pT = [ps(sc, f"pT{i}_{n}", [P, 2, P]) for i in range(2)]
                    pP = [ps(sc, f"pP{i}_{n}", [P, 512]) for i in range(2)]
                    staged, transposed, tcopied, mapped, taken = (sem(f"pre_{a}_{n}") for a in ("staged", "transposed", "tcopied", "mapped", "taken"))
                    h_sent = [sem(f"h_sent{i}_{n}") for i in range(2)]
                    turn_begun, blocks_zero = sem(f"pre_turn_begun_{n}"), sem(f"blocks_zero_{n}")
                    with nc.Block() as block:
                        @block.scalar
                        def _(act):
                            nw = 0
                            act.wait_ge(blocks_zero, 3)
                            for dst, src in f["loads"](ws, wv, fc1, fc2, wos, wov):
                                act.dma_start(dst, src).then_inc(w_in, 16)
                                nw += 16
                            act.wait_ge(w_in, nw)
                            for ap, s in f["scale"](ws, wv, fc1, fc2, wos, wov):
                                last = nc.scalar.mul(ap, ap, s)
                            last.then_inc(w_scaled, 1)

                            def stage(t_, slot):
                                wait(act, transposed, t_ - 3)
                                nc.scalar.copy(xst[slot][:], one(x[:, ds(t_, 1), :])).then_inc(staged, 1)

                            def body(t_, slot, turn):
                                if not isinstance(t_, int) or t_ + 2 < NT:
                                    stage(t_ + 2, (slot + 2) % 4)
                                act.wait_ge(transposed, t_ + 1)
                                wait(act, mapped, t_ - 1)
                                nc.scalar.copy(xT[slot % 2][:, 0, :], pT[slot % 2][:, 0, :])
                                nc.scalar.copy(xT[slot % 2][0:NV, 1, :], pT[slot % 2][0:NV, 1, :]).then_inc(tcopied, 1)
                            stage(0, 0)
                            stage(1, 1)
                            steps(act, NT, 4, body, tail=2)

                        @block.tensor
                        def _(pe):
                            def transposes(t_, slot):
                                pe.wait_ge(staged, t_ + 1)
                                wait(pe, tcopied, t_ - 1)
                                stand(pe, turn_begun)
                                nc.tensor.transpose(pT[slot % 2][:, 0, :], xst[slot % 4][:, 0:P], ident[:])
                                nc.tensor.transpose(pT[slot % 2][0:NV, 1, :], xst[slot % 4][:, P:C], ident[:]).then_inc(transposed, 1)

                            def body(t_, slot, turn):
                                if not (isinstance(t_, int) and t_ == NT - 1):
                                    transposes(t_ + 1, slot + 1)
                                pe.wait_ge(tcopied, t_ + 1)
                                wait(pe, taken, t_ - 1)
                                c0, b = NS + NSC + 4 * NV, slot % 2
                                nc.tensor.matmul(pP[b][:, 0:c0], xT[b][:, 0, :], ws[:], start=True, stop=False, skip_group_check=True)
                                nc.tensor.matmul(pP[b][:, c0:c0 + 2 * NV], xT[b][0:NV, 1, :], wv[:], start=False, stop=True, skip_group_check=True).then_inc(mapped, 1)
                            pe.wait_ge(w_scaled, 1)
                            transposes(0, 0)
                            steps(pe, NT, 4, body, tail=1)

                        @block.vector
                        def _(dve):
                            def body(t_, slot, turn):
                                dve.wait_ge(mapped, t_ + 1)
                                wait(dve, h_sent[slot], turn * 16)
                                a = attr[:, ds(t_, 1)]
                                p, h, s = pP[slot], hst[slot], one(sconn[:, ds(t_, 1), :])
                                vec = p[:, NS + NSC:NS + NSC + 6 * NV].rearrange("p (i c) -> p i c", i=3)
                                nc.vector.tensor_scalar(h[:, 0:NS], p[:, 0:NS], a, None, ALU.mult)
                                nc.vector.tensor_scalar(h[:, NS:C].rearrange("p (i c) -> p i c", i=3), vec[:, :, 0:NV], a, None, ALU.mult)
                                nc.vector.tensor_scalar(s[:, 0:NSC], p[:, NS:NS + NSC], a, None, ALU.mult)
                                nc.vector.tensor_scalar(s[:, NSC:NSC + 96].rearrange("p (i c) -> p i c", i=3), vec[:, :, NV:2 * NV], a, None, ALU.mult).then_inc(taken, 1)
                            nc.vector.memset(ws[:], 0.0).then_inc(blocks_zero, 1)
                            nc.vector.memset(fc1[:], 0.0).then_inc(blocks_zero, 1)
                            nc.vector.memset(fc2[:], 0.0).then_inc(blocks_zero, 1)
                            steps(dve, NT, 2, body)

                        @block.gpsimd
                        def _(pool):
                            nc.gpsimd.memset(acc[:], 0.0).then_inc(acc_zero, 1)
                            pool.wait_ge(acc_zero, 1)

                        @block.sync
                        def _(sp):
                            def body(t_, slot, turn):
                                sp.wait_ge(taken, t_ + 1)
                                sp.dma_start(h_dram[ds(t_ * P, P), :], hst[slot][:]).then_inc(h_sent[slot], 16)
                            steps(sp, NT, 2, body)
                            sp.wait_ge(h_sent[0], 16 * ((NT + 1) // 2))
                            sp.wait_ge(h_sent[1], 16 * (NT // 2))

                with ExitStack() as sc:
                    recb = [sb(sc, f"recb{i}_{n}", [P, TPG, WD]) for i in range(RSLOTS)]
                    rowb = [sb(sc, f"rowb{i}_{n}", [P, TPG, C]) for i in range(RSLOTS)]
                    oh = [sb(sc, f"oh{i}_{n}", [P, TPG, P]) for i in range(SLOTS)]
                    prod = [sb(sc, f"prod{i}_{n}", [P, TPG, PW]) for i in range(SLOTS)]
                    msg = [sb(sc, f"msg{i}_{n}", [P, TPG, MW]) for i in range(SLOTS)]
                    eT = sb(sc, f"eT_{n}", [TPG * KP, P])
                    hid = [sb(sc, f"hid{i}_{n}", [TPG * 64, P]) for i in range(2)]
                    psa = [ps(sc, f"psa{i}_{n}", [P, 512]) for i in range(2)]
                    psb = [ps(sc, f"psb{i}_{n}", [P, 512]) for i in range(2)]
                    psw = [ps(sc, f"psw{i}_{n}", [P, 512]) for i in range(2)]
                    psT = ps(sc, f"psT_{n}", [P, 512])
                    psH = ps(sc, f"psH_{n}", [P, 512])
                    rec_in = [sem(f"rec_in{i}_{n}") for i in range(RSLOTS)]
                    rows_in = [sem(f"rows_in{i}_{n}") for i in range(RSLOTS)]
                    (oh_ready, agg_done, evac_done, gather_turn, e_turned, eT_ready, fc1_done, hid_ready, fc2_done, prod_ready) = (
                        sem(f"{a}_{n}") for a in ("oh_ready", "agg_done", "evac_done", "gather_turn", "e_turned", "eT_ready",
                                                  "fc1_done", "hid_ready", "fc2_done", "prod_ready"))
                    scaled, msg_ready = sem(f"scaled_{n}"), sem(f"msg_ready_{n}")
                    ones_ready, turn_begun = sem(f"ones_ready_{n}"), sem(f"edge_turn_begun_{n}")
                    with nc.Block() as block:
                        @block.sync
                        def _(sp):
                            def body(g, slot, turn):
                                wait(sp, agg_done, g - (RSLOTS - 1))
                                sp.dma_start(recb[slot][:, :, KC:WD], rec[:, ds(TPG * g, TPG), KC:WD]).then_inc(rec_in[slot], 16)
                            steps(sp, NG, RSLOTS, body)

                        @block.gpsimd
                        def _(pool):
                            def body(g, slot, turn):
                                pool.wait_ge(rec_in[slot], (turn + 1) * 16)
                                wait(pool, prod_ready, g - (RSLOTS - 1))
                                stand(pool, gather_turn)
                                for k in range(TPG):
                                    pool.indirect_dma_start(rowb[slot][:, k, :], None, h_dram,
                                                            bass.IndirectOffsetOnAxis(recb[slot][:, k, D_IDX:D_IDX + 1].bitcast(U32), 0)).then_inc(rows_in[slot], 16)
                            steps(pool, NG, RSLOTS, body)

                        @block.scalar
                        def _(act):
                            def turned(g):
                                act.wait_ge(e_turned, g + 1)
                                wait(act, fc1_done, g)
                                for k in range(TPG):
                                    last = nc.scalar.copy(eT[KP * k:KP * k + K, :], psT[0:K, k * P:(k + 1) * P])
                                last.then_inc(eT_ready, 1)

                            def hidden(g, slot):
                                act.wait_ge(fc1_done, g + 1)
                                wait(act, fc2_done, g - 1)
                                nc.scalar.activation(hid[slot % 2][:], psH[:, 0:P], ACT.Silu, scale=f["silu_scale"]).then_inc(hid_ready, 1)

                            def scale(g, slot, k):
                                act.wait_ge(prod_ready, g + 1)
                                wait(act, agg_done, g - (SLOTS - 1))
                                rb, pr, m = recb[slot], prod[slot % SLOTS], msg[slot % SLOTS]
                                last = nc.scalar.activation(m[:, k, 0:C], pr[:, k, 0:C], ACT.Copy, scale=rb[:, k, D_E4:D_E4 + 1])
                                for i in range(3 if one_l else 0):
                                    last = nc.scalar.activation(m[:, k, 352 + 96 * i:448 + 96 * i], pr[:, k, 224 + 2 * NV * i:320 + 2 * NV * i],
                                                                ACT.Copy, scale=rb[:, k, D_E4 + 1 + i:D_E4 + 2 + i])
                                for i in range(0 if one_l else 3):
                                    last = nc.scalar.activation(m[:, k, 352 + NV * i:384 + NV * i], pr[:, k, 224 + NV * i:256 + NV * i],
                                                                ACT.Copy, scale=rb[:, k, D_E4 + 1 + i:D_E4 + 2 + i])
                                last.then_inc(scaled, 1)

                            def body(g, slot, turn):
                                near = not isinstance(g, int) or g + 1 < NG
                                far = not isinstance(g, int) or g + LEAD < NG
                                if near:
                                    scale(g + 1, (slot + 1) % RSLOTS, 0)
                                if far:
                                    turned(g + LEAD)
                                if near:
                                    scale(g + 1, (slot + 1) % RSLOTS, 1)
                                if far:
                                    hidden(g + LEAD, slot + LEAD)
                            act.wait_ge(ones_ready, SLOTS + 1)
                            for g in range(LEAD):
                                turned(g)
                                hidden(g, g)
                            for k in range(TPG):
                                scale(0, 0, k)
                            steps(act, NG, RSLOTS, body, tail=LEAD)

                        @block.vector
                        def _(dve):
                            def products(g, slot, turn):
                                dve.wait_ge(rec_in[slot], (turn + 1) * 16)
                                wait(dve, agg_done, g - (SLOTS - 1))
                                wait(dve, scaled, (g - (SLOTS - 1)) * TPG)
                                b = slot % SLOTS
                                nc.vector.tensor_tensor(oh[b][:], iota[:].unsqueeze(1).broadcast_to([P, TPG, P]),
                                                        recb[slot][:, :, D_LOC:D_LOC + 1].broadcast_to([P, TPG, P]), ALU.is_equal)
                                dve.wait_ge(rows_in[slot], (turn + 1) * (16 * TPG))
                                dve.wait_ge(fc2_done, g + 1)
                                w = psw[slot % 2][:, 0:TPG * NW].rearrange("p (k c) -> p k c", k=TPG)
                                row, pr = rowb[slot], prod[b]
                                es = row[:, :, 0:NS].unsqueeze(2).broadcast_to([P, TPG, 2, NS])
                                ev = row[:, :, NS:C].rearrange("p k (i c) -> p k i c", i=3)

                                def mul(dst, x_, wcol, m):
                                    return nc.vector.tensor_tensor(dst, w[:, :, wcol:wcol + NV].unsqueeze(2).broadcast_to([P, TPG, m, NV]), x_, ALU.mult)
                                nc.vector.tensor_tensor(pr[:, :, 0:320].rearrange("p k (a c) -> p k a c", a=2)[:, :, :, 0:NS],
                                                        w[:, :, 0:2 * NS].rearrange("p k (a c) -> p k a c", a=2), es, ALU.mult)
                                last = mul(pr[:, :, NS:C].rearrange("p k (i c) -> p k i c", i=3), ev, 2 * NS, 3)
                                if one_l:
                                    seq = pr[:, :, 224:448].rearrange("p k (b c) -> p k b c", b=7)
                                    mul(seq[:, :, 0:7:3, :], ev, 2 * NS + NV, 3)
                                    mul(seq[:, :, 1:3, :], ev[:, :, 1:3, :], 2 * NS + 2 * NV, 2)
                                    last = mul(seq[:, :, 4:6, :], ev[:, :, 0:2, :], 2 * NS + 2 * NV, 2)
                                else:
                                    last = mul(pr[:, :, 224:320].rearrange("p k (i c) -> p k i c", i=3), ev, 2 * NS + NV, 3)
                                last.then_inc(prod_ready, 1)
                                dve.wait_ge(prod_ready, g + 1)
                                m = msg[b]
                                e1 = recb[slot][:, :, D_E4 + 1:D_E4 + 4].unsqueeze(3)
                                last = nc.vector.tensor_tensor(m[:, :, C:352].rearrange("p k (i c) -> p k i c", i=3),
                                                               pr[:, :, C:C + NS].unsqueeze(2).broadcast_to([P, TPG, 3, NS]),
                                                               e1.broadcast_to([P, TPG, 3, NS]), ALU.mult)
                                last.then_inc(msg_ready, 1)

                            def body(g, slot, turn):
                                tile = dve.value_load(gtile["d"][0:1, ds(g, 1)], min_val=0, max_val=NT - 1)
                                if not isinstance(g, int) or g + 2 < NG:
                                    products(g + 2, (slot + 2) % RSLOTS, turn + (slot + 2) // RSLOTS)
                                dve.wait_ge(agg_done, g + 1)
                                wait(dve, evac_done, g)
                                a = one(acc[:, ds(tile, 1), :])
                                last = nc.vector.tensor_tensor(a[:, 0:WA], psa[slot % 2][:, 0:WA], a[:, 0:WA], ALU.add)
                                if WB:
                                    last = nc.vector.tensor_tensor(a[:, WA:WA + WB], psb[slot % 2][:, 0:WB], a[:, WA:WA + WB], ALU.add)
                                last.then_inc(evac_done, 1)

                            for b in range(SLOTS):
                                nc.vector.memset(msg[b][:, :, MW - 1:MW], 1.0).then_inc(ones_ready, 1)
                            nc.vector.memset(eT[:], 0.0).then_inc(ones_ready, 1)
                            products(0, 0, 0)
                            products(1, 1, 0)
                            steps(dve, NG, RSLOTS, body, tail=2)

                        @block.tensor
                        def _(pe):
                            def turn_e(g, slot, turn):
                                pe.wait_ge(rec_in[slot], (turn + 1) * 16)
                                wait(pe, eT_ready, g)
                                stand(pe, turn_begun)
                                for k in range(TPG):
                                    last = nc.tensor.transpose(psT[0:K, k * P:(k + 1) * P], recb[slot][:, k, KC:KC + K], ident[:])
                                last.then_inc(e_turned, 1)

                            def first(g):
                                pe.wait_ge(eT_ready, g + 1)
                                wait(pe, hid_ready, g)
                                stand(pe, turn_begun)
                                nc.tensor.matmul(psH[:, 0:P], fc1[:], eT[:], start=True, stop=True).then_inc(fc1_done, 1)

                            def second(g, slot):
                                pe.wait_ge(hid_ready, g + 1)
                                wait(pe, prod_ready, g - 1)
                                nc.tensor.matmul(psw[slot % 2][:, 0:TPG * NW], hid[slot % 2][:], fc2[:], start=True, stop=True).then_inc(fc2_done, 1)

                            def sums(slot, k):
                                b, st, en = slot % 2, k == 0, k == TPG - 1
                                last = nc.tensor.matmul(psa[b][:, 0:WA], oh[slot % SLOTS][:, k, :], msg[slot % SLOTS][:, k, 0:WA], start=st, stop=en)
                                if WB:
                                    last = nc.tensor.matmul(psb[b][:, 0:WB], oh[slot % SLOTS][:, k, :], msg[slot % SLOTS][:, k, WA:MW], start=st, stop=en)
                                return last

                            def body(g, slot, turn):
                                far = not isinstance(g, int) or g + LEAD < NG
                                if far:
                                    turn_e(g + LEAD, (slot + LEAD) % RSLOTS, turn + (slot + LEAD) // RSLOTS)
                                if not isinstance(g, int) or g + LEAD - 1 < NG:
                                    second(g + LEAD - 1, slot + LEAD - 1)
                                pe.wait_ge(msg_ready, g + 1)
                                pe.wait_ge(scaled, g * TPG + 1)
                                wait(pe, evac_done, g - 1)
                                sums(slot, 0)
                                if far:
                                    first(g + LEAD)
                                pe.wait_ge(scaled, (g + 1) * TPG)
                                sums(slot, 1).then_inc(agg_done, 1)
                            pe.wait_ge(ones_ready, SLOTS + 1)
                            for g in range(LEAD):
                                turn_e(g, g, 0)
                                first(g)
                                if g < LEAD - 1:
                                    second(g, g)
                            steps(pe, NG, RSLOTS, body, tail=LEAD)

                with ExitStack() as sc:
                    sg = [sb(sc, f"sg{i}_{n}", [P, 96 + 3 * KV]) for i in range(4)]
                    tmp = [sb(sc, f"tmp{i}_{n}", [P, NV]) for i in range(4)]
                    sT = [sb(sc, f"sT{i}_{n}", [P, 4, P]) for i in range(2)]
                    pT = [ps(sc, f"qT{i}_{n}", [P, 4, P]) for i in range(2)]
                    pO = [ps(sc, f"pO{i}_{n}", [P, 512]) for i in range(2)]
                    factor = sb(sc, f"factor_{n}", [P, 3, NT])
                    gates = sb(sc, f"gates_{n}", [P, NT, 96]) if one_l else None
                    staged, t_summed, transposed, tcopied, mapped, taken, f_step, acted, gated, y_step = (
                        sem(f"post_{a}_{n}") for a in ("staged", "t_summed", "transposed", "tcopied", "mapped", "taken", "f_step", "acted", "gated", "y_step"))
                    with nc.Block() as block:
                        @block.vector
                        def _(dve):
                            def stage(t_, slot):
                                a = one(acc[:, ds(t_, 1), :])
                                wait(dve, transposed, t_ - 3)
                                s_ = sg[slot]
                                vec = s_[:, 96:96 + 3 * KV].rearrange("p (i c) -> p i c", i=3)
                                if one_l:
                                    def blk(k, j):
                                        c0 = 352 + 96 * k + NV * j
                                        return a[:, c0:c0 + NV]
                                    nc.vector.tensor_tensor(tmp[slot][:], blk(0, 0), blk(1, 1), ALU.add).then_inc(t_summed, 1)
                                else:
                                    nc.vector.tensor_tensor(tmp[slot][:], a[:, 352:384], a[:, 384:416], ALU.add).then_inc(t_summed, 1)
                                nc.vector.tensor_copy(s_[:, 0:NS], a[:, 0:NS])
                                nc.vector.tensor_copy(vec[:, :, NS:NS + NV], a[:, NS:C].rearrange("p (i c) -> p i c", i=3))
                                nc.vector.tensor_copy(vec[:, :, 0:NS], a[:, C:352].rearrange("p (i c) -> p i c", i=3))
                                if one_l:
                                    nc.vector.tensor_tensor(vec[:, 0, 96:128], blk(2, 1), blk(1, 0), ALU.subtract)
                                    nc.vector.tensor_tensor(vec[:, 1, 96:128], blk(0, 2), blk(2, 0), ALU.subtract)
                                    nc.vector.tensor_tensor(vec[:, 2, 96:128], blk(1, 2), blk(0, 1), ALU.subtract)
                                    dve.wait_ge(t_summed, t_ + 1)
                                    nc.vector.tensor_tensor(s_[:, NS:96], tmp[slot][:], blk(2, 2), ALU.add).then_inc(staged, 1)
                                else:
                                    dve.wait_ge(t_summed, t_ + 1)
                                    nc.vector.tensor_tensor(s_[:, NS:96], tmp[slot][:], a[:, 416:448], ALU.add).then_inc(staged, 1)

                            def body(t_, slot, turn):
                                if not isinstance(t_, int) or t_ + 2 < NT:
                                    stage(t_ + 2, (slot + 2) % 4)
                                dve.wait_ge(mapped, t_ + 1)
                                s_ = one(sconn[:, ds(t_, 1), :])
                                if one_l:
                                    nc.vector.scalar_tensor_tensor(s_, pO[slot % 2][:, 0:192], attr[:, ds(t_, 1)], s_, ALU.mult, ALU.add).then_inc(taken, 1)
                                else:
                                    coef = factor[:, 1, ds(t_, 1)]
                                    nc.vector.tensor_scalar(factor[:, 2, ds(t_, 1)], pO[slot % 2][:, 0:1], coef, coef, ALU.mult, ALU.mult).then_inc(acted, 1)
                                    dve.wait_ge(acted, t_ + 1)
                                    nc.vector.scalar_tensor_tensor(s_, pO[slot % 2][:, 1:161], factor[:, 2, ds(t_, 1)], s_, ALU.mult, ALU.add).then_inc(taken, 1)

                            if not one_l:
                                nc.vector.tensor_scalar(factor[:, 0, :].unsqueeze(2), acc[:, :, MW - 1:MW], 1.0, None, ALU.max).then_inc(f_step, 1)
                                dve.wait_ge(f_step, 1)
                                nc.vector.reciprocal(factor[:, 0, :], factor[:, 0, :]).then_inc(f_step, 1)
                                dve.wait_ge(f_step, 2)
                                nc.vector.tensor_tensor(factor[:, 1, :], factor[:, 0, :], attr[:], ALU.mult).then_inc(f_step, 1)
                                dve.wait_ge(f_step, 3)
                            stage(0, 0)
                            stage(1, 1)
                            steps(dve, NT, 4, body, tail=2)
                            dve.wait_ge(taken, NT)
                            if one_l:
                                dve.wait_ge(gated, 1)
                                g_ = gates[:, :, NS:96].unsqueeze(2).broadcast_to([P, NT, 3, NV])
                                v_ = sconn[:, :, 96:192].rearrange("p t (i c) -> p t i c", i=3)
                                nc.vector.tensor_tensor(v_, g_, v_, ALU.mult).then_inc(y_step, 1)
                                dve.wait_ge(y_step, 1)
                                scal, v0 = gates[:, :, 0:NS], 96
                            else:
                                scal, v0 = sconn[:, :, 0:NS], NS
                            nc.vector.tensor_tensor(x[:, :, OS:OS + NS], x[:, :, OS:OS + NS], scal, ALU.add)
                            for i in range(3):
                                o = x[:, :, OV[i]:OV[i] + NV]
                                nc.vector.tensor_tensor(o, o, sconn[:, :, v0 + NV * i:v0 + NV * (i + 1)], ALU.add)

                        @block.tensor
                        def _(pe):
                            def transposes(t_, slot):
                                pe.wait_ge(staged, t_ + 1)
                                wait(pe, tcopied, t_ - 1)
                                nc.tensor.transpose(pT[slot % 2][0:96, 0, :], sg[slot % 4][:, 0:96], ident[:])
                                for i in range(3):
                                    last = nc.tensor.transpose(pT[slot % 2][0:KV, 1 + i, :], sg[slot % 4][:, 96 + KV * i:96 + KV * (i + 1)], ident[:])
                                last.then_inc(transposed, 1)

                            def body(t_, slot, turn):
                                if not (isinstance(t_, int) and t_ == NT - 1):
                                    transposes(t_ + 1, slot + 1)
                                pe.wait_ge(tcopied, t_ + 1)
                                wait(pe, taken, t_ - 1)
                                nc.tensor.matmul(pO[slot % 2][:, 0:NO], sT[slot % 2][0:96, 0, :], wos[:], start=True, stop=False, skip_group_check=True)
                                for i in range(3):
                                    last = nc.tensor.matmul(pO[slot % 2][:, NO + NV * i:NO + NV * (i + 1)], sT[slot % 2][0:KV, 1 + i, :], wov[:], start=False, stop=(i == 2), skip_group_check=True)
                                last.then_inc(mapped, 1)
                            transposes(0, 0)
                            steps(pe, NT, 4, body, tail=1)

                        @block.scalar
                        def _(act):
                            def body(t_, slot, turn):
                                act.wait_ge(transposed, t_ + 1)
                                wait(act, mapped, t_ - 1)
                                nc.scalar.copy(sT[slot % 2][0:96, 0, :], pT[slot % 2][0:96, 0, :])
                                nc.scalar.copy(sT[slot % 2][0:KV, 1:4, :], pT[slot % 2][0:KV, 1:4, :]).then_inc(tcopied, 1)
                            steps(act, NT, 4, body)
                            if one_l:
                                act.wait_ge(taken, NT)
                                nc.scalar.activation(gates[:, :, 0:NS], sconn[:, :, 0:NS], ACT.Silu)
                                nc.scalar.activation(gates[:, :, NS:96], sconn[:, :, NS:96], ACT.Sigmoid).then_inc(gated, 1)

        inv = lambda d: float(1.0 / np.sqrt(np.float64(d)))
        r3, r32 = inv(3), inv(NV)
        p0, p3 = "L0_gnn_", "L3_gnn_"
        flat = lambda ap: ap.rearrange("u o w -> (u o) w")
        product_layer(
            0, t["x"], "d",
            {"lm_s": t[p0 + "Lm_s"], "wm_ss": t[p0 + "Wm_ss"], "wm_vv": t[p0 + "Wm_vv"], "wm_sv": t[p0 + "Wm_sv"], "lm_v": t[p0 + "Lm_v"],
             "wm_vs": t[p0 + "Wm_vs"], "lu_s": t[p0 + "Lu_s"], "lu_v": t[p0 + "Lu_v"], "wu_ss": t[p0 + "Wu_ss"], "wu_vv": t[p0 + "Wu_vv"],
             "wu_sv": t[p0 + "Wu_sv"], "wu_vs": t[p0 + "Wu_vs"], "dist": 3, "r": (0, 1, 2)},
            {"lm_s": 1 / 8, "wm_ss": 1 / 8, "wm_vv": r3 * r32, "wm_sv": 1 / 8, "lm_v": r32, "wm_vs": r32, "lu_s": 1 / 8, "lu_v": r32,
             "wu_ss": 1 / 64, "wu_vv": r3 / 32, "wu_sv": inv(2048), "wu_vs": inv(2048)})
        end_stage()
        layernorm(0)

        def vector_blocks(ws, nsc, linear, connection):
            at = [(NS + NV * i, NS + nsc + 2 * NV * i) for i in range(2)]
            return [(ws[r:r + NV, c:c + NV], linear) for r, c in at] + [(ws[r:r + NV, c + NV:c + 2 * NV], connection) for r, c in at]

        p1 = "L1_gnn_"
        filter_layer(1, {
            "fc_in": 64, "fc_col": D_E64, "nw": 224, "nsc": 96, "wa": 320, "wb": 320, "no": 96, "kv": 128, "silu_scale": 1 / 8,
            "loads": lambda ws, wv, fc1, fc2, wos, wov: (
                (ws[0:NS, 0:NS], t[p1 + "lin1_ws"]), (ws[0:NS, NS:NS + 96], t[p1 + "sc_ws"]), (wv[:, 0:NV], t[p1 + "lin1_wv"]),
                *vector_blocks(ws, 96, t[p1 + "lin1_wv"], t[p1 + "sc_wv"]),
                (wv[:, NV:2 * NV], t[p1 + "sc_wv"]), *(((fc1[64 * k:64 * (k + 1), 64 * k:64 * (k + 1)]), t[p1 + "fc_w1"]) for k in range(TPG)),
                *(((fc2[64 * k:64 * (k + 1), 224 * k:224 * (k + 1)]), t[p1 + "fc_w2"]) for k in range(TPG)),
                (wos[:], t[p1 + "lin2_ws"]), (wov[:], t[p1 + "lin2_wv"])),
            "scale": lambda ws, wv, fc1, fc2, wos, wov: (
                (ws[0:NS, :], 1 / 8), (ws[NS:P, :], r32), (wv[:], r32), (fc2[:], 1 / 8), (wos[0:NS, :], inv(96) / 4), (wos[NS:96, :], inv(96) / 4 * r3),
                (wov[0:96, :], inv(128) / 4), (wov[96:128, :], inv(128) / 4 * inv(2)))})
        end_stage()
        layernorm(1)

        p2 = "L2_gnn_"
        filter_layer(2, {
            "fc_in": 16, "fc_col": D_E16, "nw": 192, "nsc": 64, "wa": 449, "wb": 0, "no": 65, "kv": 96, "silu_scale": 1 / 4,
            "loads": lambda ws, wv, fc1, fc2, wos, wov: (
                (ws[0:NS, 0:NS], t[p2 + "Wl1_0"]), (ws[0:NS, NS:2 * NS], t[p2 + "Wsc0"]), (wv[:, 0:NV], t[p2 + "Wl1_1"]),
                *vector_blocks(ws, NS, t[p2 + "Wl1_1"], t[p2 + "Wsc1"]),
                (wv[:, NV:2 * NV], t[p2 + "Wsc1"]), *(((fc1[32 * k:32 * k + 16, 64 * k:64 * (k + 1)]), t[p2 + "Wfc1"]) for k in range(TPG)),
                *(((fc2[64 * k:64 * (k + 1), 192 * k:192 * (k + 1)]), t[p2 + "Wfc2"]) for k in range(TPG)),
                (wos[:, 0:1], t[p2 + "Wa"]), (wos[:, 1:65], t[p2 + "Wl2_s"]), (wov[:], t[p2 + "Wl2_v"])),
            "scale": lambda ws, wv, fc1, fc2, wos, wov: (
                (ws[0:NS, :], 1 / 8), (ws[NS:P, :], r32), (wv[:], r32), (fc2[:], 1 / 8), (wos[0:NS, :], inv(96)), (wos[NS:96, :], inv(96) * r3),
                (wov[:], inv(96)))})
        end_stage()

        product_layer(
            3, h_dram, None,
            {"lm_s": t[p3 + "lm0"], "wm_ss": flat(t[p3 + "wm000"]), "wm_vv": flat(t[p3 + "wm110"]), "wm_sv": flat(t[p3 + "wm011"]),
             "lm_v": t[p3 + "lm1"], "wm_vs": flat(t[p3 + "wm101"]), "lu_s": t[p3 + "lu0"], "lu_v": t[p3 + "lu1"], "wu_ss": t[p3 + "wu000"],
             "wu_vv": t[p3 + "wu110"], "wu_sv": t[p3 + "wu011"], "wu_vs": t[p3 + "wu101"], "dist": 3, "r": (0, 1, 2)},
            {"lm_s": 1 / 8, "wm_ss": inv(96), "wm_vv": r3 * inv(96), "wm_sv": inv(96), "lm_v": r32, "wm_vs": inv(96), "lu_s": 1 / 8,
             "lu_v": r32, "wu_ss": inv(5120), "wu_vv": r3 * inv(5120), "wu_sv": 1 / 64, "wu_vs": 1 / 64},
            before=lambda sums: layernorm(2, gathered=True, clear=sums))
        end_stage()
        layernorm(3, to_output=True)


_INS = ["x", "src", "dst", "edge_attr_16", "edge_attr_4", "edge_attr_64", "node_vec1"]
_INS += ["L0_gnn_" + a for a in ("Wm_ss", "Wm_vv", "Wm_sv", "Wm_vs", "Lm_s", "Lm_v", "Wu_ss", "Wu_vv", "Wu_sv", "Wu_vs", "Lu_s", "Lu_v")]
_INS += ["L1_gnn_" + a for a in ("lin1_ws", "lin1_wv", "fc_w1", "fc_w2", "sc_ws", "sc_wv", "lin2_ws", "lin2_wv")]
_INS += ["L2_gnn_" + a for a in ("Wfc1", "Wfc2", "Wsc0", "Wsc1", "Wl1_0", "Wl1_1", "Wl2_s", "Wl2_v", "Wa")]
_INS += ["L3_gnn_" + a for a in ("wm000", "wm011", "wm101", "wm110", "lm0", "lm1", "wu000", "wu011", "wu101", "wu110", "lu0", "lu1")]


def kernel(**inputs):
    import concourse.bacc as bacc
    from concourse import mybir
    from concourse.bass_utils import run_bass_kernel_spmd

    nc = bacc.Bacc("TRN2", target_bir_lowering=False, num_devices=1)
    arrays, tensors = {}, {}
    cols = permutation()
    for name in _INS:
        a = np.asarray(inputs[name])
        if name == "x":
            a = a[:, cols]
        a = np.ascontiguousarray(a)
        arrays[f"in_{name}"] = a
        tensors[name] = nc.dram_tensor(f"in_{name}", a.shape, mybir.dt.from_np(a.dtype), kind="ExternalInput").ap()
    out = nc.dram_tensor("out_rows", (N, C), mybir.dt.float32, kind="ExternalOutput").ap()
    build(nc, tensors, out)
    got = run_bass_kernel_spmd(nc, [arrays], core_ids=[0]).results[0]["out_rows"]
    back = np.empty_like(cols)
    back[cols] = np.arange(C)
    return got[:, back]
```
